# Optimizing a Trainium2 kernel written in Bass

```python
import numpy as np
import jax
import jax.numpy as jnp

def _softmax(x, axis=-1):
    return jax.nn.softmax(x, axis=axis)

def _gelu(x):
    return jax.nn.gelu(x, approximate=True)

def _silu(x):
    return jax.nn.silu(x)

def _sigmoid(x):
    return jax.nn.sigmoid(x)

def _layernorm(x, axis=-1, eps=1e-05):
    m = jnp.mean(x, axis=axis, keepdims=True)
    v = jnp.var(x, axis=axis, keepdims=True)
    return (x - m) / jnp.sqrt(v + eps)

def _scatter_add(tgt, idx, src, axis=0):
    return tgt.at[idx].add(src)

def _segment_sum(src, seg, n):
    return jax.ops.segment_sum(src, seg, n)
kernel_name = 'mk_gnn_preln_d2_gnn_r8_42a9e3'

def setup_inputs(seed: int=0):
    np.random.seed(seed)
    _w = jnp.asarray

    def _rec_inputs():
        import jax
        import jax.numpy as jnp
        _gk = jax.random.key(seed)
        x = -0.000202 + 1 * jax.random.normal(jax.random.fold_in(_gk, 1), (6250, 128), jnp.float32)
        _s = jax.random.randint(jax.random.fold_in(_gk, 2), (50000,), 0, 6250, jnp.int32)
        _d = jax.random.randint(jax.random.fold_in(_gk, 3), (50000,), 0, 6250, jnp.int32)
        _loop = jnp.arange(6250, dtype=jnp.int32)
        src = jnp.concatenate([_s, _d, _loop])
        dst = jnp.concatenate([_d, _s, _loop])
        _o = jnp.argsort(dst, stable=True)
        src = src[_o]
        dst = dst[_o]
        edge_attr_64 = 0.000102155 + 1.00015 * jax.random.normal(jax.random.fold_in(_gk, 12), (106250, 64), jnp.float32)
        edge_weight = jax.random.uniform(jax.random.fold_in(_gk, 14), (106250,), jnp.float32, 0.0, 0.999999)
        return (x, src, dst, edge_attr_64, edge_weight)
    x, src, dst, edge_attr_64, edge_weight = _rec_inputs()

    def _L0_gnn_setup():
        import jax, jax.numpy as jnp
        import numpy as np
        N, E, F_IN, H, C = (6250, 100000, 128, 4, 32)
        NEG_SLOPE = 0.2
        key = jax.random.key(seed)
        k1, k2, k3, k4, k5, k6, k7 = jax.random.split(key, 7)
        nodes = jax.random.normal(k1, (N, F_IN), dtype=jnp.float32)
        senders = jax.random.randint(k2, (E,), 0, N, dtype=jnp.int32)
        receivers = jax.random.randint(k3, (E,), 0, N, dtype=jnp.int32)
        W = jax.random.normal(k4, (F_IN, H * C), dtype=jnp.float32) / np.sqrt(F_IN)
        b_lin = jnp.zeros((H * C,), dtype=jnp.float32)
        alpha = jax.random.normal(k5, (1, H, 2 * C), dtype=jnp.float32)
        bias = jnp.zeros((H * C,), dtype=jnp.float32)
        return {'nodes': nodes, 'senders': senders, 'receivers': receivers, 'W': W, 'b_lin': b_lin, 'alpha': alpha, 'bias': bias}
    _L0_gnn_all = _L0_gnn_setup()
    _L0_gnn_in = {k: v for k, v in _L0_gnn_all.items() if k in ('W', 'b_lin', 'alpha', 'bias')}
    del _L0_gnn_all

    def _L1_gnn_setup():
        import jax, jax.numpy as jnp
        import numpy as np
        N_NODES = 12500
        N_EDGES = 62500
        IN_CH = 128
        EDGE_CH = 64

        def _glorot(key, shape):
            fan_in, fan_out = (shape[0], shape[1])
            lim = (6.0 / (fan_in + fan_out)) ** 0.5
            return jax.random.uniform(key, shape, jnp.float32, -lim, lim)
        key = jax.random.key(seed)
        ks = jax.random.split(key, 14)
        x = jax.random.normal(ks[0], (N_NODES, IN_CH), jnp.float32)
        edge_index = jax.random.randint(ks[1], (2, N_EDGES), 0, N_NODES, jnp.int64)
        edge_attr = jax.random.normal(ks[2], (N_EDGES, EDGE_CH), jnp.float32)
        timestamps = jax.random.uniform(ks[3], (N_EDGES,), jnp.float32)
        We1 = _glorot(ks[4], (EDGE_CH, 2 * EDGE_CH))
        be1 = jnp.zeros((2 * EDGE_CH,), jnp.float32)
        We2 = _glorot(ks[5], (2 * EDGE_CH, IN_CH))
        be2 = jnp.zeros((IN_CH,), jnp.float32)
        Wt = _glorot(ks[6], (1, IN_CH))
        bt = jnp.zeros((IN_CH,), jnp.float32)
        Wn1 = _glorot(ks[7], (2 * IN_CH, IN_CH))
        bn1 = jnp.zeros((IN_CH,), jnp.float32)
        Wn2 = _glorot(ks[8], (IN_CH, IN_CH))
        bn2 = jnp.zeros((IN_CH,), jnp.float32)
        return {'x': x, 'edge_index': edge_index, 'edge_attr': edge_attr, 'timestamps': timestamps, 'We1': We1, 'be1': be1, 'We2': We2, 'be2': be2, 'Wt': Wt, 'bt': bt, 'Wn1': Wn1, 'bn1': bn1, 'Wn2': Wn2, 'bn2': bn2}
    _L1_gnn_all = _L1_gnn_setup()
    _L1_gnn_in = {k: v for k, v in _L1_gnn_all.items() if k in ('We1', 'be1', 'We2', 'be2', 'Wt', 'bt', 'Wn1', 'bn1', 'Wn2', 'bn2')}
    del _L1_gnn_all
    return {'x': x, 'src': src, 'dst': dst, 'edge_attr_64': edge_attr_64, 'edge_weight': edge_weight, 'L0_gnn_W': _L0_gnn_in['W'], 'L0_gnn_b_lin': _L0_gnn_in['b_lin'], 'L0_gnn_alpha': _L0_gnn_in['alpha'], 'L0_gnn_bias': _L0_gnn_in['bias'], 'L1_gnn_We1': _L1_gnn_in['We1'], 'L1_gnn_be1': _L1_gnn_in['be1'], 'L1_gnn_We2': _L1_gnn_in['We2'], 'L1_gnn_be2': _L1_gnn_in['be2'], 'L1_gnn_Wt': _L1_gnn_in['Wt'], 'L1_gnn_bt': _L1_gnn_in['bt'], 'L1_gnn_Wn1': _L1_gnn_in['Wn1'], 'L1_gnn_bn1': _L1_gnn_in['bn1'], 'L1_gnn_Wn2': _L1_gnn_in['Wn2'], 'L1_gnn_bn2': _L1_gnn_in['bn2']}

def reference(x, src, dst, edge_attr_64, edge_weight, L0_gnn_W, L0_gnn_b_lin, L0_gnn_alpha, L0_gnn_bias, L1_gnn_We1, L1_gnn_be1, L1_gnn_We2, L1_gnn_be2, L1_gnn_Wt, L1_gnn_bt, L1_gnn_Wn1, L1_gnn_bn1, L1_gnn_Wn2, L1_gnn_bn2):
    import jax
    import jax.numpy as jnp

    def _L0_gnn_ref(nodes, senders, receivers, W, b_lin, alpha, bias):
        import jax, jax.numpy as jnp
        import numpy as np
        N, E, F_IN, H, C = (6250, 100000, 128, 4, 32)
        NEG_SLOPE = 0.2
        n = nodes.shape[0]
        x = nodes @ W + b_lin
        loop = jnp.arange(n, dtype=senders.dtype)
        snd = jnp.concatenate([senders, loop])
        rcv = jnp.concatenate([receivers, loop])
        sent = x[snd]
        recvd = x[rcv]
        feat = jnp.concatenate([sent, recvd], axis=1).reshape(-1, H, 2 * C)
        logits = jnp.sum(feat * alpha, axis=-1)
        logits = jax.nn.leaky_relu(logits, negative_slope=NEG_SLOPE)
        seg_max = jax.ops.segment_max(logits, rcv, num_segments=n)
        e = jnp.exp(logits - seg_max[rcv])
        denom = jax.ops.segment_sum(e, rcv, num_segments=n)
        att = e / denom[rcv]
        msgs = att[:, :, None] * sent.reshape(-1, H, C)
        out = jax.ops.segment_sum(msgs, rcv, num_segments=n)
        out = out.reshape(-1, H * C)
        out = out + bias
        return out

    def _L1_gnn_ref(x, edge_index, edge_attr, timestamps, We1, be1, We2, be2, Wt, bt, Wn1, bn1, Wn2, bn2):
        import jax, jax.numpy as jnp
        import numpy as np
        N_NODES = 12500
        N_EDGES = 62500
        IN_CH = 128
        EDGE_CH = 64

        def _glorot(key, shape):
            fan_in, fan_out = (shape[0], shape[1])
            lim = (6.0 / (fan_in + fan_out)) ** 0.5
            return jax.random.uniform(key, shape, jnp.float32, -lim, lim)
        ts = timestamps[:, None]
        ef = jax.nn.relu(edge_attr @ We1 + be1) @ We2 + be2
        tw = jax.nn.sigmoid(ts @ Wt + bt)
        ef = ef * tw
        row, col = (edge_index[0], edge_index[1])
        combined = jnp.concatenate([x[row], ef], axis=1)
        msg = jax.nn.relu(combined @ Wn1 + bn1) @ Wn2 + bn2
        out = jax.ops.segment_sum(msg, col, num_segments=x.shape[0])
        return out + x
    edge_index = jnp.stack([src, dst])
    h = jnp.maximum(_layernorm(x, axis=-1), 0.0)
    x = x + _L0_gnn_ref(h, src, dst, L0_gnn_W, L0_gnn_b_lin, L0_gnn_alpha, L0_gnn_bias)
    h = jnp.maximum(_layernorm(x, axis=-1), 0.0)
    x = x + _L1_gnn_ref(h, edge_index, edge_attr_64, edge_weight, L1_gnn_We1, L1_gnn_be1, L1_gnn_We2, L1_gnn_be2, L1_gnn_Wt, L1_gnn_bt, L1_gnn_Wn1, L1_gnn_bn1, L1_gnn_Wn2, L1_gnn_bn2)
    return x

_drawn_inputs = setup_inputs


def setup_inputs(seed=0):
    import zlib

    import numpy as np

    out = dict(_drawn_inputs(seed))
    spreads = {'L0_gnn_b_lin': (0.0, 0.1),
     'L0_gnn_bias': (0.0, 0.1),
     'L1_gnn_be1': (0.0, 0.32),
     'L1_gnn_be2': (0.0, 0.1),
     'L1_gnn_bt': (0.0, 0.64),
     'L1_gnn_bn1': (0.0, 0.1),
     'L1_gnn_bn2': (0.0, 0.1)}
    factors = {'edge_weight': 8.0, 'L1_gnn_Wt': 6.954}
    for name, (base, spread) in spreads.items():
        noise = np.random.default_rng([zlib.crc32(name.encode()), seed]).standard_normal(out[name].shape)
        drawn = base * np.exp(spread * noise) if base else spread * noise
        out[name] = jnp.asarray(drawn.astype(out[name].dtype))
    for name, factor in factors.items():
        out[name] = (out[name] * factor).astype(out[name].dtype)
    return out
```

```python
from contextlib import ExitStack

import concourse.bass as bass
from concourse import mybir
from concourse.alu_op_type import AluOpType as ALU

P = 128
N = 6250
E = 106250
CH = 128
EC = 64
HEADS = 4
HC = CH // HEADS
SH = 2
NB = (N + P - 1) // P
NPAD = NB * P
CB = 7
CHUNKS = NB // CB
TG = 4
GE = TG * P
RG = 8
HALF = RG // 2
GROUPS = -(-E // (GE * RG)) * RG
TILES = GROUPS * TG
ROUNDS = GROUPS // RG
EPAD = TILES * P
RT = RG * TG
ACCW = (N + P + P - 1) // P * P
BIG = 1.0e38
EPS = 1e-5
LCOL = 5


def gnn_layers(nc, a, out, table1, table2, lo_dram, lin_dram, w_dram, carry_dram, carried_dram):
    fp32, bf16, i32 = mybir.dt.float32, mybir.dt.bfloat16, mybir.dt.int32
    ACT = mybir.ActivationFunctionType
    AX = mybir.AxisListType
    ds = bass.ds

    ctx = ExitStack()
    with ctx:
        ctx.enter_context(nc.allow_non_contiguous_dma(reason="columns of 128 numbers"))

        def sb(name, shape, dt=fp32, st=ctx):
            return st.enter_context(nc.sbuf_tensor(name, shape, dt))

        def sem(name):
            return ctx.enter_context(nc.semaphore(name))

        bank = [ctx.enter_context(nc.psum_tensor(f"bank{n}", [P, 512], fp32)) for n in range(8)]

        x_rows = sb("x_rows", [P, NB, CH])
        feat = sb("feat", [P, NB, CH])
        logit = sb("logit", [P, NB, HEADS])
        acc = sb("acc", [P, ACCW])
        acc_w = sb("acc_w", [LCOL, ACCW])
        ident = sb("ident", [P, P])
        iota_row = sb("iota_row", [P, P])
        iota_col = sb("iota_col", [P, 1])
        iota_int = sb("iota_int", [P, P], i32)
        iota_cint = sb("iota_cint", [P, 1], i32)
        eps_col = sb("eps_col", [P, 1])
        dst_rel = sb("dst_rel", [P, TILES])
        dst_first = sb("dst_first", [1, TILES], i32)
        edge_w = sb("edge_w", [P, TILES, LCOL])
        rows = sb("rows", [P, RG, TG, CH])
        index = sb("index", [P, RG, TG], i32)
        onehot = sb("onehot", [P, 2, TG, P])
        wl_node = sb("wl_node", [LCOL, CH])
        wn2 = sb("wn2", [P, CH])

        with ExitStack() as st:
            normed = sb("normed", [P, 3, CB, CH], st=st)
            squares = sb("squares", [P, 2, CB, CH], st=st)
            feats_t = sb("feats_t", [P, 2, CB * P], st=st)
            nmean = sb("nmean", [P, NB], st=st)
            sums = sb("sums", [P, NB], st=st)
            sqsum = sb("sqsum", [P, NB], st=st)
            std = sb("std", [P, NB], st=st)
            rstd = sb("rstd", [P, NB], st=st)
            w0 = sb("w0", [P, CH], st=st)
            w0_t = sb("w0_t", [P, CH], st=st)
            w0_ext = sb("w0_ext", [P, CH + HEADS], st=st)
            alpha_bd = sb("alpha_bd", [P, HEADS], st=st)
            blin_col = sb("blin_col", [P, 1], st=st)
            blin_rep = sb("blin_rep", [P, P], st=st)
            bias_ext = sb("bias_ext", [P, CH + HEADS], st=st)
            zlogit = sb("zlogit", [P, NB, HEADS], st=st)

            x_in, w_in, const_set, iota_done, sel_done = (sem(n) for n in ("x_in", "w_in", "const_set", "iota_done", "sel_done"))
            chain = sem("a_chain")
            w_t, w_tc, wa_done, wa_copied, ba_ready = (sem(n) for n in ("w_t", "w_tc", "wa_done", "wa_copied", "ba_ready"))
            centred, squared, varsum, std_done, norm_done, turned, relu_done, projected, rows_done, table_out = (
                sem(n) for n in ("centred", "squared", "varsum", "std_done", "norm_done", "turned", "relu_done",
                                 "projected", "rows_done", "table_out"))
            zero_done = sem("zero_done")
            small_sync = sem("small_sync")
            with nc.Block() as block:
                @block.sync
                def _(sp):
                    sp.dma_start(x_rows[:, :, :], a["x"].rearrange("(b p) c -> p b c", p=P)).then_inc(x_in, 16)
                    sp.dma_start(wn2[:, :], a["Wn2"]).then_inc(w_in, 16)
                    for c in range(CHUNKS):
                        sp.wait_ge(rows_done, 3 * (c + 1))
                        sp.dma_start(table1[c * CB * P:(c + 1) * CB * P, :].rearrange("(b p) c -> p b c", p=P),
                                     feat[:, c * CB:(c + 1) * CB, :]).then_inc(table_out, 16)
                    sp.wait_ge(table_out, 16 * CHUNKS)

                @block.gpsimd
                def _(gp):
                    gp.iota(iota_int[:, :], pattern=[[1, P]], base=0, channel_multiplier=0).then_inc(iota_done, 1)
                    gp.iota(iota_cint[:, :], pattern=[[1, 1]], base=0, channel_multiplier=1).then_inc(iota_done, 1)
                    gp.memset(ident[:, :], 0.0).then_inc(sel_done, 1)
                    gp.wait_ge(sel_done, 1)
                    gp.affine_select(out=ident[:, :], in_=ident[:, :], compare_op=ALU.not_equal, fill=1.0, base=0,
                                     pattern=[[-1, P]], channel_multiplier=1).then_inc(sel_done, 1)
                    gp.memset(eps_col[:, :], EPS).then_inc(sel_done, 1)
                    gp.memset(alpha_bd[:, :], 0.0).then_inc(const_set, 1)
                    gp.memset(wl_node[:, :], 0.0).then_inc(const_set, 1)
                    gp.memset(acc[:, :], 0.0).then_inc(zero_done, 1)
                    gp.memset(acc_w[:, :], 0.0).then_inc(zero_done, 1)
                    gp.wait_ge(zero_done, 2)

                @block.scalar
                def _(act):
                    act.dma_start(w0[:, :], a["W"]).then_inc(w_in, 16)
                    act.dma_start(blin_col[:, :], a["b_lin"].rearrange("(c o) -> c o", o=1)).then_inc(w_in, 16)
                    act.dma_start(bias_ext[:, 0:CH], a["b_lin"].partition_broadcast(P)).then_inc(w_in, 16)
                    act.wait_ge(const_set, 2)
                    for h in range(HEADS):
                        half = (h % 2) * 64
                        act.dma_start(alpha_bd[half:half + 64, h:h + 1],
                                      a["alpha"][0, h, :].rearrange("(c o) -> c o", o=1)).then_inc(w_in, 16)
                    act.dma_start(wl_node[2:3, :], a["bn2"].rearrange("(o c) -> o c", o=1)).then_inc(w_in, 16)
                    act.wait_ge(w_in, 16 * 9)
                    act.wait_ge(sel_done, 3)
                    act.activation(blin_rep[:, :], ident[:, :], ACT.Identity, bias=blin_col[:, 0:1], scale=0.0).then_inc(w_tc, 1)
                    act.wait_ge(w_t, 1)
                    act.copy(w0_t[:, :], bank[0][:, 0:P]).then_inc(w_tc, 1)
                    act.wait_ge(wa_done, 1)
                    act.copy(w0_ext[:, 0:CH], w0[:, :]).then_inc(wa_copied, 1)
                    act.copy(w0_ext[:, CH:CH + HEADS], bank[1][:, 0:HEADS]).then_inc(wa_copied, 1)
                    act.copy(bias_ext[:, CH:CH + HEADS], bank[1][:, 8:8 + HEADS]).then_inc(ba_ready, 1)

                    def square(c):
                        act.wait_ge(centred, c + 1)
                        if c >= 2:
                            act.wait_ge(varsum, c - 1)
                        act.activation(squares[:, c % 2], normed[:, c % 3], ACT.Square).then_inc(squared, 1)

                    def root(c):
                        act.wait_ge(varsum, c + 1)
                        act.activation(std[:, c * CB:(c + 1) * CB], sqsum[:, c * CB:(c + 1) * CB], ACT.Sqrt,
                                       bias=eps_col[:, 0:1], scale=1.0 / CH).then_inc(std_done, 1)

                    def turn_relu(c):
                        act.wait_ge(turned, c + 1)
                        if c >= 2:
                            act.wait_ge(projected, c - 1)
                        act.activation(feats_t[:, c % 2, 0:4 * P], bank[2][:, :], ACT.Relu).then_inc(relu_done, 1)
                        act.activation(feats_t[:, c % 2, 4 * P:], bank[3][:, 0:3 * P], ACT.Relu).then_inc(relu_done, 1)
                    for s in range(CHUNKS + 2):
                        if s < CHUNKS:
                            square(s)
                            root(s)
                        if s >= 1 and s - 1 < CHUNKS:
                            turn_relu(s - 1)

                @block.vector
                def _(dve):
                    n = [0]

                    def link(ins):
                        n[0] += 1
                        ins.then_inc(chain, 1)
                        dve.wait_ge(chain, n[0])

                    dve.wait_ge(iota_done, 2)
                    link(dve.tensor_copy(iota_row[:, :], iota_int[:, :]))
                    link(dve.tensor_copy(iota_col[:, :], iota_cint[:, :]))
                    dve.wait_ge(x_in, 16)

                    def centre(c):
                        blk = slice(c * CB, (c + 1) * CB)
                        link(dve.tensor_reduce(sums[:, blk], x_rows[:, blk, :], AX.X, ALU.add))
                        link(dve.tensor_scalar(nmean[:, blk], sums[:, blk], -1.0 / CH, None, ALU.mult))
                        if c >= 3:
                            dve.wait_ge(turned, c - 2)
                        dve.tensor_tensor(normed[:, c % 3], x_rows[:, blk, :],
                                          nmean[:, blk].unsqueeze(2).broadcast_to([P, CB, CH]), ALU.add).then_inc(centred, 1)

                    def variance(c):
                        dve.wait_ge(squared, c + 1)
                        dve.tensor_reduce(sqsum[:, c * CB:(c + 1) * CB], squares[:, c % 2], AX.X, ALU.add).then_inc(varsum, 1)

                    def scale(c):
                        blk = slice(c * CB, (c + 1) * CB)
                        dve.wait_ge(std_done, c + 1)
                        link(dve.reciprocal(rstd[:, blk], std[:, blk]))
                        dve.tensor_tensor(normed[:, c % 3], normed[:, c % 3],
                                          rstd[:, blk].unsqueeze(2).broadcast_to([P, CB, CH]), ALU.mult).then_inc(norm_done, 1)

                    def evacuate(c):
                        if c == 0:
                            dve.wait_ge(ba_ready, 1)
                            dve.wait_ge(w_in, 16 * 9)
                        dve.wait_ge(projected, c + 1)
                        for b0, m, bk in ((0, 3, 4), (3, 3, 5), (6, 1, 6)):
                            ps = bank[bk][:, 0:m * (CH + HEADS)].rearrange("p (m n) -> p m n", m=m)
                            at = slice(c * CB + b0, c * CB + b0 + m)
                            dve.tensor_tensor(feat[:, at, :], ps[:, :, 0:CH],
                                              bias_ext[:, 0:CH].unsqueeze(1).broadcast_to([P, m, CH]), ALU.add).then_inc(rows_done, 1)
                            dve.tensor_tensor(zlogit[:, at, :], ps[:, :, CH:],
                                              bias_ext[:, CH:].unsqueeze(1).broadcast_to([P, m, HEADS]), ALU.add).then_inc(small_sync, 1)
                    for s in range(CHUNKS + 2):
                        if s < CHUNKS:
                            centre(s)
                            variance(s)
                            scale(s)
                        if s >= 2:
                            evacuate(s - 2)
                    dve.wait_ge(small_sync, 3 * CHUNKS)
                    dve.scalar_tensor_tensor(logit[:, :, :].rearrange("p b h -> p (b h)"), zlogit[:, :, :].rearrange("p b h -> p (b h)"), 0.2,
                                             zlogit[:, :, :].rearrange("p b h -> p (b h)"), ALU.mult, ALU.max).then_inc(small_sync, 1)
                    dve.wait_ge(small_sync, 3 * CHUNKS + 1)

                @block.tensor
                def _(pe):
                    pe.wait_ge(w_in, 16 * 9)
                    pe.wait_ge(sel_done, 3)
                    pe.transpose(bank[0][:, 0:P], w0[:, :], ident[:, :]).then_inc(w_t, 1)
                    pe.wait_ge(w_tc, 2)
                    pe.matmul(bank[1][:, 0:HEADS], w0_t[:, :], alpha_bd[:, :], start=True, stop=True)
                    pe.matmul(bank[1][:, 8:8 + HEADS], blin_rep[:, :], alpha_bd[:, :], start=True, stop=True).then_inc(wa_done, 1)

                    def turn(c):
                        pe.wait_ge(norm_done, c + 1)
                        if c >= 1:
                            pe.wait_ge(relu_done, 2 * c)
                        for b in range(CB):
                            last = pe.transpose(bank[2 + b // 4][:, b % 4 * P:(b % 4 + 1) * P], normed[:, c % 3, b, :], ident[:, :])
                        last.then_inc(turned, 1)

                    def project(c):
                        if c == 0:
                            pe.wait_ge(wa_copied, 2)
                        pe.wait_ge(relu_done, 2 * (c + 1))
                        if c >= 1:
                            pe.wait_ge(small_sync, 3 * c)
                            pe.wait_ge(rows_done, 3 * c)
                        for b in range(CB):
                            o = b % 3 * (CH + HEADS)
                            last = pe.matmul(bank[4 + b // 3][:, o:o + CH + HEADS], feats_t[:, c % 2, b * P:(b + 1) * P],
                                             w0_ext[:, :], start=True, stop=True)
                        last.then_inc(projected, 1)
                    for s in range(CHUNKS + 1):
                        if s < CHUNKS:
                            turn(s)
                        if s >= 1:
                            project(s - 1)

        with ExitStack() as st:
            src_lin = sb("src_lin", [P, EPAD // P], i32, st)
            lo_int = sb("lo_int", [P, EPAD // P], i32, st)
            lo_bf = sb("lo_bf", [P, EPAD // P], bf16, st)
            hi_int = sb("hi_int", [P, TILES], i32, st)
            src_hi = sb("src_hi", [P, TILES], st=st)
            tab = sb("tab", [P, 3, SH, NB], bf16, st)
            tab_rest = sb("tab_rest", [P, SH, NB], st=st)
            lo_all = sb("lo_all", [P, 2, HALF * GE], bf16, st)
            onehot_lo = sb("onehot_lo", [P, 2, GE], bf16, st)
            onehot_hi = sb("onehot_hi", [P, 2, TG, NB], bf16, st)
            iota_hi = sb("iota_hi", [P, NB], bf16, st)
            picked = sb("picked", [P, 2, TG * SH, NB], st=st)
            edge_logit = sb("edge_logit", [P, TILES, SH], st=st)
            dst_int = sb("dst_int", [P, TILES], i32, st)
            first_all = sb("first_all", [P, TILES], i32, st)

            idx_in, prep, lo_out, hi_ready, ohl_done, ohh_done, sel_prod, pick_done, red_done = (
                sem(n) for n in ("idx_in", "prep", "lo_out", "hi_ready", "ohl_done", "ohh_done", "sel_prod", "pick_done", "red_done"))
            lo_in = [sem(f"lo_in{h}") for h in range(2)]
            with nc.Block() as block:
                @block.sync
                def _(sp):
                    sp.dma_start(src_lin[:, :], a["src_lin"]).then_inc(idx_in, 16)
                    sp.dma_start(hi_int[:, :], a["src_tile"]).then_inc(idx_in, 16)
                    sp.dma_start(dst_int[:, :], a["dst_tile"]).then_inc(idx_in, 16)
                    sp.dma_start(first_all[:, :], a["dst_first"].rearrange("o t -> (o t)").partition_broadcast(P)).then_inc(idx_in, 16)
                    sp.dma_start(dst_first[:, :], a["dst_first"]).then_inc(idx_in, 16)
                    sp.wait_ge(prep, 2)
                    sp.dma_start(lo_dram.rearrange("(p n) -> p n", p=P), lo_bf[:, :]).then_inc(lo_out, 16)
                    sp.wait_ge(lo_out, 16)

                    def load(i, first):
                        for h in range(2):
                            if not first:
                                sp.wait_ge(ohl_done, RG * (i - 1) + HALF * (h + 1))
                            sp.dma_start(lo_all[:, h, :], lo_dram[ds((i * RG + h * HALF) * GE, HALF * GE)].partition_broadcast(P)).then_inc(lo_in[h], 16)
                    load(0, True)
                    with sp.Fori(1, ROUNDS) as i:
                        load(i, False)

                @block.vector
                def _(dve):
                    n = [0]

                    def link(ins):
                        n[0] += 1
                        ins.then_inc(prep, 1)
                        dve.wait_ge(prep, n[0])
                    dve.wait_ge(idx_in, 16 * 5)
                    link(dve.tensor_scalar(lo_int[:, :], src_lin[:, :], P - 1, None, ALU.bitwise_and))
                    link(dve.tensor_copy(lo_bf[:, :], lo_int[:, :]))
                    link(dve.tensor_scalar(hi_int[:, :], hi_int[:, :], 7, None, ALU.logical_shift_right))
                    link(dve.tensor_copy(src_hi[:, :], hi_int[:, :]))
                    link(dve.tensor_tensor(dst_rel[:, :], dst_int[:, :], first_all[:, :], ALU.subtract))
                    link(dve.tensor_copy(iota_hi[:, :], iota_row[:, 0:NB]))
                    link(dve.tensor_copy(tab_rest[:, :, :], logit[:, :, 0:SH].rearrange("p b h -> p h b")))
                    for part in range(3):
                        link(dve.tensor_copy(tab[:, part], tab_rest[:, :, :]))
                        if part < 2:
                            link(dve.tensor_tensor(tab_rest[:, :, :], tab_rest[:, :, :], tab[:, part], ALU.subtract))
                    dve.memset(edge_w[:, :, :], 1.0).then_inc(hi_ready, 1)

                    def masks(i, k, first):
                        if k % HALF == 0:
                            dve.wait_ge(lo_in[k // HALF], 16 * (i + 1))
                        if not (first and k < 2):
                            dve.wait_ge(pick_done, i * RG + k - 1)
                            dve.wait_ge(sel_prod, i * RG + k - 1)
                        dve.tensor_scalar(onehot_lo[:, k % 2], lo_all[:, k // HALF, k % HALF * GE:(k % HALF + 1) * GE],
                                          iota_col[:, 0:1], None, ALU.is_equal).then_inc(ohl_done, 1)
                        dve.tensor_tensor(onehot_hi[:, k % 2], iota_hi[:, :].unsqueeze(1).broadcast_to([P, TG, NB]),
                                          src_hi[:, ds(i * RT + k * TG, TG)].unsqueeze(2).broadcast_to([P, TG, NB]),
                                          ALU.is_equal).then_inc(ohh_done, 1)

                    def pick(i, k):
                        dve.wait_ge(pick_done, i * RG + k + 1)
                        dve.wait_ge(ohh_done, i * RG + k + 1)
                        dve.tensor_tensor(picked[:, k % 2].rearrange("p (t h) b -> p t h b", h=SH),
                                          bank[k % 2][:, 0:TG * SH * NB].rearrange("p (t h b) -> p t h b", t=TG, h=SH),
                                          onehot_hi[:, k % 2].unsqueeze(2).broadcast_to([P, TG, SH, NB]), ALU.mult).then_inc(sel_prod, 1)
                        dve.wait_ge(sel_prod, i * RG + k + 1)
                        dve.tensor_reduce(edge_logit[:, ds(i * RT + k * TG, TG), :].rearrange("p t h -> p (t h)"),
                                          picked[:, k % 2], AX.X, ALU.add).then_inc(red_done, 1)

                    def steps(i, first):
                        for k in range(RG):
                            masks(i, k, first)
                            if k:
                                pick(i, k - 1)
                            elif not first:
                                pick(i - 1, RG - 1)
                    steps(0, True)
                    with dve.Fori(1, ROUNDS) as i:
                        steps(i, False)
                    pick(ROUNDS - 1, RG - 1)
                    dve.wait_ge(red_done, GROUPS)
                    dve.wait_ge(hi_ready, 1)

                @block.tensor
                def _(pe):
                    pe.wait_ge(prep, 12)

                    def look(i, k, first):
                        pe.wait_ge(ohl_done, i * RG + k + 1)
                        if not (first and k < 2):
                            pe.wait_ge(sel_prod, i * RG + k - 1)
                        for t in range(TG):
                            for part in range(3):
                                last = pe.matmul(bank[k % 2][:, t * SH * NB:(t + 1) * SH * NB], onehot_lo[:, k % 2, t * P:(t + 1) * P],
                                                 tab[:, part].rearrange("p h b -> p (h b)"), start=(part == 0), stop=(part == 2))
                        last.then_inc(pick_done, 1)
                    for k in range(RG):
                        look(0, k, True)
                    with pe.Fori(1, ROUNDS) as i:
                        for k in range(RG):
                            look(i, k, False)

            turned_l = sb("turned_l", [P, SH, 7, P], st=st)
            t_done, t_copied, lin_out = (sem(n) for n in ("t_done", "t_copied", "lin_out"))
            TB = [(b * P, min(P, TILES - b * P)) for b in range((TILES + P - 1) // P)]
            with nc.Block() as block:
                @block.tensor
                def _(pe):
                    for b, (t0, m) in enumerate(TB):
                        if b >= 4:
                            pe.wait_ge(t_copied, b - 3)
                        for h in range(SH):
                            last = pe.transpose(bank[b % 4][0:m, h * P:(h + 1) * P], edge_logit[:, t0:t0 + m, h], ident[:, :])
                        last.then_inc(t_done, 1)

                @block.scalar
                def _(act):
                    for b, (t0, m) in enumerate(TB):
                        act.wait_ge(t_done, b + 1)
                        act.copy(turned_l[0:m, :, b, :], bank[b % 4][0:m, 0:SH * P].rearrange("p (h n) -> p h n", h=SH)).then_inc(t_copied, 1)

                @block.sync
                def _(sp):
                    for b, (t0, m) in enumerate(TB):
                        sp.wait_ge(t_copied, b + 1)
                        sp.dma_start(lin_dram[:, t0 * P:(t0 + m) * P].rearrange("h (t p) -> t h p", p=P), turned_l[0:m, :, b, :]).then_inc(lin_out, 16)
                    sp.wait_ge(lin_out, 16 * len(TB))

        with ExitStack() as st:
            L = EPAD // P
            lg = sb("lg", [P, SH, L], st=st)
            dn = sb("dn", [P, 3, L], i32, st)
            starts = sb("starts", [P, L], st=st)
            ends = sb("ends", [P, L], st=st)
            pen_f = sb("pen_f", [P, L], st=st)
            pen_b = sb("pen_b", [P, L], st=st)
            run = sb("run", [P, SH, L], st=st)
            run2 = sb("run2", [P, SH, L], st=st)
            res = sb("res", [P, 2 * SH, L], st=st)
            cols = sb("cols", [P, 2, SH + 1], st=st)
            rowv = sb("rowv", [1, 2, SH + 1, P], st=st)
            rowc = sb("rowc", [1, 2, SH, P + 1], st=st)
            carry = sb("carry", [P, 2, SH], st=st)
            blocks_w = rows[:, :, :, :].rearrange("p g t c -> p (g t c)")[:, 0:2 * SH * 7 * P].rearrange("p (k b n) -> p k b n", k=2 * SH, b=7)
            lg_in, sc, col_out, row_in, carry_out, carry_in, col_ready, row_ready, m_ready, w_exp, res_ready, res_out, bl_in, bt_done, bt_copied = (
                sem(n) for n in ("lg_in", "sc", "col_out", "row_in", "carry_out", "carry_in", "col_ready", "row_ready",
                                 "m_ready", "w_exp", "res_ready", "res_out", "bl_in", "bt_done", "bt_copied"))
            FB = TILES // P
            REST = TILES - FB * P
            with nc.Block() as block:
                @block.sync
                def _(sp):
                    sp.dma_start(lg[:, :, :], lin_dram.rearrange("h (p n) -> p h n", p=P)).then_inc(lg_in, 16)
                    for j in range(3):
                        sp.dma_start(dn[:, j, :], a["dst_line"][j:j + EPAD].rearrange("(p n) -> p n", p=P)).then_inc(lg_in, 16)
                    for way in range(2):
                        sp.wait_ge(col_ready, way + 1)
                        sp.dma_start(carry_dram[way], cols[:, way, :]).then_inc(col_out, 16)
                        sp.wait_ge(col_out, 16 * (way + 1))
                        sp.dma_start(rowv[:, way], carry_dram[way:way + 1].rearrange("o q k -> o k q")).then_inc(row_in, 16)
                        sp.wait_ge(row_ready, way + 1)
                        sp.dma_start(carried_dram[way:way + 1, :, :], rowc[:, way, :, way:way + P]).then_inc(carry_out, 16)
                        sp.wait_ge(carry_out, 16 * (way + 1))
                        sp.dma_start(carry[:, way], carried_dram[way].rearrange("k q -> q k")).then_inc(carry_in, 16)
                    sp.wait_ge(res_ready, 1)
                    sp.wait_ge(w_exp, 1)
                    sp.dma_start(w_dram.rearrange("k (p n) -> p k n", p=P), res[:, :, :]).then_inc(res_out, 16)
                    sp.wait_ge(res_out, 16)
                    for k in range(2 * SH):
                        sp.dma_start(blocks_w[:, k, 0:FB, :], w_dram[k, 0:FB * P * P].rearrange("(b t p) -> t b p", t=P, p=P)).then_inc(bl_in, 16)
                    sp.dma_start(blocks_w[0:REST, :, FB, :], w_dram[:, FB * P * P:].rearrange("k (t p) -> t k p", p=P)).then_inc(bl_in, 16)

                @block.vector
                def _(dve):
                    n = [0]

                    def link(ins):
                        n[0] += 1
                        ins.then_inc(sc, 1)
                        dve.wait_ge(sc, n[0])
                    dve.wait_ge(lg_in, 16 * 4)
                    link(dve.tensor_tensor(starts[:, :], dn[:, 0, :], dn[:, 1, :], ALU.not_equal))
                    link(dve.tensor_tensor(ends[:, :], dn[:, 2, :], dn[:, 1, :], ALU.not_equal))
                    link(dve.tensor_scalar(pen_f[:, :], starts[:, :], -BIG, None, ALU.mult))
                    link(dve.tensor_scalar(pen_b[:, :], ends[:, :], -BIG, None, ALU.mult))
                    link(dve.tensor_reduce(cols[:, 0, SH:SH + 1], pen_f[:, :], AX.X, ALU.min))
                    link(dve.tensor_reduce(cols[:, 1, SH:SH + 1], pen_b[:, :], AX.X, ALU.min))
                    link(dve.memset(rowc[:, :, :, :], -BIG))
                    for way, (pen, src, dst) in enumerate(((pen_f, lg, run), (pen_b, run, run2))):
                        back = way == 1

                        def line(v):
                            return v[:, ::-1] if back else v
                        for h in range(SH):
                            link(dve.tensor_tensor_scan(line(run2[:, h, :]), line(pen[:, :]), line(src[:, h, :]), -BIG, ALU.add, ALU.max))
                        end = 0 if back else L - 1
                        link(dve.tensor_copy(cols[:, way, 0:SH], run2[:, :, end:end + 1].rearrange("p h o -> p (h o)")))
                        dve.engine_nop().then_inc(col_ready, 1)
                        dve.wait_ge(row_in, 16 * (way + 1))
                        for h in range(SH):
                            o = rowc[:, way, h, 0:P] if back else rowc[:, way, h, 1:P + 1]
                            link(dve.tensor_tensor_scan(line(o), line(rowv[:, way, SH, :]), line(rowv[:, way, h, :]), -BIG, ALU.add, ALU.max))
                        dve.engine_nop().then_inc(row_ready, 1)
                        dve.wait_ge(carry_in, 16 * (way + 1))
                        for h in range(SH):
                            link(dve.tensor_tensor_scan(line(dst[:, h, :]), line(pen[:, :]), line(src[:, h, :]),
                                                        carry[:, way, h:h + 1], ALU.add, ALU.max))
                    link(dve.tensor_tensor(lg[:, :, :], lg[:, :, :], run2[:, :, :], ALU.subtract))
                    dve.engine_nop().then_inc(m_ready, 1)
                    dve.tensor_tensor(res[:, SH:, :], run2[:, :, :], ends[:, :].unsqueeze(1).broadcast_to([P, SH, L]), ALU.mult).then_inc(res_ready, 1)

                @block.scalar
                def _(act):
                    act.wait_ge(m_ready, 1)
                    act.activation(res[:, 0:SH, :], lg[:, :, :], ACT.Exp).then_inc(w_exp, 1)
                    for b in range(FB + 1):
                        m = P if b < FB else REST
                        act.wait_ge(bt_done, b + 1)
                        ps = bank[b % 4][:, :].rearrange("p (k n) -> p n k", k=2 * SH)
                        act.copy(edge_w[:, b * P:b * P + m, 0:SH], ps[:, 0:m, 0:SH]).then_inc(bt_copied, 1)
                        act.copy(edge_w[:, b * P:b * P + m, SH + 1:], ps[:, 0:m, SH:]).then_inc(bt_copied, 1)
                    act.wait_ge(bt_copied, 2 * (FB + 1))

                @block.tensor
                def _(pe):
                    pe.wait_ge(bl_in, 16 * (2 * SH + 1))
                    for b in range(FB + 1):
                        m = P if b < FB else REST
                        if b >= 4:
                            pe.wait_ge(bt_copied, 2 * (b - 3))
                        for k in range(2 * SH):
                            last = pe.transpose(bank[b % 4][:, k * P:k * P + m], blocks_w[0:m, k, b, :], ident[0:m, 0:m])
                        last.then_inc(bt_done, 1)

        idx_ready = [[sem(f"idx_ready{q}_{h}") for h in range(2)] for q in range(2)]
        gathered = [[sem(f"gathered{q}_{k}") for k in range(RG)] for q in range(2)]

        def load_indices(sp, q, i, h, first):
            if not first:
                for k in range(h * HALF, (h + 1) * HALF):
                    sp.wait_ge(gathered[q][k], 16 * TG * i)
            sp.dma_start(index[:, h * HALF:(h + 1) * HALF, :].rearrange("p g t -> p (g t)"),
                         a["src_tile"][:, ds(i * RT + h * HALF * TG, HALF * TG)]).then_inc(idx_ready[q][h], 16)

        slot_taken = sem("slot_taken")

        def gather(gp, q, table, i, k, first, used):
            if k % HALF == 0:
                gp.wait_ge(idx_ready[q][k // HALF], 16 * (i + 1))
            if not first:
                gp.wait_ge(used, RG * (i - 1) + k + 1)
            gp.sem_inc(slot_taken, 1)
            for t in range(TG):
                gp.indirect_dma_start(rows[:, k, t, :], None, table,
                                      bass.IndirectOffsetOnAxis(index[:, k, t:t + 1], 0)).then_inc(gathered[q][k], 16)

        def first_nodes(dve, regs, i, h):
            dve.load(regs, dst_first[0:1, ds(i * RT + h * HALF * TG, HALF * TG)])
            return [dve.snap(r, min_val=0, max_val=N) for r in regs]

        with ExitStack() as st:
            stat = sb("stat", [P, 2, TG, LCOL], st=st)
            oh0, scaled0, stat0, agg0, acc0, accw0 = (sem(n) for n in ("oh0", "scaled0", "stat0", "agg0", "acc0", "accw0"))
            with nc.Block() as block:
                @block.sync
                def _(sp):
                    for h in range(2):
                        load_indices(sp, 0, 0, h, True)
                    with sp.Fori(1, ROUNDS) as i:
                        for h in range(2):
                            load_indices(sp, 0, i, h, False)

                @block.gpsimd
                def _(gp):
                    for k in range(RG):
                        gather(gp, 0, table1, 0, k, True, agg0)
                    with gp.Fori(1, ROUNDS) as i:
                        for k in range(RG):
                            gather(gp, 0, table1, i, k, False, agg0)

                @block.scalar
                def _(act):
                    def weigh(i, k, first):
                        if not (first and k < 2):
                            act.wait_ge(agg0, i * RG + k - 1)
                        act.copy(stat[:, k % 2].rearrange("p t c -> p (t c)"),
                                 edge_w[:, ds(i * RT + k * TG, TG), :].rearrange("p t c -> p (t c)")).then_inc(stat0, 1)
                        act.wait_ge(gathered[0][k], 16 * TG * (i + 1))
                        act.wait_ge(stat0, i * RG + k + 1)
                        for t in range(TG):
                            for h in range(SH):
                                last = act.activation(rows[:, k, t, h * HC:(h + 1) * HC], rows[:, k, t, h * HC:(h + 1) * HC], ACT.Copy,
                                                      scale=stat[:, k % 2, t, h:h + 1])
                                last.then_inc(scaled0, 1)
                    for k in range(RG):
                        weigh(0, k, True)
                    with act.Fori(1, ROUNDS) as i:
                        for k in range(RG):
                            weigh(i, k, False)

                @block.vector
                def _(dve):
                    regs = [dve.alloc_register(f"first0_{n}") for n in range(HALF * TG)]

                    def masks(i, k, first):
                        if not (first and k < 2):
                            dve.wait_ge(agg0, i * RG + k - 1)
                        for t in range(TG):
                            dve.tensor_scalar(onehot[:, k % 2, t, :], iota_row[:, :], dst_rel[:, ds(i * RT + k * TG + t, 1)], None,
                                              ALU.is_equal).then_inc(oh0, 1)

                    def add(i, k, at):
                        dve.wait_ge(agg0, i * RG + k + 1)
                        for t in range(TG):
                            v = at[t]
                            if not (k == 0 and t == 0 and isinstance(i, int) and i == 0):
                                dve.wait_ge(acc0, (i * RG + k) * TG + t)
                                dve.wait_ge(accw0, (i * RG + k) * TG + t)
                            dve.tensor_tensor(acc[:, ds(v, P)], acc[:, ds(v, P)], bank[k % 2][:, t * P:(t + 1) * P], ALU.add).then_inc(acc0, 1)
                            dve.tensor_tensor(acc_w[:, ds(v, P)], acc_w[:, ds(v, P)], bank[2 + k % 2][0:LCOL, t * P:(t + 1) * P],
                                              ALU.add).then_inc(accw0, 1)

                    def steps(i, first):
                        for k in range(RG):
                            masks(i, k, first)
                            if k == 0 and not first:
                                add(i - 1, RG - 1, steps.at[-TG:])
                            elif k:
                                add(i, k - 1, steps.at[(k - 1) % HALF * TG:])
                            if k % HALF == 0:
                                steps.at = first_nodes(dve, regs, i, k // HALF)
                    steps(0, True)
                    with dve.Fori(1, ROUNDS) as i:
                        steps.at = [dve.snap(r, min_val=0, max_val=N) for r in regs]
                        steps(i, False)
                    add(ROUNDS - 1, RG - 1, [dve.snap(r, min_val=0, max_val=N) for r in regs][-TG:])
                    dve.wait_ge(acc0, TILES)
                    dve.wait_ge(accw0, TILES)

                @block.tensor
                def _(pe):
                    def aggregate(i, k, first):
                        pe.wait_ge(oh0, (i * RG + k + 1) * TG)
                        pe.wait_ge(scaled0, (i * RG + k + 1) * TG * SH)
                        pe.wait_ge(stat0, i * RG + k + 1)
                        if not (first and k < 2):
                            pe.wait_ge(acc0, (i * RG + k - 1) * TG)
                            pe.wait_ge(accw0, (i * RG + k - 1) * TG)
                        for t in range(TG):
                            pe.matmul(bank[k % 2][:, t * P:(t + 1) * P], rows[:, k, t, :], onehot[:, k % 2, t, :], start=True, stop=True)
                            last = pe.matmul(bank[2 + k % 2][0:LCOL, t * P:(t + 1) * P], stat[:, k % 2, t, :], onehot[:, k % 2, t, :],
                                             start=True, stop=True)
                        last.then_inc(agg0, 1)
                    for k in range(RG):
                        aggregate(0, k, True)
                    with pe.Fori(1, ROUNDS) as i:
                        for k in range(RG):
                            aggregate(i, k, False)

        with ExitStack() as st:
            sums_t = sb("sums_t", [P, NB, LCOL], st=st)
            top = sb("top", [P, NB, HEADS], st=st)
            seg = sb("seg", [P, NB, HEADS], st=st)
            den = sb("den", [P, NB, HEADS], st=st)
            ca = sb("ca", [P, NB, HEADS], st=st)
            cb = sb("cb", [P, NB, HEADS], st=st)
            bias_all = sb("bias_all", [P, CH], st=st)
            bn1_all = sb("bn1_all", [P, CH], st=st)
            wn1a = sb("wn1a", [P, CH], st=st)
            part = sb("part", [P, 2, CB, CH], st=st)
            normed1 = sb("normed1", [P, 3, CB, CH], st=st)
            squares1 = sb("squares1", [P, 1, CB, CH], st=st)
            turned1 = sb("turned1", [P, 1, CB * P], st=st)
            proj = sb("proj", [P, 2, CB, CH], st=st)
            stats = sb("stats", [P, 5, NB], st=st)
            (b_in, sw_t, sw_c, b_chain, e_in, e_done, s_t, comb, centred1, squared1, varsum1, std1, norm1, hrelu1, turned1_s, relu1_s,
             proj1, rows1, table1_out, base1) = (
                sem(n) for n in ("b_in", "sw_t", "sw_c", "b_chain", "e_in", "e_done", "s_t", "comb", "centred1", "squared1", "varsum1",
                                 "std1", "norm1", "hrelu1", "turned1_s", "relu1_s", "proj1", "rows1", "table1_out", "base1"))
            with nc.Block() as block:
                @block.sync
                def _(sp):
                    sp.dma_start(bias_all[:, :], a["bias"].partition_broadcast(P)).then_inc(b_in, 16)
                    sp.dma_start(bn1_all[:, :], a["bn1"].partition_broadcast(P)).then_inc(b_in, 16)
                    sp.dma_start(wn1a[:, :], a["Wn1"][0:CH, :]).then_inc(b_in, 16)
                    for c in range(CHUNKS):
                        sp.wait_ge(rows1, 2 * (c + 1))
                        sp.dma_start(table2[c * CB * P:(c + 1) * CB * P, :].rearrange("(b p) c -> p b c", p=P), proj[:, c % 2]).then_inc(table1_out, 16)
                        sp.wait_ge(table1_out, 16 * (c + 1))

                @block.tensor
                def _(pe):
                    for b in range(NB):
                        last = pe.transpose(bank[7][:, b * LCOL:(b + 1) * LCOL], acc_w[:, b * P:(b + 1) * P], ident[0:LCOL, 0:LCOL])
                    last.then_inc(sw_t, 1)

                    def turn_sums(c):
                        if c >= 1:
                            pe.wait_ge(comb, c)
                        for b in range(CB):
                            last = pe.transpose(bank[b // 4][:, b % 4 * P:(b % 4 + 1) * P], acc[:, (c * CB + b) * P:(c * CB + b + 1) * P], ident[:, :])
                        last.then_inc(s_t, 1)

                    def turn(c):
                        pe.wait_ge(hrelu1, c + 1)
                        if c >= 1:
                            pe.wait_ge(relu1_s, 2 * c)
                        for b in range(CB):
                            last = pe.transpose(bank[2 + b // 4][:, b % 4 * P:(b % 4 + 1) * P], normed1[:, c % 3, b, :], ident[:, :])
                        last.then_inc(turned1_s, 1)

                    def project(c):
                        pe.wait_ge(relu1_s, 2 * (c + 1))
                        pe.wait_ge(b_in, 16 * 3)
                        if c >= 1:
                            pe.wait_ge(rows1, 2 * c)
                        for b in range(CB):
                            last = pe.matmul(bank[4 + b // 4][:, b % 4 * P:(b % 4 + 1) * P], turned1[:, 0, b * P:(b + 1) * P], wn1a[:, :],
                                             start=True, stop=True)
                        last.then_inc(proj1, 1)
                    turn_sums(0)
                    for c in range(CHUNKS):
                        if c + 1 < CHUNKS:
                            turn_sums(c + 1)
                        turn(c)
                        project(c)

                @block.vector
                def _(dve):
                    n = [0]

                    def link(ins):
                        n[0] += 1
                        ins.then_inc(b_chain, 1)
                        dve.wait_ge(b_chain, n[0])
                    dve.wait_ge(sw_t, 1)
                    link(dve.tensor_copy(sums_t[:, :, :].rearrange("p b c -> p (b c)"), bank[7][:, 0:NB * LCOL]))
                    link(dve.tensor_copy(seg[:, :, 0:SH], sums_t[:, :, SH + 1:]))
                    link(dve.tensor_copy(seg[:, :, SH:], logit[:, :, SH:]))
                    link(dve.tensor_tensor(top[:, :, :], seg[:, :, :], logit[:, :, :], ALU.max))
                    link(dve.tensor_tensor(seg[:, :, :], seg[:, :, :], top[:, :, :], ALU.subtract))
                    link(dve.tensor_tensor(cb[:, :, :], logit[:, :, :], top[:, :, :], ALU.subtract))
                    dve.engine_nop().then_inc(e_in, 1)
                    dve.wait_ge(e_done, 2)
                    link(dve.tensor_tensor(den[:, :, 0:SH], sums_t[:, :, 0:SH], ca[:, :, 0:SH], ALU.mult))
                    link(dve.tensor_tensor(den[:, :, SH:], sums_t[:, :, SH:SH + 1].broadcast_to([P, NB, SH]), ca[:, :, SH:], ALU.mult))
                    link(dve.tensor_tensor(den[:, :, :], den[:, :, :], cb[:, :, :], ALU.add))
                    link(dve.reciprocal(den[:, :, :], den[:, :, :]))
                    link(dve.tensor_tensor(ca[:, :, :], ca[:, :, :], den[:, :, :], ALU.mult))
                    link(dve.tensor_tensor(cb[:, :, :], cb[:, :, :], den[:, :, :], ALU.mult))
                    dve.wait_ge(b_in, 16 * 3)

                    def heads(v):
                        return v.rearrange("p b (h c) -> p b h c", h=HEADS)

                    def per_head(v, b0, m):
                        return v[:, b0:b0 + m, :].unsqueeze(3).broadcast_to([P, m, HEADS, HC])

                    def combine(c):
                        blk = slice(c * CB, (c + 1) * CB)
                        dve.wait_ge(s_t, c + 1)
                        for j, (b0, m) in enumerate(((0, 4), (4, 3))):
                            ins = dve.tensor_tensor(heads(part[:, 0, b0:b0 + m]), heads(bank[j][:, 0:m * P].rearrange("p (m c) -> p m c", m=m)),
                                                    per_head(ca, c * CB + b0, m), ALU.mult)
                            link(ins)
                        dve.engine_nop().then_inc(comb, 1)
                        link(dve.tensor_tensor(heads(part[:, 1]), heads(feat[:, blk, :]), per_head(cb, c * CB, CB), ALU.mult))
                        link(dve.tensor_tensor(part[:, 0], part[:, 0], part[:, 1], ALU.add))
                        link(dve.tensor_tensor(part[:, 0], part[:, 0], bias_all[:, :].unsqueeze(1).broadcast_to([P, CB, CH]), ALU.add))
                        link(dve.tensor_tensor(x_rows[:, blk, :], x_rows[:, blk, :], part[:, 0], ALU.add))

                    def centre(c):
                        blk = slice(c * CB, (c + 1) * CB)
                        link(dve.tensor_reduce(stats[:, 0, blk], x_rows[:, blk, :], AX.X, ALU.add))
                        link(dve.tensor_scalar(stats[:, 1, blk], stats[:, 0, blk], -1.0 / CH, None, ALU.mult))
                        dve.tensor_tensor(normed1[:, c % 3], x_rows[:, blk, :],
                                          stats[:, 1, blk].unsqueeze(2).broadcast_to([P, CB, CH]), ALU.add).then_inc(centred1, 1)

                    def scale(c):
                        blk = slice(c * CB, (c + 1) * CB)
                        dve.wait_ge(squared1, c + 1)
                        dve.tensor_reduce(stats[:, 2, blk], squares1[:, 0], AX.X, ALU.add).then_inc(varsum1, 1)
                        dve.wait_ge(std1, c + 1)
                        link(dve.reciprocal(stats[:, 4, blk], stats[:, 3, blk]))
                        dve.tensor_tensor(normed1[:, c % 3], normed1[:, c % 3],
                                          stats[:, 4, blk].unsqueeze(2).broadcast_to([P, CB, CH]), ALU.mult).then_inc(norm1, 1)

                    def residual(c):
                        blk = slice(c * CB, (c + 1) * CB)
                        dve.wait_ge(hrelu1, c + 1)
                        dve.tensor_tensor(x_rows[:, blk, :], x_rows[:, blk, :], normed1[:, c % 3], ALU.add).then_inc(base1, 1)

                    def evacuate(c):
                        dve.wait_ge(proj1, c + 1)
                        if c >= 2:
                            dve.wait_ge(table1_out, 16 * (c - 1))
                        for j, (b0, m) in enumerate(((0, 4), (4, 3))):
                            dve.tensor_tensor(proj[:, c % 2, b0:b0 + m], bank[4 + j][:, 0:m * P].rearrange("p (m c) -> p m c", m=m),
                                              bn1_all[:, :].unsqueeze(1).broadcast_to([P, m, CH]), ALU.add).then_inc(rows1, 1)
                    for c in range(CHUNKS + 1):
                        if c < CHUNKS:
                            combine(c)
                            centre(c)
                            scale(c)
                        if c >= 1:
                            residual(c - 1)
                            evacuate(c - 1)
                    dve.wait_ge(base1, CHUNKS)

                @block.scalar
                def _(act):
                    act.wait_ge(e_in, 1)
                    act.activation(ca[:, :, :], seg[:, :, :], ACT.Exp).then_inc(e_done, 1)
                    act.activation(cb[:, :, :], cb[:, :, :], ACT.Exp).then_inc(e_done, 1)
                    for c in range(CHUNKS):
                        blk = slice(c * CB, (c + 1) * CB)
                        act.wait_ge(centred1, c + 1)
                        act.activation(squares1[:, 0], normed1[:, c % 3], ACT.Square).then_inc(squared1, 1)
                        act.wait_ge(varsum1, c + 1)
                        act.activation(stats[:, 3, blk], stats[:, 2, blk], ACT.Sqrt, bias=eps_col[:, 0:1], scale=1.0 / CH).then_inc(std1, 1)
                        act.wait_ge(norm1, c + 1)
                        act.activation(normed1[:, c % 3], normed1[:, c % 3], ACT.Relu).then_inc(hrelu1, 1)
                        act.wait_ge(turned1_s, c + 1)
                        if c >= 1:
                            act.wait_ge(proj1, c)
                        act.copy(turned1[:, 0, 0:4 * P], bank[2][:, :]).then_inc(relu1_s, 1)
                        act.copy(turned1[:, 0, 4 * P:], bank[3][:, 0:3 * P]).then_inc(relu1_s, 1)

        with ExitStack() as st:
            we1 = sb("we1", [EC, CH], st=st)
            we2 = sb("we2", [P, CH], st=st)
            wn1b = sb("wn1b", [P, CH], st=st)
            be1 = sb("be1", [P, 1], st=st)
            be2 = sb("be2", [P, 1], st=st)
            wt = sb("wt", [P, 1], st=st)
            bt = sb("bt", [P, 1], st=st)
            ea = sb("ea", [EC, 2, HALF * GE], st=st)
            ts = sb("ts", [P, 2, HALF * GE], st=st)
            hidden = sb("hidden", [P, 2, GE], st=st)
            gate = sb("gate", [P, 2, GE], st=st)
            ef = sb("ef", [P, 2, GE], st=st)
            pre = sb("pre", [P, 2, TG, P], st=st)
            msg = sb("msg", [P, 2, TG, P], st=st)
            w1_in, zero1, oh1, h1, r1, h2, gt, efd, z1, radd, r2, agg1, acc1 = (
                sem(n) for n in ("w1_in", "zero1", "oh1", "h1", "r1", "h2", "gt", "efd", "z1", "radd", "r2", "agg1", "acc1"))
            ea_in = [sem(f"ea_in{h}") for h in range(2)]
            ts_in = [sem(f"ts_in{h}") for h in range(2)]
            with nc.Block() as block:
                @block.sync
                def _(sp):
                    sp.dma_start(we1[:, :], a["We1"]).then_inc(w1_in, 16)
                    sp.dma_start(we2[:, :], a["We2"]).then_inc(w1_in, 16)
                    sp.dma_start(wn1b[:, :], a["Wn1"][CH:, :]).then_inc(w1_in, 16)
                    for col, name in ((be1, "be1"), (be2, "be2"), (bt, "bt")):
                        sp.dma_start(col[:, :], a[name].rearrange("(c o) -> c o", o=1)).then_inc(w1_in, 16)
                    sp.dma_start(wt[:, :], a["Wt"].rearrange("o c -> c o")).then_inc(w1_in, 16)

                    def load(i, first):
                        for h in range(2):
                            load_indices(sp, 1, i, h, first)
                            e0 = (i * RG + h * HALF) * GE
                            if not first:
                                sp.wait_ge(h1, RG * (i - 1) + HALF * (h + 1))
                                sp.wait_ge(gt, RG * (i - 1) + HALF * (h + 1))
                            sp.dma_start(ea[:, h, :], a["ea_t"][:, ds(e0, HALF * GE)]).then_inc(ea_in[h], 16)
                            sp.dma_start(ts[:, h, :], a["ts"][ds(e0, HALF * GE)].partition_broadcast(P)).then_inc(ts_in[h], 16)
                    load(0, True)
                    with sp.Fori(1, ROUNDS) as i:
                        load(i, False)

                @block.gpsimd
                def _(gp):
                    for k in range(RG):
                        gather(gp, 1, table2, 0, k, True, radd)
                    with gp.Fori(1, ROUNDS) as i:
                        for k in range(RG):
                            gather(gp, 1, table2, i, k, False, radd)

                def skewed(eng, parts):
                    def steps(i, first):
                        for k in range(RG):
                            for lag, part_of in parts:
                                if k >= lag:
                                    part_of(i, k - lag, first)
                                elif not first:
                                    part_of(i - 1, k - lag + RG, False)
                    steps(0, True)
                    with eng.Fori(1, ROUNDS) as i:
                        steps(i, False)
                    for k in range(3):
                        for lag, part_of in parts:
                            if k < lag:
                                part_of(ROUNDS - 1, k - lag + RG, False)

                @block.tensor
                def _(pe):
                    pe.wait_ge(w1_in, 16 * 7)

                    def first_product(i, k, first):
                        if k % HALF == 0:
                            pe.wait_ge(ea_in[k // HALF], 16 * (i + 1))
                        if not (first and k < 2):
                            pe.wait_ge(r1, i * RG + k - 1)
                        pe.matmul(bank[k % 2][:, :], we1[:, :], ea[:, k // HALF, k % HALF * GE:(k % HALF + 1) * GE], start=True, stop=True).then_inc(h1, 1)

                    def second_product(i, k, first):
                        pe.wait_ge(r1, i * RG + k + 1)
                        if not (first and k < 2):
                            pe.wait_ge(efd, i * RG + k - 1)
                        pe.matmul(bank[2 + k % 2][:, :], we2[:, :], hidden[:, k % 2], start=True, stop=True).then_inc(h2, 1)

                    def third_product(i, k, first):
                        pe.wait_ge(efd, i * RG + k + 1)
                        if not (first and k < 2):
                            pe.wait_ge(radd, i * RG + k - 1)
                        for t in range(TG):
                            last = pe.matmul(bank[4 + k % 2][:, t * P:(t + 1) * P], ef[:, k % 2, t * P:(t + 1) * P], wn1b[:, :], start=True, stop=True)
                        last.then_inc(z1, 1)

                    def aggregate(i, k, first):
                        pe.wait_ge(r2, i * RG + k + 1)
                        pe.wait_ge(oh1, (i * RG + k + 1) * TG)
                        if not (first and k < 2):
                            pe.wait_ge(acc1, (i * RG + k - 1) * TG)
                        for t in range(TG):
                            last = pe.matmul(bank[6 + k % 2][:, t * P:(t + 1) * P], msg[:, k % 2, t, :], onehot[:, k % 2, t, :], start=True, stop=True)
                        last.then_inc(agg1, 1)
                    skewed(pe, ((0, first_product), (1, second_product), (2, third_product), (3, aggregate)))

                @block.scalar
                def _(act):
                    act.wait_ge(w1_in, 16 * 7)

                    def relu_hidden(i, k, first):
                        act.wait_ge(h1, i * RG + k + 1)
                        if not (first and k < 2):
                            act.wait_ge(h2, i * RG + k - 1)
                        act.activation(hidden[:, k % 2], bank[k % 2][:, :], ACT.Relu, bias=be1[:, 0:1]).then_inc(r1, 1)

                    def time_gate(i, k, first):
                        if k % HALF == 0:
                            act.wait_ge(ts_in[k // HALF], 16 * (i + 1))
                        if not (first and k < 2):
                            act.wait_ge(efd, i * RG + k - 1)
                        act.activation(gate[:, k % 2], ts[:, k // HALF, k % HALF * GE:(k % HALF + 1) * GE], ACT.Sigmoid,
                                       bias=bt[:, 0:1], scale=wt[:, 0:1]).then_inc(gt, 1)

                    def relu_message(i, k, first):
                        act.wait_ge(radd, i * RG + k + 1)
                        if not (first and k < 2):
                            act.wait_ge(agg1, i * RG + k - 1)
                        act.activation(msg[:, k % 2], pre[:, k % 2], ACT.Relu).then_inc(r2, 1)
                    skewed(act, ((0, relu_hidden), (0, time_gate), (2, relu_message)))

                @block.vector
                def _(dve):
                    regs = [dve.alloc_register(f"first1_{n}") for n in range(HALF * TG)]
                    dve.memset(acc[:, :], 0.0).then_inc(zero1, 1)
                    dve.wait_ge(zero1, 1)
                    dve.wait_ge(w1_in, 16 * 7)

                    def masks(i, k, first):
                        if not (first and k < 2):
                            dve.wait_ge(agg1, i * RG + k - 1)
                        for t in range(TG):
                            dve.tensor_scalar(onehot[:, k % 2, t, :], iota_row[:, :], dst_rel[:, ds(i * RT + k * TG + t, 1)], None,
                                              ALU.is_equal).then_inc(oh1, 1)

                    def gated(i, k, first):
                        dve.wait_ge(h2, i * RG + k + 1)
                        dve.wait_ge(gt, i * RG + k + 1)
                        if not (first and k < 2):
                            dve.wait_ge(z1, i * RG + k - 1)
                        dve.scalar_tensor_tensor(ef[:, k % 2], bank[2 + k % 2][:, :], be2[:, 0:1], gate[:, k % 2], ALU.add, ALU.mult).then_inc(efd, 1)

                    def add_sender(i, k, first):
                        dve.wait_ge(z1, i * RG + k + 1)
                        dve.wait_ge(gathered[1][k], 16 * TG * (i + 1))
                        if not (first and k < 2):
                            dve.wait_ge(r2, i * RG + k - 1)
                        dve.tensor_tensor(pre[:, k % 2], bank[4 + k % 2][:, :].rearrange("p (t c) -> p t c", t=TG), rows[:, k], ALU.add).then_inc(radd, 1)

                    at = [None]

                    def add(i, k, first):
                        if k % HALF == 0:
                            at[0] = first_nodes(dve, regs, i, k // HALF)
                        dve.wait_ge(agg1, i * RG + k + 1)
                        for t in range(TG):
                            v = at[0][k % HALF * TG + t]
                            if not (first and k == 0 and t == 0):
                                dve.wait_ge(acc1, (i * RG + k) * TG + t)
                            dve.tensor_tensor(acc[:, ds(v, P)], acc[:, ds(v, P)], bank[6 + k % 2][:, t * P:(t + 1) * P], ALU.add).then_inc(acc1, 1)

                    def steps(i, first):
                        for k in range(RG):
                            for lag, part_of in ((2, masks), (1, gated), (2, add_sender), (3, add)):
                                if k >= lag:
                                    part_of(i, k - lag, first)
                                elif not first:
                                    part_of(i - 1, k - lag + RG, False)
                    steps(0, True)
                    with dve.Fori(1, ROUNDS) as i:
                        at[0] = [dve.snap(r, min_val=0, max_val=N) for r in regs]
                        steps(i, False)
                    at[0] = [dve.snap(r, min_val=0, max_val=N) for r in regs]
                    for k in range(3):
                        for lag, part_of in ((2, masks), (1, gated), (2, add_sender), (3, add)):
                            if k < lag:
                                part_of(ROUNDS - 1, k - lag + RG, False)
                    dve.wait_ge(acc1, TILES)

        with ExitStack() as st:
            outs = sb("outs", [P, 2, CB, CH], st=st)
            f_done, o_done, o_out = (sem(n) for n in ("f_done", "o_done", "o_out"))
            with nc.Block() as block:
                @block.tensor
                def _(pe):
                    for c in range(CHUNKS):
                        if c >= 2:
                            pe.wait_ge(o_done, 2 * (c - 1))
                        for b in range(CB):
                            o = slice((c * CB + b) * P, (c * CB + b + 1) * P)
                            ps = bank[c % 2 * 2 + b // 4][:, b % 4 * P:(b % 4 + 1) * P]
                            pe.matmul(ps, acc[:, o], wn2[:, :], start=True, stop=False)
                            last = pe.matmul(ps, acc_w[:, o], wl_node[:, :], start=False, stop=True)
                        last.then_inc(f_done, 1)

                @block.vector
                def _(dve):
                    for c in range(CHUNKS):
                        dve.wait_ge(f_done, c + 1)
                        if c >= 2:
                            dve.wait_ge(o_out, 16 * (c - 1))
                        for j, (b0, m) in enumerate(((0, 4), (4, 3))):
                            dve.tensor_tensor(outs[:, c % 2, b0:b0 + m], bank[c % 2 * 2 + j][:, 0:m * P].rearrange("p (m c) -> p m c", m=m),
                                              x_rows[:, c * CB + b0:c * CB + b0 + m, :], ALU.add).then_inc(o_done, 1)

                @block.sync
                def _(sp):
                    for c in range(CHUNKS):
                        sp.wait_ge(o_done, 2 * (c + 1))
                        n0 = c * CB * P
                        full = min(CB, (N - n0) // P)
                        sp.dma_start(out[n0:n0 + full * P, :].rearrange("(b p) c -> p b c", p=P), outs[:, c % 2, 0:full, :]).then_inc(o_out, 16)
                        if full < CB:
                            sp.wait_ge(o_out, 16 * (c + 1))
                            rest = N - n0 - full * P
                            sp.dma_start(out[n0 + full * P:N, :], outs[0:rest, c % 2, full, :]).then_inc(o_out, 16)
                        else:
                            sp.wait_ge(o_out, 16 * (c + 1))
                    sp.wait_ge(o_out, 16 * (CHUNKS + 1))


def kernel(**inputs):
    import numpy as np
    import concourse.bacc as bacc
    from concourse.bass_utils import run_bass_kernel_spmd

    def arr(name):
        return np.ascontiguousarray(np.asarray(inputs[name]))

    def padded(v, shape, fill=0):
        full = np.full(shape, fill, v.dtype)
        full[tuple(slice(0, s) for s in v.shape)] = v
        return full

    src = padded(arr("src"), (EPAD,))
    dst = padded(arr("dst"), (EPAD,), N)
    line = np.full((EPAD + 2,), -1, dst.dtype)
    line[1:EPAD + 1] = dst
    feed = {
        "x": padded(arr("x"), (NPAD, CH)),
        "src_lin": src.reshape(P, EPAD // P),
        "src_tile": np.ascontiguousarray(src.reshape(TILES, P).T),
        "dst_tile": np.ascontiguousarray(dst.reshape(TILES, P).T),
        "dst_first": np.ascontiguousarray(dst.reshape(TILES, P)[:, 0]).reshape(1, TILES),
        "dst_line": line,
        "ea_t": np.ascontiguousarray(padded(arr("edge_attr_64"), (EPAD, EC)).T),
        "ts": padded(arr("edge_weight"), (EPAD,)),
        "W": arr("L0_gnn_W"), "b_lin": arr("L0_gnn_b_lin"), "alpha": arr("L0_gnn_alpha"), "bias": arr("L0_gnn_bias"),
        "We1": arr("L1_gnn_We1"), "be1": arr("L1_gnn_be1"), "We2": arr("L1_gnn_We2"), "be2": arr("L1_gnn_be2"),
        "Wt": arr("L1_gnn_Wt"), "bt": arr("L1_gnn_bt"), "Wn1": arr("L1_gnn_Wn1"), "bn1": arr("L1_gnn_bn1"),
        "Wn2": arr("L1_gnn_Wn2"), "bn2": arr("L1_gnn_bn2"),
    }
    nc = bacc.Bacc("TRN2", target_bir_lowering=False, num_devices=1)
    arrays, aps = {}, {}
    for name, v in feed.items():
        arrays[f"in_{name}"] = v
        aps[name] = nc.dram_tensor(f"in_{name}", v.shape, mybir.dt.from_np(v.dtype), kind="ExternalInput").ap()
    fp32, bf16 = mybir.dt.float32, mybir.dt.bfloat16
    out = nc.dram_tensor("out_0", (N, CH), fp32, kind="ExternalOutput").ap()
    table1 = nc.dram_tensor("table1", (NPAD, CH), fp32, kind="Internal").ap()
    table2 = nc.dram_tensor("table2", (NPAD, CH), fp32, kind="Internal").ap()
    lo_dram = nc.dram_tensor("lo_dram", (EPAD,), bf16, kind="Internal").ap()
    lin_dram = nc.dram_tensor("lin_dram", (SH, EPAD), fp32, kind="Internal").ap()
    w_dram = nc.dram_tensor("w_dram", (2 * SH, EPAD), fp32, kind="Internal").ap()
    carry_dram = nc.dram_tensor("carry_dram", (2, P, SH + 1), fp32, kind="Internal").ap()
    carried_dram = nc.dram_tensor("carried_dram", (2, SH, P), fp32, kind="Internal").ap()
    gnn_layers(nc, aps, out, table1, table2, lo_dram, lin_dram, w_dram, carry_dram, carried_dram)
    return run_bass_kernel_spmd(nc, [arrays], core_ids=[0]).results[0]["out_0"]
```

```python
from contextlib import ExitStack

import concourse.bass as bass
from concourse import mybir
from concourse.alu_op_type import AluOpType as ALU

P = 128
N = 6250
E = 106250
CH = 128
EC = 64
HEADS = 4
HC = CH // HEADS
SH = 2
NB = (N + P - 1) // P
NPAD = NB * P
CB = 7
CHUNKS = NB // CB
TG = 4
GE = TG * P
RG = 8
HALF = RG // 2
GROUPS = -(-E // (GE * RG)) * RG
TILES = GROUPS * TG
ROUNDS = GROUPS // RG
EPAD = TILES * P
RT = RG * TG
ACCW = (N + P + P - 1) // P * P
BIG = 1.0e38
EPS = 1e-5
SECTIONS = (4, 8, 14)
PAIRS = RG // 2
PREP_PARTS, PREP_ALL = 4, 16
OLD_IN, NEW_IN = 16 * 4, 16 * 3
LCOL = 5


def bl_count(n):
    tiles = SECTIONS[n] * RT
    return 16 * (4 * (tiles // P > 0) + (tiles % P > 0))


def gnn_layers(nc, a, out, table1, table2, parts_dram, lin_dram, w_dram, carry_dram, carried_dram, bound_dram):
    fp32, bf16, i32 = mybir.dt.float32, mybir.dt.bfloat16, mybir.dt.int32
    ACT = mybir.ActivationFunctionType
    AX = mybir.AxisListType
    ds = bass.ds

    ctx = ExitStack()
    with ctx:
        ctx.enter_context(nc.allow_non_contiguous_dma(reason="columns of 128 numbers"))

        def sb(name, shape, dt=fp32, st=ctx):
            return st.enter_context(nc.sbuf_tensor(name, shape, dt))

        def sem(name):
            return ctx.enter_context(nc.semaphore(name))

        bank = [ctx.enter_context(nc.psum_tensor(f"bank{n}", [P, 512], fp32)) for n in range(8)]

        x_rows = sb("x_rows", [P, NB, CH])
        feat = sb("feat", [P, NB, CH])
        logit = sb("logit", [P, NB, HEADS])
        acc = sb("acc", [P, ACCW])
        acc_w = sb("acc_w", [LCOL, ACCW])
        ident = sb("ident", [P, P])
        iota_row = sb("iota_row", [P, P])
        iota_col = sb("iota_col", [P, 1])
        iota_int = sb("iota_int", [P, P], i32)
        iota_cint = sb("iota_cint", [P, 1], i32)
        eps_col = sb("eps_col", [P, 1])
        dst_rel = sb("dst_rel", [P, TILES])
        dst_first = sb("dst_first", [1, TILES], i32)
        rows = sb("rows", [P, RG, TG, CH])
        index = sb("index", [P, RG, TG], i32)
        onehot = sb("onehot", [P, 2, TG, P])
        wl_node = sb("wl_node", [LCOL, CH])
        wn2 = sb("wn2", [P, CH])

        with ExitStack() as st:
            normed = sb("normed", [P, 3, CB, CH], st=st)
            squares = sb("squares", [P, 2, CB, CH], st=st)
            feats_t = sb("feats_t", [P, 2, CB * P], st=st)
            nmean = sb("nmean", [P, NB], st=st)
            sums = sb("sums", [P, NB], st=st)
            sqsum = sb("sqsum", [P, NB], st=st)
            std = sb("std", [P, NB], st=st)
            rstd = sb("rstd", [P, NB], st=st)
            w0 = sb("w0", [P, CH], st=st)
            w0_t = sb("w0_t", [P, CH], st=st)
            w0_ext = sb("w0_ext", [P, CH + HEADS], st=st)
            alpha_bd = sb("alpha_bd", [P, HEADS], st=st)
            blin_col = sb("blin_col", [P, 1], st=st)
            blin_rep = sb("blin_rep", [P, P], st=st)
            bias_ext = sb("bias_ext", [P, CH + HEADS], st=st)
            zlogit = sb("zlogit", [P, NB, HEADS], st=st)

            x_in, w_in, const_set, iota_done, sel_done = (sem(n) for n in ("x_in", "w_in", "const_set", "iota_done", "sel_done"))
            chain = sem("a_chain")
            w_t, w_tc, wa_done, wa_copied, ba_ready = (sem(n) for n in ("w_t", "w_tc", "wa_done", "wa_copied", "ba_ready"))
            centred, squared, varsum, std_done, norm_done, turned, relu_done, projected, rows_done, table_out = (
                sem(n) for n in ("centred", "squared", "varsum", "std_done", "norm_done", "turned", "relu_done",
                                 "projected", "rows_done", "table_out"))
            zero_done = sem("zero_done")
            small_sync = sem("small_sync")
            with nc.Block() as block:
                @block.sync
                def _(sp):
                    sp.dma_start(x_rows[:, :, :], a["x"].rearrange("(b p) c -> p b c", p=P)).then_inc(x_in, 16)
                    sp.dma_start(wn2[:, :], a["Wn2"]).then_inc(w_in, 16)
                    for c in range(CHUNKS):
                        sp.wait_ge(rows_done, 3 * (c + 1))
                        sp.dma_start(table1[c * CB * P:(c + 1) * CB * P, :].rearrange("(b p) c -> p b c", p=P),
                                     feat[:, c * CB:(c + 1) * CB, :]).then_inc(table_out, 16)
                    sp.wait_ge(table_out, 16 * CHUNKS)

                @block.gpsimd
                def _(gp):
                    gp.iota(iota_int[:, :], pattern=[[1, P]], base=0, channel_multiplier=0).then_inc(iota_done, 1)
                    gp.iota(iota_cint[:, :], pattern=[[1, 1]], base=0, channel_multiplier=1).then_inc(iota_done, 1)
                    gp.memset(ident[:, :], 0.0).then_inc(sel_done, 1)
                    gp.wait_ge(sel_done, 1)
                    gp.affine_select(out=ident[:, :], in_=ident[:, :], compare_op=ALU.not_equal, fill=1.0, base=0,
                                     pattern=[[-1, P]], channel_multiplier=1).then_inc(sel_done, 1)
                    gp.memset(eps_col[:, :], EPS).then_inc(sel_done, 1)
                    gp.memset(alpha_bd[:, :], 0.0).then_inc(const_set, 1)
                    gp.memset(wl_node[:, :], 0.0).then_inc(const_set, 1)
                    gp.memset(acc[:, :], 0.0).then_inc(zero_done, 1)
                    gp.memset(acc_w[:, :], 0.0).then_inc(zero_done, 1)
                    gp.wait_ge(zero_done, 2)

                @block.scalar
                def _(act):
                    act.dma_start(w0[:, :], a["W"]).then_inc(w_in, 16)
                    act.dma_start(blin_col[:, :], a["b_lin"].rearrange("(c o) -> c o", o=1)).then_inc(w_in, 16)
                    act.dma_start(bias_ext[:, 0:CH], a["b_lin"].partition_broadcast(P)).then_inc(w_in, 16)
                    act.wait_ge(const_set, 2)
                    for h in range(HEADS):
                        half = (h % 2) * 64
                        act.dma_start(alpha_bd[half:half + 64, h:h + 1],
                                      a["alpha"][0, h, :].rearrange("(c o) -> c o", o=1)).then_inc(w_in, 16)
                    act.dma_start(wl_node[2:3, :], a["bn2"].rearrange("(o c) -> o c", o=1)).then_inc(w_in, 16)
                    act.wait_ge(w_in, 16 * 9)
                    act.wait_ge(sel_done, 3)
                    act.activation(blin_rep[:, :], ident[:, :], ACT.Identity, bias=blin_col[:, 0:1], scale=0.0).then_inc(w_tc, 1)
                    act.wait_ge(w_t, 1)
                    act.copy(w0_t[:, :], bank[0][:, 0:P]).then_inc(w_tc, 1)
                    act.wait_ge(wa_done, 1)
                    act.copy(w0_ext[:, 0:CH], w0[:, :]).then_inc(wa_copied, 1)
                    act.copy(w0_ext[:, CH:CH + HEADS], bank[1][:, 0:HEADS]).then_inc(wa_copied, 1)
                    act.copy(bias_ext[:, CH:CH + HEADS], bank[1][:, 8:8 + HEADS]).then_inc(ba_ready, 1)

                    def square(c):
                        act.wait_ge(centred, c + 1)
                        if c >= 2:
                            act.wait_ge(varsum, c - 1)
                        act.activation(squares[:, c % 2], normed[:, c % 3], ACT.Square).then_inc(squared, 1)

                    def root(c):
                        act.wait_ge(varsum, c + 1)
                        act.activation(std[:, c * CB:(c + 1) * CB], sqsum[:, c * CB:(c + 1) * CB], ACT.Sqrt,
                                       bias=eps_col[:, 0:1], scale=1.0 / CH).then_inc(std_done, 1)

                    def turn_relu(c):
                        act.wait_ge(turned, c + 1)
                        if c >= 2:
                            act.wait_ge(projected, c - 1)
                        act.activation(feats_t[:, c % 2, 0:4 * P], bank[2][:, :], ACT.Relu).then_inc(relu_done, 1)
                        act.activation(feats_t[:, c % 2, 4 * P:], bank[3][:, 0:3 * P], ACT.Relu).then_inc(relu_done, 1)
                    for s in range(CHUNKS + 2):
                        if s < CHUNKS:
                            square(s)
                            root(s)
                        if s >= 1 and s - 1 < CHUNKS:
                            turn_relu(s - 1)

                @block.vector
                def _(dve):
                    n = [0]

                    def link(ins):
                        n[0] += 1
                        ins.then_inc(chain, 1)
                        dve.wait_ge(chain, n[0])

                    dve.wait_ge(iota_done, 2)
                    link(dve.tensor_copy(iota_row[:, :], iota_int[:, :]))
                    link(dve.tensor_copy(iota_col[:, :], iota_cint[:, :]))
                    dve.wait_ge(x_in, 16)

                    def centre(c):
                        blk = slice(c * CB, (c + 1) * CB)
                        link(dve.tensor_reduce(sums[:, blk], x_rows[:, blk, :], AX.X, ALU.add))
                        link(dve.tensor_scalar(nmean[:, blk], sums[:, blk], -1.0 / CH, None, ALU.mult))
                        if c >= 3:
                            dve.wait_ge(turned, c - 2)
                        dve.tensor_tensor(normed[:, c % 3], x_rows[:, blk, :],
                                          nmean[:, blk].unsqueeze(2).broadcast_to([P, CB, CH]), ALU.add).then_inc(centred, 1)

                    def variance(c):
                        dve.wait_ge(squared, c + 1)
                        dve.tensor_reduce(sqsum[:, c * CB:(c + 1) * CB], squares[:, c % 2], AX.X, ALU.add).then_inc(varsum, 1)

                    def scale(c):
                        blk = slice(c * CB, (c + 1) * CB)
                        dve.wait_ge(std_done, c + 1)
                        link(dve.reciprocal(rstd[:, blk], std[:, blk]))
                        dve.tensor_tensor(normed[:, c % 3], normed[:, c % 3],
                                          rstd[:, blk].unsqueeze(2).broadcast_to([P, CB, CH]), ALU.mult).then_inc(norm_done, 1)

                    def evacuate(c):
                        if c == 0:
                            dve.wait_ge(ba_ready, 1)
                            dve.wait_ge(w_in, 16 * 9)
                        dve.wait_ge(projected, c + 1)
                        for b0, m, bk in ((0, 3, 4), (3, 3, 5), (6, 1, 6)):
                            ps = bank[bk][:, 0:m * (CH + HEADS)].rearrange("p (m n) -> p m n", m=m)
                            at = slice(c * CB + b0, c * CB + b0 + m)
                            dve.tensor_tensor(feat[:, at, :], ps[:, :, 0:CH],
                                              bias_ext[:, 0:CH].unsqueeze(1).broadcast_to([P, m, CH]), ALU.add).then_inc(rows_done, 1)
                            dve.tensor_tensor(zlogit[:, at, :], ps[:, :, CH:],
                                              bias_ext[:, CH:].unsqueeze(1).broadcast_to([P, m, HEADS]), ALU.add).then_inc(small_sync, 1)
                    for s in range(CHUNKS + 2):
                        if s < CHUNKS:
                            centre(s)
                            variance(s)
                            scale(s)
                        if s >= 2:
                            evacuate(s - 2)
                    dve.wait_ge(small_sync, 3 * CHUNKS)
                    dve.scalar_tensor_tensor(logit[:, :, :].rearrange("p b h -> p (b h)"), zlogit[:, :, :].rearrange("p b h -> p (b h)"), 0.2,
                                             zlogit[:, :, :].rearrange("p b h -> p (b h)"), ALU.mult, ALU.max).then_inc(small_sync, 1)
                    dve.wait_ge(small_sync, 3 * CHUNKS + 1)

                @block.tensor
                def _(pe):
                    pe.wait_ge(w_in, 16 * 9)
                    pe.wait_ge(sel_done, 3)
                    pe.transpose(bank[0][:, 0:P], w0[:, :], ident[:, :]).then_inc(w_t, 1)
                    pe.wait_ge(w_tc, 2)
                    pe.matmul(bank[1][:, 0:HEADS], w0_t[:, :], alpha_bd[:, :], start=True, stop=True)
                    pe.matmul(bank[1][:, 8:8 + HEADS], blin_rep[:, :], alpha_bd[:, :], start=True, stop=True).then_inc(wa_done, 1)

                    def turn(c):
                        pe.wait_ge(norm_done, c + 1)
                        if c >= 1:
                            pe.wait_ge(relu_done, 2 * c)
                        for b in range(CB):
                            last = pe.transpose(bank[2 + b // 4][:, b % 4 * P:(b % 4 + 1) * P], normed[:, c % 3, b, :], ident[:, :])
                        last.then_inc(turned, 1)

                    def project(c):
                        if c == 0:
                            pe.wait_ge(wa_copied, 2)
                        pe.wait_ge(relu_done, 2 * (c + 1))
                        if c >= 1:
                            pe.wait_ge(small_sync, 3 * c)
                            pe.wait_ge(rows_done, 3 * c)
                        for b in range(CB):
                            o = b % 3 * (CH + HEADS)
                            last = pe.matmul(bank[4 + b // 3][:, o:o + CH + HEADS], feats_t[:, c % 2, b * P:(b + 1) * P],
                                             w0_ext[:, :], start=True, stop=True)
                        last.then_inc(projected, 1)
                    for s in range(CHUNKS + 1):
                        if s < CHUNKS:
                            turn(s)
                        if s >= 1:
                            project(s - 1)

        idx_ready = [[sem(f"idx_ready{q}_{h}") for h in range(2)] for q in range(2)]
        gathered = [[sem(f"gathered{q}_{k}") for k in range(RG)] for q in range(2)]

        def load_indices(sp, q, i, h, first):
            if not first:
                for k in range(h * HALF, (h + 1) * HALF):
                    sp.wait_ge(gathered[q][k], 16 * TG * i)
            sp.dma_start(index[:, h * HALF:(h + 1) * HALF, :].rearrange("p g t -> p (g t)"),
                         a["src_tile"][:, ds(i * RT + h * HALF * TG, HALF * TG)]).then_inc(idx_ready[q][h], 16)

        slot_taken = sem("slot_taken")

        def gather(gp, q, table, i, k, first, used):
            if k % HALF == 0:
                gp.wait_ge(idx_ready[q][k // HALF], 16 * (i + 1))
            if not first:
                gp.wait_ge(used, RG * (i - 1) + k + 1)
            gp.sem_inc(slot_taken, 1)
            for t in range(TG):
                gp.indirect_dma_start(rows[:, k, t, :], None, table,
                                      bass.IndirectOffsetOnAxis(index[:, k, t:t + 1], 0)).then_inc(gathered[q][k], 16)

        def first_nodes(dve, regs, i, h):
            dve.load(regs, dst_first[0:1, ds(i * RT + h * HALF * TG, HALF * TG)])
            return [dve.snap(r, min_val=0, max_val=N) for r in regs]

        with ExitStack() as st:
            SR = max(SECTIONS)
            ST = SR * RT
            TB = (ST + P - 1) // P
            lg = sb("lg", [P, SH, ST], st=st)
            run2 = sb("run2", [P, SH, ST], st=st)
            src_lin = lg[:, :, :].rearrange("p h n -> p (h n)").bitcast(i32)[:, 0:EPAD // P]
            part_int = run2[:, :, :].rearrange("p h n -> p (h n)").bitcast(i32)[:, 0:EPAD // P]
            part_bf = sb("part_bf", [P, 2, EPAD // P], bf16, st)
            dst_int = src_lin[:, 0:TILES]
            first_all = part_int[:, 0:TILES]
            tab = sb("tab", [P, 3, SH * NB], bf16, st)
            tab_rest = sb("tab_rest", [P, SH * NB], st=st)
            row_block = sb("row_block", [SH * NB, 1], st=st)
            row_head = sb("row_head", [SH * NB, SH], st=st)
            lo_all = sb("lo_all", [P, PAIRS, 2 * GE], bf16, st)
            hi_all = sb("hi_all", [SH * NB, PAIRS, 2 * GE], bf16, st)
            onehot_lo = sb("onehot_lo", [P, 2, GE], bf16, st)
            picked = sb("picked", [SH * NB, 2, GE], st=st)
            edge_logit = sb("edge_logit", [P, ST, SH], st=st)
            edge_w = sb("edge_w", [P, ST, LCOL], st=st)
            stat = sb("stat", [P, 2, TG, LCOL], st=st)
            dn = sb("dn", [P, 3, ST], i32, st)
            ends = sb("ends", [P, ST], st=st)
            pen_f = sb("pen_f", [P, ST], st=st)
            pen_b = sb("pen_b", [P, ST], st=st)
            run = sb("run", [P, SH, ST], st=st)
            cols = sb("cols", [P, 2, SH + 1], st=st)
            rowv = sb("rowv", [1, 2, SH + 1, P], st=st)
            rowc = sb("rowc", [1, 2, SH, P + 1], st=st)
            carry = sb("carry", [P, 2, SH], st=st)
            blocks_w = sb("blocks_w", [P, 2 * SH, TB, P], st=st)
            turned_l = blocks_w[:, 0:SH, :, :]
            old_new = sb("old_new", [P, 2, 1], st=st)
            old_new_w = sb("old_new_w", [SH, 2, 1], st=st)
            old_row = sb("old_row", [1, SH], st=st)
            bound = sb("bound", [P, 2], i32, st)
            same = sb("same", [P, 1], st=st)
            factor = sb("factor", [P, 1], st=st)
            factor_w = sb("factor_w", [SH, 1], st=st)

            idx_in, prep, parts_out, dst_in, rel_done = (sem(n) for n in ("idx_in", "prep", "parts_out", "dst_in", "rel_done"))
            look_in = [sem(f"look_in{q}") for q in range(PAIRS)]
            ohl_done, look1, pick_done, look2, logit_done = (sem(n) for n in ("ohl_done", "look1", "pick_done", "look2", "logit_done"))
            oh0, scaled0, stat0, agg0, acc0, accw0 = (sem(n) for n in ("oh0", "scaled0", "stat0", "agg0", "acc0", "accw0"))
            (t_done, t_copied, lin_out, lg_in, dn_in, sc, col_out, row_in, carry_out, carry_in, col_ready, row_ready, m_ready, w_exp,
             res_ready, res_out, bl_in, bt_done, bt_copied, old_out, old_in, new_in, delta_ready, factor_done, bound_in) = (
                sem(n) for n in ("t_done", "t_copied", "lin_out", "lg_in", "dn_in", "sc", "col_out", "row_in", "carry_out", "carry_in",
                                 "col_ready", "row_ready", "m_ready", "w_exp", "res_ready", "res_out", "bl_in", "bt_done", "bt_copied",
                                 "old_out", "old_in", "new_in", "delta_ready", "factor_done", "bound_in"))

            def before(j, k, pairs=1):
                k -= 2 * pairs
                return (j, k) if k >= 0 else (j - 1, k + RG)

            first_round = [sum(SECTIONS[:n]) for n in range(len(SECTIONS) + 1)]

            def tile_blocks(n):
                tiles = SECTIONS[n] * RT
                return [(t, min(P, tiles - t)) for t in range(0, tiles, P)]

            def looked(n):
                two = SECTIONS[n + 1] // 2 if n + 1 < len(SECTIONS) else 0
                return two, SECTIONS[n] - two

            blocks_before = [sum(len(tile_blocks(m)) for m in range(n)) for n in range(len(SECTIONS) + 1)]

            def section_rounds(eng, n, one_round):
                two, rest = looked(n)
                a0, a1 = first_round[n], first_round[n + 1]

                def look_of(i):
                    return a1 + (i - a0) * 2
                if two:
                    one_round(a0, True, look_of(a0))
                    if two > 1:
                        with eng.Fori(a0 + 1, a0 + two) as i:
                            one_round(i, False, look_of(i))
                if rest:
                    b0 = a0 + two
                    one_round(b0, two == 0, None)
                    if rest > 1:
                        with eng.Fori(b0 + 1, a1) as i:
                            one_round(i, False, None)

            with nc.Block() as block:
                @block.sync
                def _(sp):
                    sp.dma_start(src_lin[:, :], a["src_lin"]).then_inc(idx_in, 16)
                    sp.dma_start(dst_first[:, :], a["dst_first"]).then_inc(idx_in, 16)
                    for h in range(2):
                        load_indices(sp, 0, 0, h, True)
                    sp.wait_ge(prep, PREP_PARTS)
                    sp.dma_start(parts_dram.rearrange("k (p n) -> p k n", p=P), part_bf[:, :, :]).then_inc(parts_out, 16)
                    sp.dma_start(dst_int, a["dst_tile"]).then_inc(dst_in, 16)
                    sp.dma_start(first_all, a["dst_first"].rearrange("o t -> (o t)").partition_broadcast(P)).then_inc(dst_in, 16)
                    sp.wait_ge(parts_out, 16)

                    def load_parts(j, q, first=False):
                        if not first:
                            sp.wait_ge(ohl_done, RG * (j - 1) + 2 * (q + 1))
                            sp.wait_ge(pick_done, RG * (j - 1) + 2 * (q + 1))
                        e0 = (j * RG + 2 * q) * GE
                        sp.dma_start(lo_all[:, q, :], parts_dram[0, ds(e0, 2 * GE)].partition_broadcast(P)).then_inc(look_in[q], 16)
                        sp.dma_start(hi_all[:, q, :], parts_dram[1, ds(e0, 2 * GE)].partition_broadcast(SH * NB)).then_inc(look_in[q], 16)
                    for q in range(PAIRS):
                        load_parts(0, q, True)
                    with sp.Fori(1, SECTIONS[0] + 1) as j:
                        for q in range(PAIRS):
                            load_parts(j, q)

                    def look_round(i, look, more):
                        for q in range(PAIRS - 1):
                            load_parts(look + 1, q)
                        load_indices(sp, 0, i + 1, 0, False)
                        load_parts(look + 1, PAIRS - 1)
                        if more:
                            for q in range(PAIRS - 1):
                                load_parts(look + 2, q)
                        load_indices(sp, 0, i + 1, 1, False)
                        if more:
                            load_parts(look + 2, PAIRS - 1)

                    for n in range(len(SECTIONS)):
                        two, rest = looked(n)
                        a0, a1 = first_round[n], first_round[n + 1]
                        if two:
                            ends_here = first_round[n + 2] == ROUNDS
                            last = a0 + two - 1
                            with sp.Fori(a0, last + (not ends_here)) as i:
                                look_round(i, a1 + (i - a0) * 2, True)
                            if ends_here:
                                look_round(last, a1 + (last - a0) * 2, False)
                        if rest:
                            with sp.Fori(a0 + two, min(a1, ROUNDS - 1)) as i:
                                for h in range(2):
                                    load_indices(sp, 0, i + 1, h, False)

                @block.gpsimd
                def _(gp):
                    for k in range(RG):
                        gather(gp, 0, table1, 0, k, True, agg0)
                    with gp.Fori(1, ROUNDS) as i:
                        for k in range(RG):
                            gather(gp, 0, table1, i, k, False, agg0)

                @block.vector
                def _(dve):
                    n_prep = [0]

                    def link(ins):
                        n_prep[0] += 1
                        ins.then_inc(prep, 1)
                        dve.wait_ge(prep, n_prep[0])
                    dve.wait_ge(idx_in, 16 * 2)
                    link(dve.tensor_scalar(part_int[:, :], src_lin[:, :], P - 1, None, ALU.bitwise_and))
                    link(dve.tensor_copy(part_bf[:, 0, :], part_int[:, :]))
                    link(dve.tensor_scalar(part_int[:, :], src_lin[:, :], 7, None, ALU.logical_shift_right))
                    link(dve.tensor_copy(part_bf[:, 1, :], part_int[:, :]))
                    assert n_prep[0] == PREP_PARTS
                    link(dve.tensor_copy(tab_rest[:, :].rearrange("p (h b) -> p h b", h=SH), logit[:, :, 0:SH].rearrange("p b h -> p h b")))
                    for part in range(3):
                        link(dve.tensor_copy(tab[:, part], tab_rest[:, :]))
                        if part < 2:
                            link(dve.tensor_tensor(tab_rest[:, :], tab_rest[:, :], tab[:, part], ALU.subtract))
                    R2 = SH * NB
                    link(dve.tensor_scalar(row_head[:, 1:2], iota_col[0:R2, :], float(NB), None, ALU.is_ge))
                    link(dve.tensor_scalar(row_head[:, 0:1], row_head[:, 1:2], -1.0, 1.0, ALU.mult, ALU.add))
                    link(dve.tensor_scalar(row_block[:, :], row_head[:, 1:2], -float(NB), None, ALU.mult))
                    link(dve.tensor_tensor(row_block[:, :], row_block[:, :], iota_col[0:R2, :], ALU.add))
                    link(dve.memset(edge_w[:, :, :], 1.0))
                    link(dve.memset(old_new[:, :, :], 0.0))
                    assert n_prep[0] == PREP_ALL
                    dve.wait_ge(dst_in, 16 * 2)
                    dve.tensor_tensor(dst_rel[:, :], dst_int, first_all, ALU.subtract).then_inc(rel_done, 1)

                    def masks_lo(j, k, first):
                        if k % 2 == 0:
                            dve.wait_ge(look_in[k // 2], 32 * (j + 1))
                        if not (first and k < 2):
                            dve.wait_ge(look1, j * RG + k - 1)
                        dve.tensor_scalar(onehot_lo[:, k % 2], lo_all[:, k // 2, k % 2 * GE:(k % 2 + 1) * GE],
                                          iota_col[:, 0:1], None, ALU.is_equal).then_inc(ohl_done, 1)

                    def pick(j, k, first):
                        dve.wait_ge(look1, j * RG + k + 1)
                        if not (first and k < 2):
                            dve.wait_ge(look2, j * RG + k - 1)
                        dve.scalar_tensor_tensor(picked[:, k % 2], hi_all[:, k // 2, k % 2 * GE:(k % 2 + 1) * GE],
                                                 row_block[:, 0:1], bank[4 + k % 2][0:SH * NB, :], ALU.is_equal, ALU.mult).then_inc(pick_done, 1)

                    def pick_pair(j, k, first=False):
                        for q in range(2):
                            pick(j, k + q, first)

                    def lookup(j, k, opening, first=False):
                        for q in range(2):
                            masks_lo(j, k + q, first)
                        if not opening:
                            pick_pair(*before(j, k), first and k == 2)

                    for k in range(0, RG, 2):
                        lookup(0, k, k == 0, True)
                    if SECTIONS[0] > 1:
                        with dve.Fori(1, SECTIONS[0]) as j:
                            for k in range(0, RG, 2):
                                lookup(j, k, False)
                    pick_pair(SECTIONS[0] - 1, RG - 2)

                    n_sc = [0]

                    def hop(ins):
                        n_sc[0] += 1
                        ins.then_inc(sc, 1)
                        dve.wait_ge(sc, n_sc[0])

                    def scan_stage(n):
                        L = SECTIONS[n] * RT
                        pf, pb, en = pen_f[:, 0:L], pen_b[:, 0:L], ends[:, 0:L]
                        dve.wait_ge(dn_in, 16 * 3 * (n + 1))
                        hop(dve.tensor_tensor(pf, dn[:, 0, 0:L], dn[:, 1, 0:L], ALU.not_equal))
                        hop(dve.tensor_tensor(en, dn[:, 2, 0:L], dn[:, 1, 0:L], ALU.not_equal))
                        hop(dve.tensor_scalar(pf, pf, -BIG, None, ALU.mult))
                        hop(dve.tensor_scalar(pb, en, -BIG, None, ALU.mult))
                        hop(dve.tensor_reduce(cols[:, 0, SH:SH + 1], pf, AX.X, ALU.min))
                        hop(dve.tensor_reduce(cols[:, 1, SH:SH + 1], pb, AX.X, ALU.min))
                        hop(dve.memset(rowc[:, :, :, :], -BIG))
                        if n:
                            dve.wait_ge(old_in, OLD_IN * n)
                            hop(dve.tensor_copy(rowc[:, 0, :, 0:1].rearrange("o h q -> o (h q)"), old_row[:, :]))
                        dve.wait_ge(lg_in, 16 * (n + 1))
                        for way, (pen, src, dst) in enumerate(((pf, lg, run), (pb, run, run2))):
                            back = way == 1

                            def line(v):
                                return v[:, ::-1] if back else v
                            for h in range(SH):
                                hop(dve.tensor_tensor_scan(line(run2[:, h, 0:L]), line(pen), line(src[:, h, 0:L]), -BIG, ALU.add, ALU.max))
                            end = 0 if back else L - 1
                            hop(dve.tensor_copy(cols[:, way, 0:SH], run2[:, :, end:end + 1].rearrange("p h o -> p (h o)")))
                            dve.engine_nop().then_inc(col_ready, 1)
                            dve.wait_ge(row_in, 16 * (2 * n + way + 1))
                            for h in range(SH):
                                o = rowc[:, way, h, 0:P] if back else rowc[:, way, h, 1:P + 1]
                                start = rowc[:, 0, h, 0:1] if way == 0 else -BIG
                                hop(dve.tensor_tensor_scan(line(o), line(rowv[:, way, SH, :]), line(rowv[:, way, h, :]), start, ALU.add, ALU.max))
                            dve.engine_nop().then_inc(row_ready, 1)
                            dve.wait_ge(carry_in, 16 * (2 * n + way + 1))
                            for h in range(SH):
                                hop(dve.tensor_tensor_scan(line(dst[:, h, 0:L]), line(pen), line(src[:, h, 0:L]),
                                                           carry[:, way, h:h + 1], ALU.add, ALU.max))
                        hop(dve.tensor_tensor(lg[:, :, 0:L], lg[:, :, 0:L], run2[:, :, 0:L], ALU.subtract))
                        dve.engine_nop().then_inc(m_ready, 1)
                        dve.tensor_tensor(run[:, :, 0:L], run2[:, :, 0:L], en.unsqueeze(1).broadcast_to([P, SH, L]), ALU.mult).then_inc(res_ready, 1)

                    def rescale(n):
                        dve.wait_ge(bound_in, 16 * 2 * n)
                        dve.wait_ge(old_in, OLD_IN * n)
                        dve.wait_ge(new_in, NEW_IN * n)
                        hop(dve.tensor_tensor(same[:, :], bound[:, 0:1], bound[:, 1:2], ALU.is_equal))
                        hop(dve.tensor_tensor(factor[:, :], old_new[:, 0, :], old_new[:, 1, :], ALU.subtract))
                        hop(dve.tensor_tensor(factor_w[:, :], old_new_w[:, 0, :], old_new_w[:, 1, :], ALU.subtract))
                        hop(dve.tensor_tensor(factor[:, :], factor[:, :], same[:, :], ALU.mult))
                        hop(dve.tensor_tensor(factor_w[:, :], factor_w[:, :], same[0:SH, :], ALU.mult))
                        dve.engine_nop().then_inc(delta_ready, 1)
                        dve.wait_ge(factor_done, 2 * n)
                        dve.load([edge_reg], bound[0:1, 0:1])
                        v = dve.snap(edge_reg, min_val=0, max_val=N)
                        hop(dve.tensor_scalar(acc[:, ds(v, 1)], acc[:, ds(v, 1)], factor[:, 0:1], None, ALU.mult))
                        hop(dve.tensor_scalar(acc_w[0:SH, ds(v, 1)], acc_w[0:SH, ds(v, 1)], factor_w[:, 0:1], None, ALU.mult))

                    regs = [dve.alloc_register(f"first0_{q}") for q in range(HALF * TG)]
                    edge_reg = dve.alloc_register("boundary")

                    def masks(i, k):
                        if not (isinstance(i, int) and i * RG + k < 2):
                            dve.wait_ge(agg0, i * RG + k - 1)
                        for t in range(TG):
                            dve.tensor_scalar(onehot[:, k % 2, t, :], iota_row[:, :], dst_rel[:, ds(i * RT + k * TG + t, 1)], None,
                                              ALU.is_equal).then_inc(oh0, 1)

                    def add(i, k, at):
                        dve.wait_ge(agg0, i * RG + k + 1)
                        for t in range(TG):
                            v = at[t]
                            if not (k == 0 and t == 0 and isinstance(i, int) and i == 0):
                                dve.wait_ge(acc0, (i * RG + k) * TG + t)
                            dve.tensor_tensor(acc[:, ds(v, P)], acc[:, ds(v, P)], bank[k % 2][:, t * P:(t + 1) * P], ALU.add).then_inc(acc0, 1)
                            if not (k == 0 and t == 0 and isinstance(i, int) and i == 0):
                                dve.wait_ge(accw0, (i * RG + k) * TG + t)
                            dve.tensor_tensor(acc_w[:, ds(v, P)], acc_w[:, ds(v, P)], bank[2 + k % 2][0:LCOL, t * P:(t + 1) * P],
                                              ALU.add).then_inc(accw0, 1)

                    at = [None]
                    for n in range(len(SECTIONS)):
                        scan_stage(n)
                        if n:
                            rescale(n)
                        else:
                            dve.wait_ge(rel_done, 1)

                        def one_round(i, first, look):
                            if not isinstance(i, int):
                                at[0] = [dve.snap(r, min_val=0, max_val=N) for r in regs]
                            for k in range(RG):
                                if look is not None:
                                    lookup(look + k // HALF, k % HALF * 2, first and k == 0)
                                masks(i, k)
                                if k:
                                    add(i, k - 1, at[0][(k - 1) % HALF * TG:])
                                elif not first:
                                    add(i - 1, RG - 1, at[0][-TG:])
                                if k % HALF == 0:
                                    at[0] = first_nodes(dve, regs, i, k // HALF)
                        section_rounds(dve, n, one_round)
                        add(first_round[n + 1] - 1, RG - 1, [dve.snap(r, min_val=0, max_val=N) for r in regs][-TG:])
                        if n + 1 < len(SECTIONS):
                            pick_pair(first_round[n + 2] - 1, RG - 2)
                        dve.wait_ge(acc0, first_round[n + 1] * RT)
                        dve.wait_ge(accw0, first_round[n + 1] * RT)

                @block.tensor
                def _(pe):
                    pe.wait_ge(prep, PREP_ALL)

                    def look_first(j, k, first):
                        pe.wait_ge(ohl_done, j * RG + k + 1)
                        if not (first and k < 2):
                            pe.wait_ge(pick_done, j * RG + k - 1)
                        for part in range(3):
                            last = pe.matmul(bank[4 + k % 2][0:SH * NB, :], tab[:, part], onehot_lo[:, k % 2], start=(part == 0), stop=(part == 2))
                        last.then_inc(look1, 1)

                    def look_second(j, k, first):
                        pe.wait_ge(pick_done, j * RG + k + 1)
                        if not (first and k < 2):
                            pe.wait_ge(logit_done, j * RG + k - 1)
                        for t in range(TG):
                            last = pe.matmul(bank[6 + k % 2][:, t * SH:(t + 1) * SH], picked[:, k % 2, t * P:(t + 1) * P], row_head[:, :],
                                             start=True, stop=True)
                        last.then_inc(look2, 1)

                    def second_pair(j, k, first=False):
                        for q in range(2):
                            look_second(j, k + q, first)

                    def lookup(j, k, opening, first=False):
                        for q in range(2):
                            look_first(j, k + q, first)
                        if not opening:
                            second_pair(*before(j, k), first and k == 2)

                    for k in range(0, RG, 2):
                        lookup(0, k, k == 0, True)
                    if SECTIONS[0] > 1:
                        with pe.Fori(1, SECTIONS[0]) as j:
                            for k in range(0, RG, 2):
                                lookup(j, k, False)
                    second_pair(SECTIONS[0] - 1, RG - 2)

                    def aggregate(i, k):
                        pe.wait_ge(oh0, (i * RG + k + 1) * TG)
                        pe.wait_ge(scaled0, (i * RG + k + 1) * TG * SH)
                        pe.wait_ge(stat0, i * RG + k + 1)
                        if not (isinstance(i, int) and i * RG + k < 2):
                            pe.wait_ge(acc0, (i * RG + k - 1) * TG)
                            pe.wait_ge(accw0, (i * RG + k - 1) * TG)
                        for t in range(TG):
                            pe.matmul(bank[k % 2][:, t * P:(t + 1) * P], rows[:, k, t, :], onehot[:, k % 2, t, :], start=True, stop=True)
                            last = pe.matmul(bank[2 + k % 2][0:LCOL, t * P:(t + 1) * P], stat[:, k % 2, t, :], onehot[:, k % 2, t, :],
                                             start=True, stop=True)
                        last.then_inc(agg0, 1)

                    for n in range(len(SECTIONS)):
                        pe.wait_ge(logit_done, first_round[n + 1] * RG)
                        for b, (t0, m) in enumerate(tile_blocks(n)):
                            if b >= 2:
                                pe.wait_ge(t_copied, blocks_before[n] + b - 1)
                            for h in range(SH):
                                last = pe.transpose(bank[6 + b % 2][0:m, h * P:(h + 1) * P], edge_logit[:, t0:t0 + m, h], ident[:, :])
                            last.then_inc(t_done, 1)
                        pe.wait_ge(bl_in, sum(bl_count(m) for m in range(n + 1)))
                        for b, (t0, m) in enumerate(tile_blocks(n)):
                            if b >= 2:
                                pe.wait_ge(bt_copied, 2 * (blocks_before[n] + b - 1))
                            for kk in range(2 * SH):
                                last = pe.transpose(bank[4 + b % 2][:, kk * P:kk * P + m], blocks_w[0:m, kk, b, :], ident[0:m, 0:m])
                            last.then_inc(bt_done, 1)
                        pe.wait_ge(bt_copied, 2 * blocks_before[n + 1])

                        def one_round(i, first, look):
                            for k in range(RG):
                                if look is not None:
                                    lookup(look + k // HALF, k % HALF * 2, first and k == 0)
                                aggregate(i, k)
                        section_rounds(pe, n, one_round)
                        if n + 1 < len(SECTIONS):
                            second_pair(first_round[n + 2] - 1, RG - 2)

                @block.scalar
                def _(act):
                    def keep(j, k):
                        act.wait_ge(look2, j * RG + k + 1)
                        act.copy(edge_logit[:, ds((j * RG + k) * TG - keep.base, TG), :].rearrange("p t h -> p (t h)"),
                                 bank[6 + k % 2][:, 0:TG * SH]).then_inc(logit_done, 1)

                    def keep_pair(j, k):
                        for q in range(2):
                            keep(j, k + q)

                    keep.base = 0
                    with act.Fori(0, SECTIONS[0]) as j:
                        for k in range(0, RG, 2):
                            keep_pair(j, k)

                    def scan_stage(n):
                        L = SECTIONS[n] * RT
                        e0, e1 = first_round[n] * RT * P, first_round[n + 1] * RT * P
                        lin = lin_dram[:, e0:e1]
                        for j in range(3):
                            act.dma_start(dn[:, j, 0:L], a["dst_line"][e0 + j:e1 + j].rearrange("(p n) -> p n", p=P)).then_inc(dn_in, 16)
                        if n:
                            act.dma_start(old_row[:, :], bound_dram[n:n + 1, 0, :]).then_inc(old_in, 16)
                            for h in range(SH):
                                act.dma_start(old_new[h * HC:(h + 1) * HC, 0, :], bound_dram[n, 0, h:h + 1].partition_broadcast(HC)).then_inc(old_in, 16)
                            act.dma_start(old_new_w[:, 0, :], bound_dram[n, 0, :].rearrange("(h o) -> h o", o=1)).then_inc(old_in, 16)
                            for q in range(2):
                                act.dma_start(bound[:, q:q + 1], a["dst_line"][e0 + q:e0 + q + 1].partition_broadcast(P)).then_inc(bound_in, 16)
                        for b, (t0, m) in enumerate(tile_blocks(n)):
                            act.wait_ge(t_done, blocks_before[n] + b + 1)
                            act.copy(turned_l[0:m, :, b, :], bank[6 + b % 2][0:m, 0:SH * P].rearrange("p (h n) -> p h n", h=SH)).then_inc(t_copied, 1)
                            act.wait_ge(t_copied, blocks_before[n] + b + 1)
                            act.dma_start(lin[:, t0 * P:(t0 + m) * P].rearrange("h (t p) -> t h p", p=P), turned_l[0:m, :, b, :]).then_inc(lin_out, 16)
                        act.wait_ge(lin_out, 16 * blocks_before[n + 1])
                        act.dma_start(lg[:, :, 0:L], lin.rearrange("h (p n) -> p h n", p=P)).then_inc(lg_in, 16)
                        for way in range(2):
                            w = 2 * n + way
                            act.wait_ge(col_ready, w + 1)
                            act.dma_start(carry_dram[way], cols[:, way, :]).then_inc(col_out, 16)
                            act.wait_ge(col_out, 16 * (w + 1))
                            act.dma_start(rowv[:, way], carry_dram[way:way + 1].rearrange("o q k -> o k q")).then_inc(row_in, 16)
                            act.wait_ge(row_ready, w + 1)
                            act.dma_start(carried_dram[way:way + 1, :, :], rowc[:, way, :, way:way + P]).then_inc(carry_out, 16)
                            act.wait_ge(carry_out, 16 * (w + 1))
                            act.dma_start(carry[:, way], carried_dram[way].rearrange("k q -> q k")).then_inc(carry_in, 16)
                        act.wait_ge(m_ready, n + 1)
                        if n:
                            act.dma_start(bound_dram[n:n + 1, 1, :], run2[0:1, :, 0]).then_inc(old_out, 16)
                        if n + 1 < len(SECTIONS):
                            act.dma_start(bound_dram[n + 1:n + 2, 0, :], run2[P - 1:P, :, L - 1]).then_inc(old_out, 16)
                        act.activation(lg[:, :, 0:L], lg[:, :, 0:L], ACT.Exp).then_inc(w_exp, 1)
                        act.wait_ge(w_exp, n + 1)
                        act.wait_ge(res_ready, n + 1)
                        act.dma_start(w_dram[0:SH, e0:e1].rearrange("k (p n) -> p k n", p=P), lg[:, :, 0:L]).then_inc(res_out, 16)
                        act.dma_start(w_dram[SH:, e0:e1].rearrange("k (p n) -> p k n", p=P), run[:, :, 0:L]).then_inc(res_out, 16)
                        if n + 1 < len(SECTIONS) or n:
                            act.wait_ge(old_out, 16 * (2 * n + (n + 1 < len(SECTIONS))))
                        if n:
                            for h in range(SH):
                                act.dma_start(old_new[h * HC:(h + 1) * HC, 1, :], bound_dram[n, 1, h:h + 1].partition_broadcast(HC)).then_inc(new_in, 16)
                            act.dma_start(old_new_w[:, 1, :], bound_dram[n, 1, :].rearrange("(h o) -> h o", o=1)).then_inc(new_in, 16)
                        act.wait_ge(res_out, 32 * (n + 1))
                        full = L // P
                        if full:
                            for kk in range(2 * SH):
                                act.dma_start(blocks_w[:, kk, 0:full, :],
                                              w_dram[kk, e0:e0 + full * P * P].rearrange("(b t p) -> t b p", t=P, p=P)).then_inc(bl_in, 16)
                        if L % P:
                            act.dma_start(blocks_w[0:L % P, :, full, :],
                                          w_dram[:, e0 + full * P * P:e1].rearrange("k (t p) -> t k p", p=P)).then_inc(bl_in, 16)
                        for b, (t0, m) in enumerate(tile_blocks(n)):
                            act.wait_ge(bt_done, blocks_before[n] + b + 1)
                            ps = bank[4 + b % 2][:, :].rearrange("p (k n) -> p n k", k=2 * SH)
                            act.copy(edge_w[:, t0:t0 + m, 0:SH], ps[:, 0:m, 0:SH]).then_inc(bt_copied, 1)
                            act.copy(edge_w[:, t0:t0 + m, SH + 1:], ps[:, 0:m, SH:]).then_inc(bt_copied, 1)
                        if n:
                            act.wait_ge(delta_ready, n)
                            act.activation(factor[:, :], factor[:, :], ACT.Exp).then_inc(factor_done, 1)
                            act.activation(factor_w[:, :], factor_w[:, :], ACT.Exp).then_inc(factor_done, 1)
                        act.wait_ge(bt_copied, 2 * blocks_before[n + 1])

                    def weigh(i, k, base):
                        if not (isinstance(i, int) and i * RG + k < 2):
                            act.wait_ge(agg0, i * RG + k - 1)
                        act.copy(stat[:, k % 2].rearrange("p t c -> p (t c)"),
                                 edge_w[:, ds(i * RT + k * TG - base, TG), :].rearrange("p t c -> p (t c)")).then_inc(stat0, 1)
                        act.wait_ge(gathered[0][k], 16 * TG * (i + 1))
                        act.wait_ge(stat0, i * RG + k + 1)
                        for t in range(TG):
                            for h in range(SH):
                                act.activation(rows[:, k, t, h * HC:(h + 1) * HC], rows[:, k, t, h * HC:(h + 1) * HC], ACT.Copy,
                                               scale=stat[:, k % 2, t, h:h + 1]).then_inc(scaled0, 1)

                    for n in range(len(SECTIONS)):
                        scan_stage(n)
                        keep.base = first_round[n + 1] * RT

                        def one_round(i, first, look):
                            for k in range(RG):
                                if look is not None and not (first and k < 2):
                                    keep_pair(*before(look + k // HALF, k % HALF * 2, 2))
                                weigh(i, k, first_round[n] * RT)
                        section_rounds(act, n, one_round)
                        if n + 1 < len(SECTIONS):
                            keep_pair(first_round[n + 2] - 1, RG - 4)
                            keep_pair(first_round[n + 2] - 1, RG - 2)

        with ExitStack() as st:
            sums_t = sb("sums_t", [P, NB, LCOL], st=st)
            top = sb("top", [P, NB, HEADS], st=st)
            seg = sb("seg", [P, NB, HEADS], st=st)
            den = sb("den", [P, NB, HEADS], st=st)
            ca = sb("ca", [P, NB, HEADS], st=st)
            cb = sb("cb", [P, NB, HEADS], st=st)
            bias_all = sb("bias_all", [P, CH], st=st)
            bn1_all = sb("bn1_all", [P, CH], st=st)
            wn1a = sb("wn1a", [P, CH], st=st)
            part = sb("part", [P, 2, CB, CH], st=st)
            normed1 = sb("normed1", [P, 3, CB, CH], st=st)
            squares1 = sb("squares1", [P, 1, CB, CH], st=st)
            turned1 = sb("turned1", [P, 1, CB * P], st=st)
            proj = sb("proj", [P, 2, CB, CH], st=st)
            stats = sb("stats", [P, 5, NB], st=st)
            (b_in, sw_t, sw_c, b_chain, e_in, e_done, s_t, comb, centred1, squared1, varsum1, std1, norm1, hrelu1, turned1_s, relu1_s,
             proj1, rows1, table1_out, base1) = (
                sem(n) for n in ("b_in", "sw_t", "sw_c", "b_chain", "e_in", "e_done", "s_t", "comb", "centred1", "squared1", "varsum1",
                                 "std1", "norm1", "hrelu1", "turned1_s", "relu1_s", "proj1", "rows1", "table1_out", "base1"))
            with nc.Block() as block:
                @block.sync
                def _(sp):
                    sp.dma_start(bias_all[:, :], a["bias"].partition_broadcast(P)).then_inc(b_in, 16)
                    sp.dma_start(bn1_all[:, :], a["bn1"].partition_broadcast(P)).then_inc(b_in, 16)
                    sp.dma_start(wn1a[:, :], a["Wn1"][0:CH, :]).then_inc(b_in, 16)
                    for c in range(CHUNKS):
                        sp.wait_ge(rows1, 2 * (c + 1))
                        sp.dma_start(table2[c * CB * P:(c + 1) * CB * P, :].rearrange("(b p) c -> p b c", p=P), proj[:, c % 2]).then_inc(table1_out, 16)
                        sp.wait_ge(table1_out, 16 * (c + 1))

                @block.tensor
                def _(pe):
                    for b in range(NB):
                        last = pe.transpose(bank[7][:, b * LCOL:(b + 1) * LCOL], acc_w[:, b * P:(b + 1) * P], ident[0:LCOL, 0:LCOL])
                    last.then_inc(sw_t, 1)

                    def turn_sums(c):
                        if c >= 1:
                            pe.wait_ge(comb, c)
                        for b in range(CB):
                            last = pe.transpose(bank[b // 4][:, b % 4 * P:(b % 4 + 1) * P], acc[:, (c * CB + b) * P:(c * CB + b + 1) * P], ident[:, :])
                        last.then_inc(s_t, 1)

                    def turn(c):
                        pe.wait_ge(hrelu1, c + 1)
                        if c >= 1:
                            pe.wait_ge(relu1_s, 2 * c)
                        for b in range(CB):
                            last = pe.transpose(bank[2 + b // 4][:, b % 4 * P:(b % 4 + 1) * P], normed1[:, c % 3, b, :], ident[:, :])
                        last.then_inc(turned1_s, 1)

                    def project(c):
                        pe.wait_ge(relu1_s, 2 * (c + 1))
                        pe.wait_ge(b_in, 16 * 3)
                        if c >= 1:
                            pe.wait_ge(rows1, 2 * c)
                        for b in range(CB):
                            last = pe.matmul(bank[4 + b // 4][:, b % 4 * P:(b % 4 + 1) * P], turned1[:, 0, b * P:(b + 1) * P], wn1a[:, :],
                                             start=True, stop=True)
                        last.then_inc(proj1, 1)
                    turn_sums(0)
                    for c in range(CHUNKS):
                        if c + 1 < CHUNKS:
                            turn_sums(c + 1)
                        turn(c)
                        project(c)

                @block.vector
                def _(dve):
                    n = [0]

                    def link(ins):
                        n[0] += 1
                        ins.then_inc(b_chain, 1)
                        dve.wait_ge(b_chain, n[0])
                    dve.wait_ge(sw_t, 1)
                    link(dve.tensor_copy(sums_t[:, :, :].rearrange("p b c -> p (b c)"), bank[7][:, 0:NB * LCOL]))
                    link(dve.tensor_copy(seg[:, :, 0:SH], sums_t[:, :, SH + 1:]))
                    link(dve.tensor_copy(seg[:, :, SH:], logit[:, :, SH:]))
                    link(dve.tensor_tensor(top[:, :, :], seg[:, :, :], logit[:, :, :], ALU.max))
                    link(dve.tensor_tensor(seg[:, :, :], seg[:, :, :], top[:, :, :], ALU.subtract))
                    link(dve.tensor_tensor(cb[:, :, :], logit[:, :, :], top[:, :, :], ALU.subtract))
                    dve.engine_nop().then_inc(e_in, 1)
                    dve.wait_ge(e_done, 2)
                    link(dve.tensor_tensor(den[:, :, 0:SH], sums_t[:, :, 0:SH], ca[:, :, 0:SH], ALU.mult))
                    link(dve.tensor_tensor(den[:, :, SH:], sums_t[:, :, SH:SH + 1].broadcast_to([P, NB, SH]), ca[:, :, SH:], ALU.mult))
                    link(dve.tensor_tensor(den[:, :, :], den[:, :, :], cb[:, :, :], ALU.add))
                    link(dve.reciprocal(den[:, :, :], den[:, :, :]))
                    link(dve.tensor_tensor(ca[:, :, :], ca[:, :, :], den[:, :, :], ALU.mult))
                    link(dve.tensor_tensor(cb[:, :, :], cb[:, :, :], den[:, :, :], ALU.mult))
                    dve.wait_ge(b_in, 16 * 3)

                    def heads(v):
                        return v.rearrange("p b (h c) -> p b h c", h=HEADS)

                    def per_head(v, b0, m):
                        return v[:, b0:b0 + m, :].unsqueeze(3).broadcast_to([P, m, HEADS, HC])

                    def combine(c):
                        blk = slice(c * CB, (c + 1) * CB)
                        dve.wait_ge(s_t, c + 1)
                        for j, (b0, m) in enumerate(((0, 4), (4, 3))):
                            ins = dve.tensor_tensor(heads(part[:, 0, b0:b0 + m]), heads(bank[j][:, 0:m * P].rearrange("p (m c) -> p m c", m=m)),
                                                    per_head(ca, c * CB + b0, m), ALU.mult)
                            link(ins)
                        dve.engine_nop().then_inc(comb, 1)
                        link(dve.tensor_tensor(heads(part[:, 1]), heads(feat[:, blk, :]), per_head(cb, c * CB, CB), ALU.mult))
                        link(dve.tensor_tensor(part[:, 0], part[:, 0], part[:, 1], ALU.add))
                        link(dve.tensor_tensor(part[:, 0], part[:, 0], bias_all[:, :].unsqueeze(1).broadcast_to([P, CB, CH]), ALU.add))
                        link(dve.tensor_tensor(x_rows[:, blk, :], x_rows[:, blk, :], part[:, 0], ALU.add))

                    def centre(c):
                        blk = slice(c * CB, (c + 1) * CB)
                        link(dve.tensor_reduce(stats[:, 0, blk], x_rows[:, blk, :], AX.X, ALU.add))
                        link(dve.tensor_scalar(stats[:, 1, blk], stats[:, 0, blk], -1.0 / CH, None, ALU.mult))
                        dve.tensor_tensor(normed1[:, c % 3], x_rows[:, blk, :],
                                          stats[:, 1, blk].unsqueeze(2).broadcast_to([P, CB, CH]), ALU.add).then_inc(centred1, 1)

                    def scale(c):
                        blk = slice(c * CB, (c + 1) * CB)
                        dve.wait_ge(squared1, c + 1)
                        dve.tensor_reduce(stats[:, 2, blk], squares1[:, 0], AX.X, ALU.add).then_inc(varsum1, 1)
                        dve.wait_ge(std1, c + 1)
                        link(dve.reciprocal(stats[:, 4, blk], stats[:, 3, blk]))
                        dve.tensor_tensor(normed1[:, c % 3], normed1[:, c % 3],
                                          stats[:, 4, blk].unsqueeze(2).broadcast_to([P, CB, CH]), ALU.mult).then_inc(norm1, 1)

                    def residual(c):
                        blk = slice(c * CB, (c + 1) * CB)
                        dve.wait_ge(hrelu1, c + 1)
                        dve.tensor_tensor(x_rows[:, blk, :], x_rows[:, blk, :], normed1[:, c % 3], ALU.add).then_inc(base1, 1)

                    def evacuate(c):
                        dve.wait_ge(proj1, c + 1)
                        if c >= 2:
                            dve.wait_ge(table1_out, 16 * (c - 1))
                        for j, (b0, m) in enumerate(((0, 4), (4, 3))):
                            dve.tensor_tensor(proj[:, c % 2, b0:b0 + m], bank[4 + j][:, 0:m * P].rearrange("p (m c) -> p m c", m=m),
                                              bn1_all[:, :].unsqueeze(1).broadcast_to([P, m, CH]), ALU.add).then_inc(rows1, 1)
                    for c in range(CHUNKS + 1):
                        if c < CHUNKS:
                            combine(c)
                            centre(c)
                            scale(c)
                        if c >= 1:
                            residual(c - 1)
                            evacuate(c - 1)
                    dve.wait_ge(base1, CHUNKS)

                @block.scalar
                def _(act):
                    act.wait_ge(e_in, 1)
                    act.activation(ca[:, :, :], seg[:, :, :], ACT.Exp).then_inc(e_done, 1)
                    act.activation(cb[:, :, :], cb[:, :, :], ACT.Exp).then_inc(e_done, 1)
                    for c in range(CHUNKS):
                        blk = slice(c * CB, (c + 1) * CB)
                        act.wait_ge(centred1, c + 1)
                        act.activation(squares1[:, 0], normed1[:, c % 3], ACT.Square).then_inc(squared1, 1)
                        act.wait_ge(varsum1, c + 1)
                        act.activation(stats[:, 3, blk], stats[:, 2, blk], ACT.Sqrt, bias=eps_col[:, 0:1], scale=1.0 / CH).then_inc(std1, 1)
                        act.wait_ge(norm1, c + 1)
                        act.activation(normed1[:, c % 3], normed1[:, c % 3], ACT.Relu).then_inc(hrelu1, 1)
                        act.wait_ge(turned1_s, c + 1)
                        if c >= 1:
                            act.wait_ge(proj1, c)
                        act.copy(turned1[:, 0, 0:4 * P], bank[2][:, :]).then_inc(relu1_s, 1)
                        act.copy(turned1[:, 0, 4 * P:], bank[3][:, 0:3 * P]).then_inc(relu1_s, 1)

        with ExitStack() as st:
            we1 = sb("we1", [EC, CH], st=st)
            we2 = sb("we2", [P, CH], st=st)
            wn1b = sb("wn1b", [P, CH], st=st)
            be1 = sb("be1", [P, 1], st=st)
            be2 = sb("be2", [P, 1], st=st)
            wt = sb("wt", [P, 1], st=st)
            bt = sb("bt", [P, 1], st=st)
            ea = sb("ea", [EC, 2, HALF * GE], st=st)
            ts = sb("ts", [P, 2, HALF * GE], st=st)
            hidden = sb("hidden", [P, 2, GE], st=st)
            gate = sb("gate", [P, 2, GE], st=st)
            ef = sb("ef", [P, 2, GE], st=st)
            pre = sb("pre", [P, 2, TG, P], st=st)
            msg = sb("msg", [P, 2, TG, P], st=st)
            w1_in, zero1, oh1, h1, r1, h2, gt, efd, z1, radd, r2, agg1, acc1 = (
                sem(n) for n in ("w1_in", "zero1", "oh1", "h1", "r1", "h2", "gt", "efd", "z1", "radd", "r2", "agg1", "acc1"))
            ea_in = [sem(f"ea_in{h}") for h in range(2)]
            ts_in = [sem(f"ts_in{h}") for h in range(2)]
            with nc.Block() as block:
                @block.sync
                def _(sp):
                    sp.dma_start(we1[:, :], a["We1"]).then_inc(w1_in, 16)
                    sp.dma_start(we2[:, :], a["We2"]).then_inc(w1_in, 16)
                    sp.dma_start(wn1b[:, :], a["Wn1"][CH:, :]).then_inc(w1_in, 16)
                    for col, name in ((be1, "be1"), (be2, "be2"), (bt, "bt")):
                        sp.dma_start(col[:, :], a[name].rearrange("(c o) -> c o", o=1)).then_inc(w1_in, 16)
                    sp.dma_start(wt[:, :], a["Wt"].rearrange("o c -> c o")).then_inc(w1_in, 16)

                    def load(i, first):
                        for h in range(2):
                            load_indices(sp, 1, i, h, first)
                            e0 = (i * RG + h * HALF) * GE
                            if not first:
                                sp.wait_ge(h1, RG * (i - 1) + HALF * (h + 1))
                                sp.wait_ge(gt, RG * (i - 1) + HALF * (h + 1))
                            sp.dma_start(ea[:, h, :], a["ea_t"][:, ds(e0, HALF * GE)]).then_inc(ea_in[h], 16)
                            sp.dma_start(ts[:, h, :], a["ts"][ds(e0, HALF * GE)].partition_broadcast(P)).then_inc(ts_in[h], 16)
                    load(0, True)
                    with sp.Fori(1, ROUNDS) as i:
                        load(i, False)

                @block.gpsimd
                def _(gp):
                    for k in range(RG):
                        gather(gp, 1, table2, 0, k, True, radd)
                    with gp.Fori(1, ROUNDS) as i:
                        for k in range(RG):
                            gather(gp, 1, table2, i, k, False, radd)

                def skewed(eng, parts):
                    def steps(i, first):
                        for k in range(RG):
                            for lag, part_of in parts:
                                if k >= lag:
                                    part_of(i, k - lag, first)
                                elif not first:
                                    part_of(i - 1, k - lag + RG, False)
                    steps(0, True)
                    with eng.Fori(1, ROUNDS) as i:
                        steps(i, False)
                    for k in range(3):
                        for lag, part_of in parts:
                            if k < lag:
                                part_of(ROUNDS - 1, k - lag + RG, False)

                @block.tensor
                def _(pe):
                    pe.wait_ge(w1_in, 16 * 7)

                    def first_product(i, k, first):
                        if k % HALF == 0:
                            pe.wait_ge(ea_in[k // HALF], 16 * (i + 1))
                        if not (first and k < 2):
                            pe.wait_ge(r1, i * RG + k - 1)
                        pe.matmul(bank[k % 2][:, :], we1[:, :], ea[:, k // HALF, k % HALF * GE:(k % HALF + 1) * GE], start=True, stop=True).then_inc(h1, 1)

                    def second_product(i, k, first):
                        pe.wait_ge(r1, i * RG + k + 1)
                        if not (first and k < 2):
                            pe.wait_ge(efd, i * RG + k - 1)
                        pe.matmul(bank[2 + k % 2][:, :], we2[:, :], hidden[:, k % 2], start=True, stop=True).then_inc(h2, 1)

                    def third_product(i, k, first):
                        pe.wait_ge(efd, i * RG + k + 1)
                        if not (first and k < 2):
                            pe.wait_ge(radd, i * RG + k - 1)
                        for t in range(TG):
                            last = pe.matmul(bank[4 + k % 2][:, t * P:(t + 1) * P], ef[:, k % 2, t * P:(t + 1) * P], wn1b[:, :], start=True, stop=True)
                        last.then_inc(z1, 1)

                    def aggregate(i, k, first):
                        pe.wait_ge(r2, i * RG + k + 1)
                        pe.wait_ge(oh1, (i * RG + k + 1) * TG)
                        if not (first and k < 2):
                            pe.wait_ge(acc1, (i * RG + k - 1) * TG)
                        for t in range(TG):
                            last = pe.matmul(bank[6 + k % 2][:, t * P:(t + 1) * P], msg[:, k % 2, t, :], onehot[:, k % 2, t, :], start=True, stop=True)
                        last.then_inc(agg1, 1)
                    skewed(pe, ((0, first_product), (1, second_product), (2, third_product), (3, aggregate)))

                @block.scalar
                def _(act):
                    act.wait_ge(w1_in, 16 * 7)

                    def relu_hidden(i, k, first):
                        act.wait_ge(h1, i * RG + k + 1)
                        if not (first and k < 2):
                            act.wait_ge(h2, i * RG + k - 1)
                        act.activation(hidden[:, k % 2], bank[k % 2][:, :], ACT.Relu, bias=be1[:, 0:1]).then_inc(r1, 1)

                    def time_gate(i, k, first):
                        if k % HALF == 0:
                            act.wait_ge(ts_in[k // HALF], 16 * (i + 1))
                        if not (first and k < 2):
                            act.wait_ge(efd, i * RG + k - 1)
                        act.activation(gate[:, k % 2], ts[:, k // HALF, k % HALF * GE:(k % HALF + 1) * GE], ACT.Sigmoid,
                                       bias=bt[:, 0:1], scale=wt[:, 0:1]).then_inc(gt, 1)

                    def relu_message(i, k, first):
                        act.wait_ge(radd, i * RG + k + 1)
                        if not (first and k < 2):
                            act.wait_ge(agg1, i * RG + k - 1)
                        act.activation(msg[:, k % 2], pre[:, k % 2], ACT.Relu).then_inc(r2, 1)
                    skewed(act, ((0, relu_hidden), (0, time_gate), (2, relu_message)))

                @block.vector
                def _(dve):
                    regs = [dve.alloc_register(f"first1_{n}") for n in range(HALF * TG)]
                    dve.memset(acc[:, :], 0.0).then_inc(zero1, 1)
                    dve.wait_ge(zero1, 1)
                    dve.wait_ge(w1_in, 16 * 7)

                    def masks(i, k, first):
                        if not (first and k < 2):
                            dve.wait_ge(agg1, i * RG + k - 1)
                        for t in range(TG):
                            dve.tensor_scalar(onehot[:, k % 2, t, :], iota_row[:, :], dst_rel[:, ds(i * RT + k * TG + t, 1)], None,
                                              ALU.is_equal).then_inc(oh1, 1)

                    def gated(i, k, first):
                        dve.wait_ge(h2, i * RG + k + 1)
                        dve.wait_ge(gt, i * RG + k + 1)
                        if not (first and k < 2):
                            dve.wait_ge(z1, i * RG + k - 1)
                        dve.scalar_tensor_tensor(ef[:, k % 2], bank[2 + k % 2][:, :], be2[:, 0:1], gate[:, k % 2], ALU.add, ALU.mult).then_inc(efd, 1)

                    def add_sender(i, k, first):
                        dve.wait_ge(z1, i * RG + k + 1)
                        dve.wait_ge(gathered[1][k], 16 * TG * (i + 1))
                        if not (first and k < 2):
                            dve.wait_ge(r2, i * RG + k - 1)
                        dve.tensor_tensor(pre[:, k % 2], bank[4 + k % 2][:, :].rearrange("p (t c) -> p t c", t=TG), rows[:, k], ALU.add).then_inc(radd, 1)

                    at = [None]

                    def add(i, k, first):
                        if k % HALF == 0:
                            at[0] = first_nodes(dve, regs, i, k // HALF)
                        dve.wait_ge(agg1, i * RG + k + 1)
                        for t in range(TG):
                            v = at[0][k % HALF * TG + t]
                            if not (first and k == 0 and t == 0):
                                dve.wait_ge(acc1, (i * RG + k) * TG + t)
                            dve.tensor_tensor(acc[:, ds(v, P)], acc[:, ds(v, P)], bank[6 + k % 2][:, t * P:(t + 1) * P], ALU.add).then_inc(acc1, 1)

                    def steps(i, first):
                        for k in range(RG):
                            for lag, part_of in ((2, masks), (1, gated), (2, add_sender), (3, add)):
                                if k >= lag:
                                    part_of(i, k - lag, first)
                                elif not first:
                                    part_of(i - 1, k - lag + RG, False)
                    steps(0, True)
                    with dve.Fori(1, ROUNDS) as i:
                        at[0] = [dve.snap(r, min_val=0, max_val=N) for r in regs]
                        steps(i, False)
                    at[0] = [dve.snap(r, min_val=0, max_val=N) for r in regs]
                    for k in range(3):
                        for lag, part_of in ((2, masks), (1, gated), (2, add_sender), (3, add)):
                            if k < lag:
                                part_of(ROUNDS - 1, k - lag + RG, False)
                    dve.wait_ge(acc1, TILES)

        with ExitStack() as st:
            outs = sb("outs", [P, 2, CB, CH], st=st)
            f_done, o_done, o_out = (sem(n) for n in ("f_done", "o_done", "o_out"))
            with nc.Block() as block:
                @block.tensor
                def _(pe):
                    for c in range(CHUNKS):
                        if c >= 2:
                            pe.wait_ge(o_done, 2 * (c - 1))
                        for b in range(CB):
                            o = slice((c * CB + b) * P, (c * CB + b + 1) * P)
                            ps = bank[c % 2 * 2 + b // 4][:, b % 4 * P:(b % 4 + 1) * P]
                            pe.matmul(ps, acc[:, o], wn2[:, :], start=True, stop=False)
                            last = pe.matmul(ps, acc_w[:, o], wl_node[:, :], start=False, stop=True)
                        last.then_inc(f_done, 1)

                @block.vector
                def _(dve):
                    for c in range(CHUNKS):
                        dve.wait_ge(f_done, c + 1)
                        if c >= 2:
                            dve.wait_ge(o_out, 16 * (c - 1))
                        for j, (b0, m) in enumerate(((0, 4), (4, 3))):
                            dve.tensor_tensor(outs[:, c % 2, b0:b0 + m], bank[c % 2 * 2 + j][:, 0:m * P].rearrange("p (m c) -> p m c", m=m),
                                              x_rows[:, c * CB + b0:c * CB + b0 + m, :], ALU.add).then_inc(o_done, 1)

                @block.sync
                def _(sp):
                    for c in range(CHUNKS):
                        sp.wait_ge(o_done, 2 * (c + 1))
                        n0 = c * CB * P
                        full = min(CB, (N - n0) // P)
                        sp.dma_start(out[n0:n0 + full * P, :].rearrange("(b p) c -> p b c", p=P), outs[:, c % 2, 0:full, :]).then_inc(o_out, 16)
                        if full < CB:
                            sp.wait_ge(o_out, 16 * (c + 1))
                            rest = N - n0 - full * P
                            sp.dma_start(out[n0 + full * P:N, :], outs[0:rest, c % 2, full, :]).then_inc(o_out, 16)
                        else:
                            sp.wait_ge(o_out, 16 * (c + 1))
                    sp.wait_ge(o_out, 16 * (CHUNKS + 1))


def kernel(**inputs):
    import numpy as np
    import concourse.bacc as bacc
    from concourse.bass_utils import run_bass_kernel_spmd

    def arr(name):
        return np.ascontiguousarray(np.asarray(inputs[name]))

    def padded(v, shape, fill=0):
        full = np.full(shape, fill, v.dtype)
        full[tuple(slice(0, s) for s in v.shape)] = v
        return full

    src = padded(arr("src"), (EPAD,))
    dst = padded(arr("dst"), (EPAD,), N)
    line = np.full((EPAD + 2,), -1, dst.dtype)
    line[1:EPAD + 1] = dst
    feed = {
        "x": padded(arr("x"), (NPAD, CH)),
        "src_lin": src.reshape(P, EPAD // P),
        "src_tile": np.ascontiguousarray(src.reshape(TILES, P).T),
        "dst_tile": np.ascontiguousarray(dst.reshape(TILES, P).T),
        "dst_first": np.ascontiguousarray(dst.reshape(TILES, P)[:, 0]).reshape(1, TILES),
        "dst_line": line,
        "ea_t": np.ascontiguousarray(padded(arr("edge_attr_64"), (EPAD, EC)).T),
        "ts": padded(arr("edge_weight"), (EPAD,)),
        "W": arr("L0_gnn_W"), "b_lin": arr("L0_gnn_b_lin"), "alpha": arr("L0_gnn_alpha"), "bias": arr("L0_gnn_bias"),
        "We1": arr("L1_gnn_We1"), "be1": arr("L1_gnn_be1"), "We2": arr("L1_gnn_We2"), "be2": arr("L1_gnn_be2"),
        "Wt": arr("L1_gnn_Wt"), "bt": arr("L1_gnn_bt"), "Wn1": arr("L1_gnn_Wn1"), "bn1": arr("L1_gnn_bn1"),
        "Wn2": arr("L1_gnn_Wn2"), "bn2": arr("L1_gnn_bn2"),
    }
    nc = bacc.Bacc("TRN2", target_bir_lowering=False, num_devices=1)
    arrays, aps = {}, {}
    for name, v in feed.items():
        arrays[f"in_{name}"] = v
        aps[name] = nc.dram_tensor(f"in_{name}", v.shape, mybir.dt.from_np(v.dtype), kind="ExternalInput").ap()
    fp32, bf16 = mybir.dt.float32, mybir.dt.bfloat16
    out = nc.dram_tensor("out_0", (N, CH), fp32, kind="ExternalOutput").ap()
    table1 = nc.dram_tensor("table1", (NPAD, CH), fp32, kind="Internal").ap()
    table2 = nc.dram_tensor("table2", (NPAD, CH), fp32, kind="Internal").ap()
    bound_dram = nc.dram_tensor("bound_dram", (len(SECTIONS), 2, SH), fp32, kind="Internal").ap()
    parts_dram = nc.dram_tensor("parts_dram", (2, EPAD), bf16, kind="Internal").ap()
    lin_dram = nc.dram_tensor("lin_dram", (SH, EPAD), fp32, kind="Internal").ap()
    w_dram = nc.dram_tensor("w_dram", (2 * SH, EPAD), fp32, kind="Internal").ap()
    carry_dram = nc.dram_tensor("carry_dram", (2, P, SH + 1), fp32, kind="Internal").ap()
    carried_dram = nc.dram_tensor("carried_dram", (2, SH, P), fp32, kind="Internal").ap()
    gnn_layers(nc, aps, out, table1, table2, parts_dram, lin_dram, w_dram, carry_dram, carried_dram, bound_dram)
    return run_bass_kernel_spmd(nc, [arrays], core_ids=[0]).results[0]["out_0"]
```

```python
from contextlib import ExitStack

import concourse.bass as bass
from concourse import mybir
from concourse.alu_op_type import AluOpType as ALU

P = 128
N = 6250
E = 106250
CH = 128
EC = 64
HEADS = 4
HC = CH // HEADS
SH = 2
NB = (N + P - 1) // P
NPAD = NB * P
CB = 7
CHUNKS = NB // CB
TG = 4
GE = TG * P
RG = 8
HALF = RG // 2
GROUPS = -(-E // (GE * RG)) * RG
TILES = GROUPS * TG
ROUNDS = GROUPS // RG
EPAD = TILES * P
RT = RG * TG
ACCW = (N + P + P - 1) // P * P
BIG = 1.0e38
EPS = 1e-5
SECTIONS = (3, 4, 6, 6, 7)
PAIRS = RG // 2
PREP_PARTS, PREP_ALL = 4, 15
OLD_IN, NEW_IN = 16 * 3, 16 * 3
LCOL = 5


def bl_count(n):
    tiles = SECTIONS[n] * RT
    return 16 * (4 * (tiles // P > 0) + (tiles % P > 0))


def gnn_layers(nc, a, out, table1, table2, parts_dram, lin_dram, w_dram, bound_dram):
    fp32, bf16, i32 = mybir.dt.float32, mybir.dt.bfloat16, mybir.dt.int32
    ACT = mybir.ActivationFunctionType
    AX = mybir.AxisListType
    ds = bass.ds

    ctx = ExitStack()
    with ctx:
        ctx.enter_context(nc.allow_non_contiguous_dma(reason="columns of 128 numbers"))

        def sb(name, shape, dt=fp32, st=ctx):
            return st.enter_context(nc.sbuf_tensor(name, shape, dt))

        def sem(name):
            return ctx.enter_context(nc.semaphore(name))

        bank = [ctx.enter_context(nc.psum_tensor(f"bank{n}", [P, 512], fp32)) for n in range(8)]

        x_rows = sb("x_rows", [P, NB, CH])
        feat = sb("feat", [P, NB, CH])
        logit = sb("logit", [P, NB, HEADS])
        acc = sb("acc", [P, ACCW])
        acc_w = sb("acc_w", [LCOL, ACCW])
        ident = sb("ident", [P, P])
        iota_row = sb("iota_row", [P, P])
        iota_col = sb("iota_col", [P, 1])
        iota_int = sb("iota_int", [P, P], i32)
        iota_cint = sb("iota_cint", [P, 1], i32)
        eps_col = sb("eps_col", [P, 1])
        dst_rel = sb("dst_rel", [P, TILES])
        dst_first = sb("dst_first", [1, TILES], i32)
        rows = sb("rows", [P, RG, TG, CH])
        index = sb("index", [P, RG, TG], i32)
        onehot = sb("onehot", [P, 2, TG, P])
        count = sb("count", [P, NB])
        bn2_all = sb("bn2_all", [P, CH])
        wn2 = sb("wn2", [P, CH])

        idx_ready = [[sem(f"idx_ready{q}_{h}") for h in range(2)] for q in range(2)]
        gathered = [[sem(f"gathered{q}_{k}") for k in range(RG)] for q in range(2)]

        def load_indices(sp, q, i, h, first):
            if not first:
                for k in range(h * HALF, (h + 1) * HALF):
                    sp.wait_ge(gathered[q][k], 16 * TG * i)
            sp.dma_start(index[:, h * HALF:(h + 1) * HALF, :].rearrange("p g t -> p (g t)"),
                         a["src_tile"][:, ds(i * RT + h * HALF * TG, HALF * TG)]).then_inc(idx_ready[q][h], 16)

        slot_taken = sem("slot_taken")

        def gather(gp, q, table, i, k, first, used):
            if k % HALF == 0:
                gp.wait_ge(idx_ready[q][k // HALF], 16 * (i + 1))
            if not first:
                gp.wait_ge(used, RG * (i - 1) + k + 1)
            gp.sem_inc(slot_taken, 1)
            for t in range(TG):
                gp.indirect_dma_start(rows[:, k, t, :], None, table,
                                      bass.IndirectOffsetOnAxis(index[:, k, t:t + 1], 0)).then_inc(gathered[q][k], 16)

        def first_nodes(dve, regs, i, h):
            dve.load(regs, dst_first[0:1, ds(i * RT + h * HALF * TG, HALF * TG)])
            return [dve.snap(r, min_val=0, max_val=N) for r in regs]

        src_lin = sb("src_lin", [P, EPAD // P], i32)
        part_int = sb("part_int", [P, EPAD // P], i32)
        part_bf = sb("part_bf", [P, 2, EPAD // P], bf16)
        dst_int = src_lin[:, 0:TILES]
        first_all = part_int[:, 0:TILES]
        idx_in, first_in, prep, parts_out, dst_in = (sem(n) for n in ("idx_in", "first_in", "prep", "parts_out", "dst_in"))

        with ExitStack() as st:
            squares = sb("squares", [P, 2, CB, CH], st=st)
            centred = sb("centred", [P, 3, CB, CH], st=st)
            normed = sb("normed", [P, 2, CB, CH], st=st)
            feats_t = sb("feats_t", [P, 2, CB * P], st=st)
            nmean = sb("nmean", [P, NB], st=st)
            sums = sb("sums", [P, NB], st=st)
            sqsum = sb("sqsum", [P, NB], st=st)
            std = sb("std", [P, NB], st=st)
            rstd = sb("rstd", [P, NB], st=st)
            w0 = sb("w0", [P, CH], st=st)
            w0_t = sb("w0_t", [P, CH], st=st)
            w0_ext = sb("w0_ext", [P, CH + HEADS], st=st)
            alpha_bd = sb("alpha_bd", [P, HEADS], st=st)
            blin_col = sb("blin_col", [P, 1], st=st)
            blin_rep = sb("blin_rep", [P, P], st=st)
            bias_ext = sb("bias_ext", [P, CH + HEADS], st=st)
            zlogit = sb("zlogit", [P, NB, HEADS], st=st)

            x_in = [sem(f"x_in{c}") for c in range(CHUNKS)]
            w_in, const_set, iota_done, sel_done = (sem(n) for n in ("w_in", "const_set", "iota_done", "sel_done"))
            chain = sem("a_chain")
            w_t, w_tc, wa_done, wa_copied, ba_ready = (sem(n) for n in ("w_t", "w_tc", "wa_done", "wa_copied", "ba_ready"))
            mean_done, centred_done, squared, varsum, std_done, norm_done, relu_done, turned, copied, projected, rows_done, table_out = (
                sem(n) for n in ("mean_done", "centred_done", "squared", "varsum", "std_done", "norm_done", "relu_done", "turned", "copied",
                                 "projected", "rows_done", "table_out"))
            zero_done, w2_in = sem("zero_done"), sem("w2_in")
            small_sync = sem("small_sync")
            with nc.Block() as block:
                @block.sync
                def _(sp):
                    for c in range(CHUNKS):
                        sp.dma_start(x_rows[:, c * CB:(c + 1) * CB, :],
                                     a["x"][c * CB * P:(c + 1) * CB * P, :].rearrange("(b p) c -> p b c", p=P)).then_inc(x_in[c], 16)
                        if c == 1:
                            sp.dma_start(src_lin[:, :], a["src_lin"]).then_inc(idx_in, 16)
                            sp.wait_ge(const_set, 1)
                            for h in range(HEADS):
                                half = (h % 2) * 64
                                sp.dma_start(alpha_bd[half:half + 64, h:h + 1],
                                             a["alpha"][0, h, :].rearrange("(c o) -> c o", o=1)).then_inc(w_in, 16)
                    sp.dma_start(wn2[:, :], a["Wn2"]).then_inc(w2_in, 16)
                    sp.dma_start(bn2_all[:, :], a["bn2"].partition_broadcast(P)).then_inc(w2_in, 16)
                    sp.dma_start(dst_first[:, :], a["dst_first"]).then_inc(first_in, 16)
                    for h in range(2):
                        load_indices(sp, 0, 0, h, True)
                    sp.wait_ge(prep, PREP_PARTS)
                    sp.dma_start(parts_dram.rearrange("k (p n) -> p k n", p=P), part_bf[:, :, :]).then_inc(parts_out, 16)
                    sp.dma_start(dst_int, a["dst_tile"]).then_inc(dst_in, 16)
                    sp.dma_start(first_all, a["dst_first"].rearrange("o t -> (o t)").partition_broadcast(P)).then_inc(dst_in, 16)
                    sp.wait_ge(first_in, 16)
                    sp.wait_ge(w2_in, 32)
                    sp.wait_ge(parts_out, 16)
                    for c in range(CHUNKS):
                        sp.wait_ge(rows_done, 3 * (c + 1))
                        sp.dma_start(table1[c * CB * P:(c + 1) * CB * P, :].rearrange("(b p) c -> p b c", p=P),
                                     feat[:, c * CB:(c + 1) * CB, :]).then_inc(table_out, 16)
                    sp.wait_ge(table_out, 16 * CHUNKS)

                @block.gpsimd
                def _(gp):
                    gp.iota(iota_int[:, :], pattern=[[1, P]], base=0, channel_multiplier=0).then_inc(iota_done, 1)
                    gp.iota(iota_cint[:, :], pattern=[[1, 1]], base=0, channel_multiplier=1).then_inc(iota_done, 1)
                    gp.memset(ident[:, :], 0.0).then_inc(sel_done, 1)
                    gp.wait_ge(sel_done, 1)
                    gp.affine_select(out=ident[:, :], in_=ident[:, :], compare_op=ALU.not_equal, fill=1.0, base=0,
                                     pattern=[[-1, P]], channel_multiplier=1).then_inc(sel_done, 1)
                    gp.memset(eps_col[:, :], EPS).then_inc(sel_done, 1)
                    gp.memset(alpha_bd[:, :], 0.0).then_inc(const_set, 1)
                    for c in range(CHUNKS):
                        blk = slice(c * CB, (c + 1) * CB)
                        gp.wait_ge(mean_done, c + 1)
                        if c >= 3:
                            gp.wait_ge(relu_done, CB * (c - 2))
                        gp.tensor_tensor(centred[:, c % 3], x_rows[:, blk, :], nmean[:, blk].unsqueeze(2).broadcast_to([P, CB, CH]),
                                         ALU.add).then_inc(centred_done, 1)
                    gp.memset(acc[:, :], 0.0).then_inc(zero_done, 1)
                    gp.memset(acc_w[:, :], 0.0).then_inc(zero_done, 1)
                    gp.wait_ge(zero_done, 2)

                @block.scalar
                def _(act):
                    act.dma_start(w0[:, :], a["W"]).then_inc(w_in, 16)
                    act.dma_start(blin_col[:, :], a["b_lin"].rearrange("(c o) -> c o", o=1)).then_inc(w_in, 16)
                    act.dma_start(bias_ext[:, 0:CH], a["b_lin"].partition_broadcast(P)).then_inc(w_in, 16)

                    def square(c):
                        act.wait_ge(centred_done, c + 1)
                        if c >= 2:
                            act.wait_ge(varsum, c - 1)
                        act.activation(squares[:, c % 2], centred[:, c % 3], ACT.Square).then_inc(squared, 1)

                    def root(c):
                        act.wait_ge(varsum, c + 1)
                        act.activation(std[:, c * CB:(c + 1) * CB], sqsum[:, c * CB:(c + 1) * CB], ACT.Sqrt,
                                       bias=eps_col[:, 0:1], scale=1.0 / CH).then_inc(std_done, 1)

                    square(0)
                    act.wait_ge(w_in, 16 * 7)
                    act.wait_ge(sel_done, 3)
                    act.activation(blin_rep[:, :], ident[:, :], ACT.Identity, bias=blin_col[:, 0:1], scale=0.0).then_inc(w_tc, 1)
                    act.wait_ge(w_t, 1)
                    act.copy(w0_t[:, :], bank[0][:, 0:P]).then_inc(w_tc, 1)
                    act.wait_ge(wa_done, 1)
                    act.copy(w0_ext[:, 0:CH], w0[:, :]).then_inc(wa_copied, 1)
                    act.copy(w0_ext[:, CH:CH + HEADS], bank[1][:, 0:HEADS]).then_inc(wa_copied, 1)
                    act.copy(bias_ext[:, CH:CH + HEADS], bank[1][:, 8:8 + HEADS]).then_inc(ba_ready, 1)

                    def normalize(c):
                        act.wait_ge(norm_done, c + 1)
                        if c >= 2:
                            act.wait_ge(turned, c - 1)
                        for b in range(c * CB, (c + 1) * CB):
                            act.activation(normed[:, c % 2, b % CB, :], centred[:, c % 3, b % CB, :], ACT.Relu,
                                           scale=rstd[:, b:b + 1]).then_inc(relu_done, 1)

                    def keep(c):
                        act.wait_ge(turned, c + 1)
                        if c >= 2:
                            act.wait_ge(projected, c - 1)
                        act.copy(feats_t[:, c % 2, 0:4 * P], bank[2][:, :]).then_inc(copied, 1)
                        act.copy(feats_t[:, c % 2, 4 * P:], bank[3][:, 0:3 * P]).then_inc(copied, 1)
                    for s in range(CHUNKS + 1):
                        if s + 1 < CHUNKS:
                            square(s + 1)
                        if s < CHUNKS:
                            root(s)
                            normalize(s)
                        if s >= 1:
                            keep(s - 1)

                @block.vector
                def _(dve):
                    n = [0]

                    def link(ins):
                        n[0] += 1
                        ins.then_inc(chain, 1)
                        dve.wait_ge(chain, n[0])

                    dve.wait_ge(iota_done, 2)
                    link(dve.tensor_copy(iota_row[:, :], iota_int[:, :]))
                    link(dve.tensor_copy(iota_col[:, :], iota_cint[:, :]))
                    def mean(c):
                        blk = slice(c * CB, (c + 1) * CB)
                        dve.wait_ge(x_in[c], 16)
                        link(dve.tensor_reduce(sums[:, blk], x_rows[:, blk, :], AX.X, ALU.add))
                        dve.tensor_scalar(nmean[:, blk], sums[:, blk], -1.0 / CH, None, ALU.mult).then_inc(mean_done, 1)

                    def scale(c):
                        blk = slice(c * CB, (c + 1) * CB)
                        dve.wait_ge(std_done, c + 1)
                        dve.reciprocal(rstd[:, blk], std[:, blk]).then_inc(norm_done, 1)

                    def evacuate(c):
                        if c == 0:
                            dve.wait_ge(ba_ready, 1)
                            dve.wait_ge(w_in, 16 * 7)
                        dve.wait_ge(projected, c + 1)
                        for b0, m, bk in ((0, 3, 4), (3, 3, 5), (6, 1, 6)):
                            ps = bank[bk][:, 0:m * (CH + HEADS)].rearrange("p (m n) -> p m n", m=m)
                            at = slice(c * CB + b0, c * CB + b0 + m)
                            dve.tensor_tensor(feat[:, at, :], ps[:, :, 0:CH],
                                              bias_ext[:, 0:CH].unsqueeze(1).broadcast_to([P, m, CH]), ALU.add).then_inc(rows_done, 1)
                            dve.tensor_tensor(zlogit[:, at, :], ps[:, :, CH:],
                                              bias_ext[:, CH:].unsqueeze(1).broadcast_to([P, m, HEADS]), ALU.add).then_inc(small_sync, 1)
                    def variance(c):
                        dve.wait_ge(squared, c + 1)
                        dve.tensor_reduce(sqsum[:, c * CB:(c + 1) * CB], squares[:, c % 2], AX.X, ALU.add).then_inc(varsum, 1)

                    mean(0)
                    mean(1)
                    dve.wait_ge(idx_in, 16)
                    for j, ins in enumerate((
                            lambda: dve.tensor_scalar(part_int[:, :], src_lin[:, :], P - 1, None, ALU.bitwise_and),
                            lambda: dve.tensor_copy(part_bf[:, 0, :], part_int[:, :]),
                            lambda: dve.tensor_scalar(part_int[:, :], src_lin[:, :], 7, None, ALU.logical_shift_right),
                            lambda: dve.tensor_copy(part_bf[:, 1, :], part_int[:, :]))):
                        ins().then_inc(prep, 1)
                        dve.wait_ge(prep, j + 1)
                    for s in range(CHUNKS + 2):
                        if s < CHUNKS:
                            variance(s)
                        if s + 2 < CHUNKS:
                            mean(s + 2)
                        if s < CHUNKS:
                            scale(s)
                        if s >= 2:
                            evacuate(s - 2)
                    dve.wait_ge(small_sync, 3 * CHUNKS)
                    dve.scalar_tensor_tensor(logit[:, :, :].rearrange("p b h -> p (b h)"), zlogit[:, :, :].rearrange("p b h -> p (b h)"), 0.2,
                                             zlogit[:, :, :].rearrange("p b h -> p (b h)"), ALU.mult, ALU.max).then_inc(small_sync, 1)
                    dve.wait_ge(small_sync, 3 * CHUNKS + 1)

                @block.tensor
                def _(pe):
                    pe.wait_ge(w_in, 16 * 7)
                    pe.wait_ge(sel_done, 3)
                    pe.transpose(bank[0][:, 0:P], w0[:, :], ident[:, :]).then_inc(w_t, 1)
                    pe.wait_ge(w_tc, 2)
                    pe.matmul(bank[1][:, 0:HEADS], w0_t[:, :], alpha_bd[:, :], start=True, stop=True)
                    pe.matmul(bank[1][:, 8:8 + HEADS], blin_rep[:, :], alpha_bd[:, :], start=True, stop=True).then_inc(wa_done, 1)

                    def turn(c):
                        pe.wait_ge(relu_done, CB * (c + 1))
                        if c >= 1:
                            pe.wait_ge(copied, 2 * c)
                        for b in range(CB):
                            last = pe.transpose(bank[2 + b // 4][:, b % 4 * P:(b % 4 + 1) * P], normed[:, c % 2, b, :], ident[:, :])
                        last.then_inc(turned, 1)

                    def project(c):
                        if c == 0:
                            pe.wait_ge(wa_copied, 2)
                        pe.wait_ge(copied, 2 * (c + 1))
                        if c >= 1:
                            pe.wait_ge(small_sync, 3 * c)
                            pe.wait_ge(rows_done, 3 * c)
                        for b in range(CB):
                            o = b % 3 * (CH + HEADS)
                            last = pe.matmul(bank[4 + b // 3][:, o:o + CH + HEADS], feats_t[:, c % 2, b * P:(b + 1) * P],
                                             w0_ext[:, :], start=True, stop=True)
                        last.then_inc(projected, 1)
                    for s in range(CHUNKS + 1):
                        if s < CHUNKS:
                            turn(s)
                        if s >= 1:
                            project(s - 1)

        with ExitStack() as st:
            SR = max(SECTIONS)
            ST = SR * RT
            TB = (ST + P - 1) // P
            lg = sb("lg", [P, SH, ST], st=st)
            run2 = sb("run2", [P, SH, ST], st=st)
            bias_all = sb("bias_all", [P, CH], st=st)
            tab = sb("tab", [P, 3, SH * NB], bf16, st)
            tab_rest = sb("tab_rest", [P, SH * NB], st=st)
            row_block = sb("row_block", [SH * NB, 1], st=st)
            row_head = sb("row_head", [SH * NB, SH], st=st)
            lo_all = sb("lo_all", [P, PAIRS, 2 * GE], bf16, st)
            hi_all = sb("hi_all", [SH * NB, PAIRS, 2 * GE], bf16, st)
            onehot_lo = sb("onehot_lo", [P, 4, GE], bf16, st)
            picked = sb("picked", [SH * NB, 2, GE], st=st)
            edge_logit = sb("edge_logit", [P, ST, SH], st=st)
            edge_w = sb("edge_w", [P, 2, ST, LCOL], st=st)
            stat = sb("stat", [P, 2, TG, LCOL], st=st)
            dn = sb("dn", [P, 3, ST], i32, st)
            ends = sb("ends", [P, ST], st=st)
            pen_f = sb("pen_f", [P, ST], st=st)
            pen_b = sb("pen_b", [P, ST], st=st)
            run = sb("run", [P, SH, ST], st=st)
            cols = sb("cols", [P, 2, 2 * SH], st=st)
            bars = sb("bars", [SH, P], st=st)
            rowc = sb("rowc", [SH, 2, P + 1], st=st)
            carry = sb("carry", [P, 2, SH], st=st)
            blocks_w = sb("blocks_w", [P, 2 * SH, TB, P], st=st)
            turned_l = blocks_w[:, 0:SH, :, :]
            old_new = sb("old_new", [P, 2, 1], st=st)
            old_new_w = sb("old_new_w", [SH, 2, 1], st=st)
            bound = sb("bound", [P, 2], i32, st)
            same = sb("same", [P, 1], st=st)
            factor = sb("factor", [P, 1], st=st)
            factor_w = sb("factor_w", [SH, 1], st=st)

            rel_done = sem("rel_done")
            bias_in, biased = sem("bias_in"), sem("biased")
            look_in = [sem(f"look_in{q}") for q in range(PAIRS)]
            ohl_done, look1, pick_done, look2, logit_done = (sem(n) for n in ("ohl_done", "look1", "pick_done", "look2", "logit_done"))
            oh0, scaled0, stat0, agg0, acc0, accw0 = (sem(n) for n in ("oh0", "scaled0", "stat0", "agg0", "acc0", "accw0"))
            (t_done, t_copied, lin_out, lg_in, dn_in, sc, col_ready, row_turned, row_ready, carry_turned, m_ready, w_exp,
             res_ready, res_out, bl_in, bt_done, bt_copied, old_out, old_in, new_in, delta_ready, factor_done, bound_in) = (
                sem(n) for n in ("t_done", "t_copied", "lin_out", "lg_in", "dn_in", "sc", "col_ready", "row_turned",
                                 "row_ready", "carry_turned", "m_ready", "w_exp", "res_ready", "res_out", "bl_in", "bt_done", "bt_copied",
                                 "old_out", "old_in", "new_in", "delta_ready", "factor_done", "bound_in"))

            def before(j, k, pairs=1):
                k -= 2 * pairs
                return (j, k) if k >= 0 else (j - 1, k + RG)

            early_banks = (4, 5, 2, 3)

            def look_bank(k, early):
                return bank[early_banks[k % 4] if early else 4 + k % 2]

            first_round = [sum(SECTIONS[:n]) for n in range(len(SECTIONS) + 1)]

            def tile_blocks(n):
                tiles = SECTIONS[n] * RT
                return [(t, min(P, tiles - t)) for t in range(0, tiles, P)]

            def looked(n):
                ahead = SECTIONS[n + 1] if n + 1 < len(SECTIONS) else 0
                return ahead // 2, ahead % 2, SECTIONS[n] - ahead // 2 - ahead % 2

            blocks_before = [sum(len(tile_blocks(m)) for m in range(n)) for n in range(len(SECTIONS) + 1)]

            def section_rounds(eng, n, one_round, flush):
                two, one, rest = looked(n)
                i0, a1 = first_round[n], first_round[n + 1]
                b0 = i0 + two + one
                hops = n + 1 < len(SECTIONS)
                assert rest >= 1
                if two:
                    one_round(i0, True, a1, RG, False)
                    if two > 1:
                        with eng.Fori(i0 + 1, i0 + two) as i:
                            one_round(i, False, a1 + (i - i0) * 2, RG, False)
                if one:
                    one_round(i0 + two, two == 0, a1 + two * 2, PAIRS, False)
                if hops:
                    flush(first_round[n + 2] - 1)
                if b0 == i0:
                    one_round(b0, True, None, 0, hops and rest == 1)
                    b0 += 1
                if a1 - hops > b0:
                    with eng.Fori(b0, a1 - hops) as i:
                        one_round(i, False, None, 0, False)
                if hops and a1 - 1 >= b0:
                    one_round(a1 - 1, False, None, 0, True)

            with nc.Block() as block:
                @block.sync
                def _(sp):
                    def load_parts(j, q, first=False):
                        if not first:
                            sp.wait_ge(ohl_done, RG * (j - 1) + 2 * (q + 1))
                            sp.wait_ge(pick_done, RG * (j - 1) + 2 * (q + 1))
                        e0 = (j * RG + 2 * q) * GE
                        sp.dma_start(lo_all[:, q, :], parts_dram[0, ds(e0, 2 * GE)].partition_broadcast(P)).then_inc(look_in[q], 16)
                        sp.dma_start(hi_all[:, q, :], parts_dram[1, ds(e0, 2 * GE)].partition_broadcast(SH * NB)).then_inc(look_in[q], 16)
                    for q in range(PAIRS):
                        load_parts(0, q, True)
                    sp.dma_start(bias_all[:, :], a["bias"].partition_broadcast(P)).then_inc(bias_in, 16)
                    with sp.Fori(1, SECTIONS[0] + 1) as j:
                        for q in range(PAIRS):
                            load_parts(j, q)

                    def look_round(i, look, more):
                        for q in range(PAIRS - 1):
                            load_parts(look + 1, q)
                        load_indices(sp, 0, i + 1, 0, False)
                        load_parts(look + 1, PAIRS - 1)
                        if more:
                            for q in range(PAIRS - 1):
                                load_parts(look + 2, q)
                        load_indices(sp, 0, i + 1, 1, False)
                        if more:
                            load_parts(look + 2, PAIRS - 1)

                    def hop_dmas(n, i):
                        L = SECTIONS[n] * RT
                        e0, e1 = first_round[n] * RT * P, first_round[n + 1] * RT * P
                        lin = lin_dram[:, e0:e1]
                        for j in range(3):
                            sp.dma_start(dn[:, j, 0:L], a["dst_line"][e0 + j:e1 + j].rearrange("(p n) -> p n", p=P)).then_inc(dn_in, 16)
                        for b, (t0, m) in enumerate(tile_blocks(n)):
                            sp.wait_ge(t_copied, blocks_before[n] + b + 1)
                            sp.dma_start(lin[:, t0 * P:(t0 + m) * P].rearrange("h (t p) -> t h p", p=P), turned_l[0:m, :, b, :]).then_inc(lin_out, 16)
                        sp.wait_ge(lin_out, 16 * blocks_before[n + 1])
                        sp.dma_start(lg[:, :, 0:L], lin.rearrange("h (p n) -> p h n", p=P)).then_inc(lg_in, 16)
                        if n:
                            for h in range(SH):
                                sp.dma_start(old_new[h * HC:(h + 1) * HC, 0, :], bound_dram[n, 0, h:h + 1].partition_broadcast(HC)).then_inc(old_in, 16)
                            sp.dma_start(old_new_w[:, 0, :], bound_dram[n, 0, :].rearrange("(h o) -> h o", o=1)).then_inc(old_in, 16)
                            for q in range(2):
                                sp.dma_start(bound[:, q:q + 1], a["dst_line"][e0 + q:e0 + q + 1].partition_broadcast(P)).then_inc(bound_in, 16)
                        if n:
                            load_indices(sp, 0, i + 1, 0, False)
                        sp.wait_ge(m_ready, n + 1)
                        if n:
                            sp.dma_start(bound_dram[n:n + 1, 1, :], run2[0:1, :, 0]).then_inc(old_out, 16)
                        if n + 1 < len(SECTIONS):
                            sp.dma_start(bound_dram[n + 1:n + 2, 0, :], run2[P - 1:P, :, L - 1]).then_inc(old_out, 16)
                        sp.wait_ge(w_exp, n + 1)
                        sp.wait_ge(res_ready, n + 1)
                        sp.dma_start(w_dram[0:SH, e0:e1].rearrange("k (p n) -> p k n", p=P), lg[:, :, 0:L]).then_inc(res_out, 16)
                        sp.dma_start(w_dram[SH:, e0:e1].rearrange("k (p n) -> p k n", p=P), run[:, :, 0:L]).then_inc(res_out, 16)
                        sp.wait_ge(old_out, 16 * (2 * n + (n + 1 < len(SECTIONS))))
                        if n:
                            for h in range(SH):
                                sp.dma_start(old_new[h * HC:(h + 1) * HC, 1, :], bound_dram[n, 1, h:h + 1].partition_broadcast(HC)).then_inc(new_in, 16)
                            sp.dma_start(old_new_w[:, 1, :], bound_dram[n, 1, :].rearrange("(h o) -> h o", o=1)).then_inc(new_in, 16)
                        sp.wait_ge(res_out, 32 * (n + 1))
                        full = L // P
                        if full:
                            for kk in range(2 * SH):
                                sp.dma_start(blocks_w[:, kk, 0:full, :],
                                             w_dram[kk, e0:e0 + full * P * P].rearrange("(b t p) -> t b p", t=P, p=P)).then_inc(bl_in, 16)
                        if L % P:
                            sp.dma_start(blocks_w[0:L % P, :, full, :],
                                         w_dram[:, e0 + full * P * P:e1].rearrange("k (t p) -> t k p", p=P)).then_inc(bl_in, 16)
                        if n:
                            load_indices(sp, 0, i + 1, 1, False)

                    hop_dmas(0, None)
                    for n in range(len(SECTIONS)):
                        two, one, rest = looked(n)
                        a0, a1 = first_round[n], first_round[n + 1]
                        if two:
                            closing = one == 0 and first_round[n + 2] == ROUNDS
                            last = a0 + two - 1
                            if last + (not closing) > a0:
                                with sp.Fori(a0, last + (not closing)) as i:
                                    look_round(i, a1 + (i - a0) * 2, True)
                            if closing:
                                look_round(last, a1 + (last - a0) * 2, False)
                        if one:
                            i = a0 + two
                            if first_round[n + 2] < ROUNDS:
                                look_round(i, first_round[n + 2] - 2, False)
                            else:
                                for h in range(2):
                                    load_indices(sp, 0, i + 1, h, False)
                        b1 = min(a1 - (n + 1 < len(SECTIONS)), ROUNDS - 1)
                        if b1 > a0 + two + one:
                            with sp.Fori(a0 + two + one, b1) as i:
                                for h in range(2):
                                    load_indices(sp, 0, i + 1, h, False)
                        if n + 1 < len(SECTIONS):
                            hop_dmas(n + 1, b1)

                @block.gpsimd
                def _(gp):
                    for k in range(RG):
                        gather(gp, 0, table1, 0, k, True, agg0)
                    with gp.Fori(1, ROUNDS) as i:
                        for k in range(RG):
                            gather(gp, 0, table1, i, k, False, agg0)

                @block.vector
                def _(dve):
                    n_prep = [PREP_PARTS]

                    def link(ins):
                        n_prep[0] += 1
                        ins.then_inc(prep, 1)
                        dve.wait_ge(prep, n_prep[0])
                    link(dve.tensor_copy(tab_rest[:, :].rearrange("p (h b) -> p h b", h=SH), logit[:, :, 0:SH].rearrange("p b h -> p h b")))
                    for part in range(3):
                        link(dve.tensor_copy(tab[:, part], tab_rest[:, :]))
                        if part < 2:
                            link(dve.tensor_tensor(tab_rest[:, :], tab_rest[:, :], tab[:, part], ALU.subtract))
                    R2 = SH * NB
                    link(dve.tensor_scalar(row_head[:, 1:2], iota_col[0:R2, :], float(NB), None, ALU.is_ge))
                    link(dve.tensor_scalar(row_head[:, 0:1], row_head[:, 1:2], -1.0, 1.0, ALU.mult, ALU.add))
                    link(dve.tensor_scalar(row_block[:, :], row_head[:, 1:2], -float(NB), None, ALU.mult))
                    link(dve.tensor_tensor(row_block[:, :], row_block[:, :], iota_col[0:R2, :], ALU.add))
                    link(dve.memset(old_new[:, :, :], 0.0))
                    assert n_prep[0] == PREP_ALL
                    dve.wait_ge(dst_in, 16 * 2)
                    dve.tensor_tensor(dst_rel[:, :], dst_int, first_all, ALU.subtract).then_inc(rel_done, 1)

                    def masks_lo(j, k, first):
                        if k % 2 == 0:
                            dve.wait_ge(look_in[k // 2], 32 * (j + 1))
                        if not (first and k < 4):
                            dve.wait_ge(look1, j * RG + k - 3)
                        dve.tensor_scalar(onehot_lo[:, k % 4], lo_all[:, k // 2, k % 2 * GE:(k % 2 + 1) * GE],
                                          iota_col[:, 0:1], None, ALU.is_equal).then_inc(ohl_done, 1)

                    def pick(j, k, first, early=False):
                        dve.wait_ge(look1, j * RG + k + 1)
                        if not (first and k < 2):
                            dve.wait_ge(look2, j * RG + k - 1)
                        dve.scalar_tensor_tensor(picked[:, k % 2], hi_all[:, k // 2, k % 2 * GE:(k % 2 + 1) * GE],
                                                 row_block[:, 0:1], look_bank(k, early)[0:SH * NB, :], ALU.is_equal, ALU.mult).then_inc(pick_done, 1)

                    def pick_pair(j, k, first=False, early=False):
                        for q in range(2):
                            pick(j, k + q, first, early)

                    def lookup(j, k, opening, first=False, early=False):
                        for q in range(2):
                            masks_lo(j, k + q, first)
                        if not opening:
                            pick_pair(*before(j, k), first and k == 2, early)

                    for k in range(0, RG, 2):
                        lookup(0, k, k == 0, True, True)
                    if SECTIONS[0] > 1:
                        with dve.Fori(1, SECTIONS[0]) as j:
                            for k in range(0, RG, 2):
                                lookup(j, k, False, False, True)
                    pick_pair(SECTIONS[0] - 1, RG - 2, False, True)

                    n_sc = [0]

                    def hop(ins):
                        n_sc[0] += 1
                        ins.then_inc(sc, 1)
                        dve.wait_ge(sc, n_sc[0])

                    def scan_hops(n):
                        L = SECTIONS[n] * RT
                        pf, pb, en = pen_f[:, 0:L], pen_b[:, 0:L], ends[:, 0:L]

                        def prepare():
                            dve.wait_ge(dn_in, 16 * 3 * (n + 1))
                            hop(dve.tensor_tensor(pf, dn[:, 0, 0:L], dn[:, 1, 0:L], ALU.not_equal))
                            hop(dve.tensor_tensor(en, dn[:, 2, 0:L], dn[:, 1, 0:L], ALU.not_equal))
                            hop(dve.tensor_scalar(pf, pf, -BIG, None, ALU.mult))
                            hop(dve.tensor_scalar(pb, en, -BIG, None, ALU.mult))
                            for way, pen in enumerate((pf, pb)):
                                hop(dve.tensor_reduce(cols[:, way, SH:SH + 1], pen, AX.X, ALU.min))
                                hop(dve.tensor_copy(cols[:, way, SH + 1:], cols[:, way, SH:SH + 1]))
                            hop(dve.memset(rowc[:, :, :], -BIG))

                        def line(v, way):
                            return v[:, ::-1] if way else v

                        def within(way):
                            pen, src = ((pf, lg), (pb, run))[way]
                            if way == 0:
                                dve.wait_ge(lg_in, 16 * (n + 1))
                            for h in range(SH):
                                hop(dve.tensor_tensor_scan(line(run2[:, h, 0:L], way), line(pen, way), line(src[:, h, 0:L], way), -BIG, ALU.add, ALU.max))
                            end = 0 if way else L - 1
                            hop(dve.tensor_copy(cols[:, way, 0:SH], run2[:, :, end:end + 1].rearrange("p h o -> p (h o)")))
                            dve.engine_nop().then_inc(col_ready, 1)

                        def across(way):
                            if n and way == 0:
                                dve.wait_ge(old_in, OLD_IN * n)
                                hop(dve.tensor_copy(rowc[:, 0, 0:1], old_new_w[:, 0, :]))
                            dve.wait_ge(row_turned, 2 * n + way + 1)
                            o = rowc[:, way, 0:P] if way else rowc[:, way, 1:P + 1]
                            start = -BIG if way else rowc[:, 0, 0:1]
                            hop(dve.tensor_copy(bars[:, :], bank[4 + way][0:SH, P:2 * P]))
                            hop(dve.tensor_tensor_scan(line(o, way), line(bars[:, :], way), line(bank[4 + way][0:SH, 0:P], way), start,
                                                       ALU.add, ALU.max))
                            dve.engine_nop().then_inc(row_ready, 1)

                        def whole(way):
                            pen, src, dst = ((pf, lg, run), (pb, run, run2))[way]
                            dve.wait_ge(carry_turned, 2 * n + way + 1)
                            hop(dve.tensor_copy(carry[:, way], bank[4 + way][:, 2 * P:2 * P + SH]))
                            for h in range(SH):
                                hop(dve.tensor_tensor_scan(line(dst[:, h, 0:L], way), line(pen, way), line(src[:, h, 0:L], way),
                                                           carry[:, way, h:h + 1], ALU.add, ALU.max))

                        def turn_back():
                            whole(0)
                            within(1)

                        def finish():
                            whole(1)
                            hop(dve.tensor_tensor(lg[:, :, 0:L], lg[:, :, 0:L], run2[:, :, 0:L], ALU.subtract))
                            dve.engine_nop().then_inc(m_ready, 1)
                            dve.tensor_tensor(run[:, :, 0:L], run2[:, :, 0:L], en.unsqueeze(1).broadcast_to([P, SH, L]), ALU.mult).then_inc(res_ready, 1)

                        def deltas():
                            if n:
                                dve.wait_ge(bound_in, 16 * 2 * n)
                                dve.wait_ge(new_in, NEW_IN * n)
                                hop(dve.tensor_tensor(same[:, :], bound[:, 0:1], bound[:, 1:2], ALU.is_equal))
                                hop(dve.tensor_tensor(factor[:, :], old_new[:, 0, :], old_new[:, 1, :], ALU.subtract))
                                hop(dve.tensor_tensor(factor_w[:, :], old_new_w[:, 0, :], old_new_w[:, 1, :], ALU.subtract))
                                hop(dve.tensor_tensor(factor[:, :], factor[:, :], same[:, :], ALU.mult))
                                hop(dve.tensor_tensor(factor_w[:, :], factor_w[:, :], same[0:SH, :], ALU.mult))
                                dve.engine_nop().then_inc(delta_ready, 1)

                        return [prepare, lambda: within(0), lambda: across(0), turn_back, lambda: across(1), finish, None, deltas]

                    def rescale(n):
                        dve.wait_ge(factor_done, 2 * n)
                        dve.load([edge_reg], bound[0:1, 0:1])
                        v = dve.snap(edge_reg, min_val=0, max_val=N)
                        hop(dve.tensor_scalar(acc[:, ds(v, 1)], acc[:, ds(v, 1)], factor[:, 0:1], None, ALU.mult))
                        hop(dve.tensor_scalar(acc_w[0:SH, ds(v, 1)], acc_w[0:SH, ds(v, 1)], factor_w[:, 0:1], None, ALU.mult))

                    regs = [dve.alloc_register(f"first0_{q}") for q in range(HALF * TG)]
                    edge_reg = dve.alloc_register("boundary")

                    def masks(i, k):
                        if not (isinstance(i, int) and i * RG + k < 2):
                            dve.wait_ge(agg0, i * RG + k - 1)
                        for t in range(TG):
                            dve.tensor_scalar(onehot[:, k % 2, t, :], iota_row[:, :], dst_rel[:, ds(i * RT + k * TG + t, 1)], None,
                                              ALU.is_equal).then_inc(oh0, 1)

                    def add(i, k, at):
                        dve.wait_ge(agg0, i * RG + k + 1)
                        for t in range(TG):
                            v = at[t]
                            if not (k == 0 and t == 0 and isinstance(i, int) and i == 0):
                                dve.wait_ge(acc0, (i * RG + k) * TG + t)
                            dve.tensor_tensor(acc[:, ds(v, P)], acc[:, ds(v, P)], bank[k % 2][:, t * P:(t + 1) * P], ALU.add).then_inc(acc0, 1)
                            if not (k == 0 and t == 0 and isinstance(i, int) and i == 0):
                                dve.wait_ge(accw0, (i * RG + k) * TG + t)
                            dve.tensor_tensor(acc_w[:, ds(v, P)], acc_w[:, ds(v, P)], bank[2 + k % 2][0:LCOL, t * P:(t + 1) * P],
                                              ALU.add).then_inc(accw0, 1)

                    at = [None]
                    for n in range(len(SECTIONS)):
                        if n:
                            rescale(n)
                            if n + 1 == len(SECTIONS):
                                dve.wait_ge(bias_in, 16)
                                dve.tensor_tensor(x_rows[:, :, :], x_rows[:, :, :], bias_all[:, :].unsqueeze(1).broadcast_to([P, NB, CH]),
                                                  ALU.add).then_inc(biased, 1)
                        else:
                            hop(dve.memset(edge_w[:, :, :, SH:SH + 1], 1.0))
                            for one in scan_hops(0):
                                if one:
                                    one()
                            dve.wait_ge(rel_done, 1)

                        def one_round(i, first, look, pairs, hops):
                            steps = scan_hops(n + 1) if hops else [None] * RG
                            if not (isinstance(i, int) and first):
                                at[0] = [dve.snap(r, min_val=0, max_val=N) for r in regs]
                            for k in range(RG):
                                if k < pairs:
                                    lookup(look + k // HALF, k % HALF * 2, first and k == 0)
                                masks(i, k)
                                if k:
                                    add(i, k - 1, at[0][(k - 1) % HALF * TG:])
                                elif not first:
                                    add(i - 1, RG - 1, at[0][-TG:])
                                if k % HALF == 0:
                                    at[0] = first_nodes(dve, regs, i, k // HALF)
                                if steps[k]:
                                    steps[k]()
                        section_rounds(dve, n, one_round, lambda j: pick_pair(j, RG - 2))
                        add(first_round[n + 1] - 1, RG - 1, [dve.snap(r, min_val=0, max_val=N) for r in regs][-TG:])
                        dve.wait_ge(acc0, first_round[n + 1] * RT)
                        dve.wait_ge(accw0, first_round[n + 1] * RT)
                    dve.wait_ge(biased, 1)

                @block.tensor
                def _(pe):
                    pe.wait_ge(prep, PREP_ALL)

                    def look_first(j, k, first, early):
                        pe.wait_ge(ohl_done, j * RG + k + 1)
                        back = 4 if early else 2
                        if not (first and k < back):
                            pe.wait_ge(pick_done, j * RG + k + 1 - back)
                        for part in range(3):
                            last = pe.matmul(look_bank(k, early)[0:SH * NB, :], tab[:, part], onehot_lo[:, k % 4], start=(part == 0), stop=(part == 2))
                        last.then_inc(look1, 1)

                    def look_second(j, k, first):
                        pe.wait_ge(pick_done, j * RG + k + 1)
                        if not (first and k < 2):
                            pe.wait_ge(logit_done, j * RG + k - 1)
                        for t in range(TG):
                            last = pe.matmul(bank[6 + k % 2][:, t * SH:(t + 1) * SH], picked[:, k % 2, t * P:(t + 1) * P], row_head[:, :],
                                             start=True, stop=True)
                        last.then_inc(look2, 1)

                    def second_pair(j, k, first=False):
                        for q in range(2):
                            look_second(j, k + q, first)

                    def lookup(j, k, opening, first=False, early=False):
                        for q in range(2):
                            look_first(j, k + q, first, early)
                        if not opening:
                            second_pair(*before(j, k), first and k == 2)

                    for k in range(0, RG, 2):
                        lookup(0, k, k == 0, True, True)
                    if SECTIONS[0] > 1:
                        with pe.Fori(1, SECTIONS[0]) as j:
                            for k in range(0, RG, 2):
                                lookup(j, k, False, False, True)
                    second_pair(SECTIONS[0] - 1, RG - 2)

                    def aggregate(i, k):
                        pe.wait_ge(oh0, (i * RG + k + 1) * TG)
                        pe.wait_ge(scaled0, (i * RG + k + 1) * TG * SH)
                        pe.wait_ge(stat0, i * RG + k + 1)
                        if not (isinstance(i, int) and i * RG + k < 2):
                            pe.wait_ge(acc0, (i * RG + k - 1) * TG)
                            pe.wait_ge(accw0, (i * RG + k - 1) * TG)
                        for t in range(TG):
                            pe.matmul(bank[k % 2][:, t * P:(t + 1) * P], rows[:, k, t, :], onehot[:, k % 2, t, :], start=True, stop=True)
                            last = pe.matmul(bank[2 + k % 2][0:LCOL, t * P:(t + 1) * P], stat[:, k % 2, t, :], onehot[:, k % 2, t, :],
                                             start=True, stop=True)
                        last.then_inc(agg0, 1)

                    def turn_logits(n):
                        pe.wait_ge(logit_done, first_round[n + 1] * RG)
                        for b, (t0, m) in enumerate(tile_blocks(n)):
                            if b >= 2:
                                pe.wait_ge(t_copied, blocks_before[n] + b - 1)
                            for h in range(SH):
                                last = pe.transpose(bank[6 + b % 2][0:m, h * P:(h + 1) * P], edge_logit[:, t0:t0 + m, h], ident[:, :])
                            last.then_inc(t_done, 1)

                    def turn_weights(n):
                        pe.wait_ge(bl_in, sum(bl_count(m) for m in range(n + 1)))
                        for b, (t0, m) in enumerate(tile_blocks(n)):
                            if b >= 2:
                                pe.wait_ge(bt_copied, 2 * (blocks_before[n] + b - 1))
                            for kk in range(2 * SH):
                                last = pe.transpose(bank[4 + b % 2][:, kk * P:kk * P + m], blocks_w[0:m, kk, b, :], ident[0:m, 0:m])
                            last.then_inc(bt_done, 1)

                    def turn_cols(n, way):
                        pe.wait_ge(col_ready, 2 * n + way + 1)
                        pe.transpose(bank[4 + way][0:SH, 0:P], cols[:, way, 0:SH], ident[:, :])
                        pe.transpose(bank[4 + way][0:SH, P:2 * P], cols[:, way, SH:], ident[:, :]).then_inc(row_turned, 1)

                    def turn_carry(n, way):
                        pe.wait_ge(row_ready, 2 * n + way + 1)
                        pe.transpose(bank[4 + way][:, 2 * P:2 * P + SH], rowc[:, way, way:way + P], ident[0:SH, 0:SH]).then_inc(carry_turned, 1)

                    def pe_hops(n):
                        return [lambda: turn_logits(n), lambda: turn_cols(n, 0), lambda: turn_carry(n, 0), lambda: turn_cols(n, 1),
                                lambda: turn_carry(n, 1), None, None, lambda: turn_weights(n)]

                    for one in pe_hops(0):
                        if one:
                            one()
                    for n in range(len(SECTIONS)):
                        pe.wait_ge(bt_copied, 2 * blocks_before[n + 1])

                        def one_round(i, first, look, pairs, hops):
                            for k in range(RG):
                                if k < pairs:
                                    lookup(look + k // HALF, k % HALF * 2, first and k == 0)
                                aggregate(i, k)
                                if hops and pe_hops(n + 1)[k]:
                                    pe_hops(n + 1)[k]()
                        section_rounds(pe, n, one_round, lambda j: second_pair(j, RG - 2))

                @block.scalar
                def _(act):
                    def keep(j, k):
                        act.wait_ge(look2, j * RG + k + 1)
                        act.copy(edge_logit[:, ds((j * RG + k) * TG - keep.base, TG), :].rearrange("p t h -> p (t h)"),
                                 bank[6 + k % 2][:, 0:TG * SH]).then_inc(logit_done, 1)

                    def keep_pair(j, k):
                        for q in range(2):
                            keep(j, k + q)

                    keep.base = 0
                    with act.Fori(0, SECTIONS[0]) as j:
                        for k in range(0, RG, 2):
                            keep_pair(j, k)

                    def rows_out(n):
                        for b, (t0, m) in enumerate(tile_blocks(n)):
                            act.wait_ge(t_done, blocks_before[n] + b + 1)
                            act.copy(turned_l[0:m, :, b, :], bank[6 + b % 2][0:m, 0:SH * P].rearrange("p (h n) -> p h n", h=SH)).then_inc(t_copied, 1)

                    def exps(n):
                        L = SECTIONS[n] * RT
                        act.wait_ge(m_ready, n + 1)
                        act.activation(lg[:, :, 0:L], lg[:, :, 0:L], ACT.Exp).then_inc(w_exp, 1)

                    def columns_in(n):
                        for b, (t0, m) in enumerate(tile_blocks(n)):
                            act.wait_ge(bt_done, blocks_before[n] + b + 1)
                            ps = bank[4 + b % 2][:, :].rearrange("p (k n) -> p n k", k=2 * SH)
                            act.copy(edge_w[:, n % 2, t0:t0 + m, 0:SH], ps[:, 0:m, 0:SH]).then_inc(bt_copied, 1)
                            act.copy(edge_w[:, n % 2, t0:t0 + m, SH + 1:], ps[:, 0:m, SH:]).then_inc(bt_copied, 1)
                        if n:
                            act.wait_ge(delta_ready, n)
                            act.activation(factor[:, :], factor[:, :], ACT.Exp).then_inc(factor_done, 1)
                            act.activation(factor_w[:, :], factor_w[:, :], ACT.Exp).then_inc(factor_done, 1)

                    def weigh(i, k, n):
                        if not (isinstance(i, int) and i * RG + k < 2):
                            act.wait_ge(agg0, i * RG + k - 1)
                        act.copy(stat[:, k % 2].rearrange("p t c -> p (t c)"),
                                 edge_w[:, n % 2, ds((i - first_round[n]) * RT + k * TG, TG), :].rearrange("p t c -> p (t c)")).then_inc(stat0, 1)
                        act.wait_ge(gathered[0][k], 16 * TG * (i + 1))
                        act.wait_ge(stat0, i * RG + k + 1)
                        for t in range(TG):
                            for h in range(SH):
                                act.activation(rows[:, k, t, h * HC:(h + 1) * HC], rows[:, k, t, h * HC:(h + 1) * HC], ACT.Copy,
                                               scale=stat[:, k % 2, t, h:h + 1]).then_inc(scaled0, 1)

                    rows_out(0)
                    exps(0)
                    columns_in(0)
                    for n in range(len(SECTIONS)):
                        act.wait_ge(bt_copied, 2 * blocks_before[n + 1])
                        keep.base = first_round[n + 1] * RT

                        def one_round(i, first, look, pairs, hops):
                            for k in range(RG):
                                if k < pairs and not (first and k < 2):
                                    keep_pair(*before(look + k // HALF, k % HALF * 2, 2))
                                weigh(i, k, n)
                                if hops and k == 0:
                                    rows_out(n + 1)
                                if hops and k == RG - 2:
                                    exps(n + 1)
                                if hops and k == RG - 1:
                                    columns_in(n + 1)

                        def flush(j):
                            keep_pair(j, RG - 4)
                            keep_pair(j, RG - 2)
                        section_rounds(act, n, one_round, flush)

        with ExitStack() as st:
            sums_t = sb("sums_t", [P, NB, LCOL], st=st)
            top = sb("top", [P, NB, HEADS], st=st)
            seg = sb("seg", [P, NB, HEADS], st=st)
            den = sb("den", [P, NB, HEADS], st=st)
            ca = sb("ca", [P, NB, HEADS], st=st)
            cb = sb("cb", [P, NB, HEADS], st=st)
            bn1_all = sb("bn1_all", [P, CH], st=st)
            wn1a = sb("wn1a", [P, CH], st=st)
            part = sb("part", [P, 2, CB, CH], st=st)
            squares1 = sb("squares1", [P, 2, CB, CH], st=st)
            turned1 = sb("turned1", [P, 2, CB * P], st=st)
            proj = sb("proj", [P, 2, CB, CH], st=st)
            total1 = sb("total1", [P, NB], st=st)
            nmean1 = sb("nmean1", [P, NB], st=st)
            sqsum1 = sb("sqsum1", [P, NB], st=st)
            std1 = sb("std1", [P, NB], st=st)
            rstd1 = sb("rstd1", [P, NB], st=st)
            shift1 = sb("shift1", [P, NB], st=st)
            (b_in, sw_t, b_chain, e_in, e_done, s_t, comb, cb_ready, owned, own, cleared, sums_kept, mean1, squared1, varsum1, std_done1, norm1, hrelu1, turned1_s,
             relu1_s, proj1, rows1, table1_out) = (
                sem(n) for n in ("b_in", "sw_t", "b_chain", "e_in", "e_done", "s_t", "comb", "cb_ready", "owned", "own", "cleared", "sums_kept", "mean1",
                                 "squared1", "varsum1", "std_done1", "norm1", "hrelu1", "turned1_s", "relu1_s", "proj1", "rows1", "table1_out"))

            def heads(v):
                return v.rearrange("p b (h c) -> p b h c", h=HEADS)

            def per_head(v, b0, m):
                return v[:, b0:b0 + m, :].unsqueeze(3).broadcast_to([P, m, HEADS, HC])

            def blocks(c):
                return slice(c * CB, (c + 1) * CB)

            with nc.Block() as block:
                @block.sync
                def _(sp):
                    sp.dma_start(bn1_all[:, :], a["bn1"].partition_broadcast(P)).then_inc(b_in, 16)
                    sp.dma_start(wn1a[:, :], a["Wn1"][0:CH, :]).then_inc(b_in, 16)
                    for h in range(2):
                        load_indices(sp, 1, 0, h, True)
                    for c in range(CHUNKS):
                        sp.wait_ge(rows1, 2 * (c + 1))
                        sp.dma_start(table2[c * CB * P:(c + 1) * CB * P, :].rearrange("(b p) c -> p b c", p=P), proj[:, c % 2]).then_inc(table1_out, 16)
                        sp.wait_ge(table1_out, 16 * (c + 1))

                @block.gpsimd
                def _(gp):
                    gp.wait_ge(cb_ready, 1)
                    for c in range(CHUNKS):
                        gp.tensor_tensor(heads(feat[:, blocks(c), :]), heads(feat[:, blocks(c), :]), per_head(cb, c * CB, CB),
                                         ALU.mult).then_inc(owned, 1)
                        gp.wait_ge(owned, c + 1)
                        gp.tensor_tensor(x_rows[:, blocks(c), :], x_rows[:, blocks(c), :], feat[:, blocks(c), :], ALU.add).then_inc(own, 1)
                    gp.wait_ge(s_t, CHUNKS)
                    gp.memset(acc[:, :], 0.0).then_inc(cleared, 1)
                    for c in range(CHUNKS):
                        gp.wait_ge(hrelu1, CB * (c + 1))
                        gp.tensor_tensor(x_rows[:, blocks(c), :], x_rows[:, blocks(c), :], feat[:, blocks(c), :], ALU.add).then_inc(cleared, 1)
                    gp.wait_ge(cleared, 1 + CHUNKS)

                @block.tensor
                def _(pe):
                    for b in range(NB):
                        last = pe.transpose(bank[7][:, b * LCOL:(b + 1) * LCOL], acc_w[:, b * P:(b + 1) * P], ident[0:LCOL, 0:LCOL])
                    last.then_inc(sw_t, 1)

                    def turn_sums(c):
                        if c == 1:
                            pe.wait_ge(sums_kept, 1)
                        if c >= 2:
                            pe.wait_ge(comb, c - 1)
                        for b in range(CB):
                            last = pe.transpose(bank[c % 2 * 6 + b // 4][:, b % 4 * P:(b % 4 + 1) * P], acc[:, (c * CB + b) * P:(c * CB + b + 1) * P], ident[:, :])
                        last.then_inc(s_t, 1)

                    def turn(c):
                        pe.wait_ge(hrelu1, CB * (c + 1))
                        if c >= 1:
                            pe.wait_ge(relu1_s, 2 * c)
                        for b in range(CB):
                            last = pe.transpose(bank[2 + b // 4][:, b % 4 * P:(b % 4 + 1) * P], feat[:, c * CB + b, :], ident[:, :])
                        last.then_inc(turned1_s, 1)

                    def project(c):
                        pe.wait_ge(relu1_s, 2 * (c + 1))
                        pe.wait_ge(b_in, 16 * 2)
                        if c >= 1:
                            pe.wait_ge(rows1, 2 * c)
                        for b in range(CB):
                            ps = bank[4 + b // 4][:, b % 4 * P:(b % 4 + 1) * P]
                            last = pe.matmul(ps, turned1[:, c % 2, b * P:(b + 1) * P], wn1a[:, :], start=True, stop=True)
                        last.then_inc(proj1, 1)
                    turn_sums(0)
                    turn_sums(1)
                    turn_sums(2)
                    for s in range(CHUNKS + 1):
                        if s + 3 < CHUNKS:
                            turn_sums(s + 3)
                        if s >= 1:
                            project(s - 1)
                        if s < CHUNKS:
                            turn(s)

                @block.vector
                def _(dve):
                    n = [0]

                    def link(ins):
                        n[0] += 1
                        ins.then_inc(b_chain, 1)
                        dve.wait_ge(b_chain, n[0])
                    dve.wait_ge(sw_t, 1)
                    link(dve.tensor_copy(sums_t[:, :, :].rearrange("p b c -> p (b c)"), bank[7][:, 0:NB * LCOL]))
                    dve.engine_nop().then_inc(sums_kept, 1)
                    link(dve.tensor_copy(count[:, :], sums_t[:, :, SH:SH + 1].rearrange("p b o -> p (b o)")))
                    link(dve.tensor_copy(seg[:, :, 0:SH], sums_t[:, :, SH + 1:]))
                    link(dve.tensor_copy(seg[:, :, SH:], logit[:, :, SH:]))
                    link(dve.tensor_tensor(top[:, :, :], seg[:, :, :], logit[:, :, :], ALU.max))
                    link(dve.tensor_tensor(seg[:, :, :], seg[:, :, :], top[:, :, :], ALU.subtract))
                    link(dve.tensor_tensor(cb[:, :, :], logit[:, :, :], top[:, :, :], ALU.subtract))
                    dve.engine_nop().then_inc(e_in, 1)
                    dve.wait_ge(e_done, 2)
                    link(dve.tensor_tensor(den[:, :, 0:SH], sums_t[:, :, 0:SH], ca[:, :, 0:SH], ALU.mult))
                    link(dve.tensor_tensor(den[:, :, SH:], sums_t[:, :, SH:SH + 1].broadcast_to([P, NB, SH]), ca[:, :, SH:], ALU.mult))
                    link(dve.tensor_tensor(den[:, :, :], den[:, :, :], cb[:, :, :], ALU.add))
                    link(dve.reciprocal(den[:, :, :], den[:, :, :]))
                    link(dve.tensor_tensor(cb[:, :, :], cb[:, :, :], den[:, :, :], ALU.mult))
                    dve.engine_nop().then_inc(cb_ready, 1)
                    link(dve.tensor_tensor(ca[:, :, :], ca[:, :, :], den[:, :, :], ALU.mult))
                    dve.wait_ge(b_in, 16 * 2)

                    def combine(c):
                        blk = blocks(c)
                        dve.wait_ge(s_t, c + 1)
                        for j, (b0, m) in enumerate(((0, 4), (4, 3))):
                            link(dve.tensor_tensor(heads(part[:, c % 2, b0:b0 + m]), heads(bank[c % 2 * 6 + j][:, 0:m * P].rearrange("p (m c) -> p m c", m=m)),
                                                   per_head(ca, c * CB + b0, m), ALU.mult))
                        dve.engine_nop().then_inc(comb, 1)
                        dve.wait_ge(own, c + 1)
                        link(dve.tensor_tensor(x_rows[:, blk, :], x_rows[:, blk, :], part[:, c % 2], ALU.add))
                        link(dve.tensor_reduce(total1[:, blk], x_rows[:, blk, :], AX.X, ALU.add))
                        dve.tensor_scalar(nmean1[:, blk], total1[:, blk], -1.0 / CH, None, ALU.mult).then_inc(mean1, 1)

                    def scale(c):
                        blk = blocks(c)
                        dve.wait_ge(std_done1, c + 1)
                        link(dve.reciprocal(rstd1[:, blk], std1[:, blk]))
                        dve.wait_ge(mean1, c + 1)
                        dve.tensor_tensor(shift1[:, blk], nmean1[:, blk], rstd1[:, blk], ALU.mult).then_inc(norm1, 1)

                    def evacuate(c):
                        dve.wait_ge(proj1, c + 1)
                        if c >= 2:
                            dve.wait_ge(table1_out, 16 * (c - 1))
                        for j, (b0, m) in enumerate(((0, 4), (4, 3))):
                            dve.tensor_tensor(proj[:, c % 2, b0:b0 + m], bank[4 + j][:, 0:m * P].rearrange("p (m c) -> p m c", m=m),
                                              bn1_all[:, :].unsqueeze(1).broadcast_to([P, m, CH]), ALU.add).then_inc(rows1, 1)

                    def variance(c):
                        dve.wait_ge(squared1, CB * (c + 1))
                        dve.tensor_reduce(sqsum1[:, blocks(c)], squares1[:, c % 2], AX.X, ALU.add).then_inc(varsum1, 1)

                    combine(0)
                    combine(1)
                    for s in range(CHUNKS + 2):
                        if s < CHUNKS:
                            variance(s)
                        if s + 2 < CHUNKS:
                            combine(s + 2)
                        if s < CHUNKS:
                            scale(s)
                        if s >= 2:
                            evacuate(s - 2)

                @block.scalar
                def _(act):
                    act.wait_ge(e_in, 1)
                    act.activation(cb[:, :, :], cb[:, :, :], ACT.Exp).then_inc(e_done, 1)
                    act.activation(ca[:, :, :], seg[:, :, :], ACT.Exp).then_inc(e_done, 1)

                    def square(c):
                        act.wait_ge(mean1, c + 1)
                        if c >= 2:
                            act.wait_ge(varsum1, c - 1)
                        for b in range(c * CB, (c + 1) * CB):
                            act.activation(squares1[:, c % 2, b % CB, :], x_rows[:, b, :], ACT.Square, bias=nmean1[:, b:b + 1]).then_inc(squared1, 1)

                    def root(c):
                        act.wait_ge(varsum1, c + 1)
                        act.activation(std1[:, blocks(c)], sqsum1[:, blocks(c)], ACT.Sqrt, bias=eps_col[:, 0:1], scale=1.0 / CH).then_inc(std_done1, 1)

                    def normalize(c):
                        act.wait_ge(norm1, c + 1)
                        for b in range(c * CB, (c + 1) * CB):
                            act.activation(feat[:, b, :], x_rows[:, b, :], ACT.Relu, scale=rstd1[:, b:b + 1],
                                           bias=shift1[:, b:b + 1]).then_inc(hrelu1, 1)

                    def keep(c):
                        act.wait_ge(turned1_s, c + 1)
                        if c >= 2:
                            act.wait_ge(proj1, c - 1)
                        act.copy(turned1[:, c % 2, 0:4 * P], bank[2][:, :]).then_inc(relu1_s, 1)
                        act.copy(turned1[:, c % 2, 4 * P:], bank[3][:, 0:3 * P]).then_inc(relu1_s, 1)
                    square(0)
                    for s in range(CHUNKS + 2):
                        if s + 1 < CHUNKS:
                            square(s + 1)
                        if s >= 1 and s - 1 < CHUNKS:
                            keep(s - 1)
                        if s < CHUNKS:
                            root(s)
                        if s < CHUNKS:
                            normalize(s)

        with ExitStack() as st:
            we1 = sb("we1", [EC, CH], st=st)
            we2 = sb("we2", [P, CH], st=st)
            wn1b = sb("wn1b", [P, CH], st=st)
            be1 = sb("be1", [P, 1], st=st)
            be2 = sb("be2", [P, 1], st=st)
            wt = sb("wt", [P, 1], st=st)
            bt = sb("bt", [P, 1], st=st)
            ea = sb("ea", [EC, 2, HALF * GE], st=st)
            ts = sb("ts", [P, 2, HALF * GE], st=st)
            hidden = sb("hidden", [P, 2, GE], st=st)
            gate = sb("gate", [P, 2, GE], st=st)
            ef = sb("ef", [P, 2, GE], st=st)
            pre = sb("pre", [P, 2, TG, P], st=st)
            msg = sb("msg", [P, 2, TG, P], st=st)
            w1_in, base1, oh1, h1, r1, h2, gt, efd, z1, radd, r2, agg1, acc1 = (
                sem(n) for n in ("w1_in", "base1", "oh1", "h1", "r1", "h2", "gt", "efd", "z1", "radd", "r2", "agg1", "acc1"))
            ea_in = [sem(f"ea_in{h}") for h in range(2)]
            ts_in = [sem(f"ts_in{h}") for h in range(2)]
            with nc.Block() as block:
                @block.sync
                def _(sp):
                    sp.dma_start(we1[:, :], a["We1"]).then_inc(w1_in, 16)
                    sp.dma_start(we2[:, :], a["We2"]).then_inc(w1_in, 16)
                    sp.dma_start(wn1b[:, :], a["Wn1"][CH:, :]).then_inc(w1_in, 16)
                    for col, name in ((be1, "be1"), (be2, "be2"), (bt, "bt")):
                        sp.dma_start(col[:, :], a[name].rearrange("(c o) -> c o", o=1)).then_inc(w1_in, 16)
                    sp.dma_start(wt[:, :], a["Wt"].rearrange("o c -> c o")).then_inc(w1_in, 16)

                    def load(i, first):
                        for h in range(2):
                            if not first:
                                load_indices(sp, 1, i, h, False)
                            e0 = (i * RG + h * HALF) * GE
                            if not first:
                                sp.wait_ge(h1, RG * (i - 1) + HALF * (h + 1))
                                sp.wait_ge(gt, RG * (i - 1) + HALF * (h + 1))
                            sp.dma_start(ea[:, h, :], a["ea_t"][:, ds(e0, HALF * GE)]).then_inc(ea_in[h], 16)
                            sp.dma_start(ts[:, h, :], a["ts"][ds(e0, HALF * GE)].partition_broadcast(P)).then_inc(ts_in[h], 16)
                    load(0, True)
                    with sp.Fori(1, ROUNDS) as i:
                        load(i, False)

                @block.gpsimd
                def _(gp):
                    for k in range(RG):
                        gather(gp, 1, table2, 0, k, True, radd)
                    with gp.Fori(1, ROUNDS) as i:
                        for k in range(RG):
                            gather(gp, 1, table2, i, k, False, radd)

                def skewed(eng, parts):
                    def steps(i, first):
                        for k in range(RG):
                            for lag, part_of in parts:
                                if k >= lag:
                                    part_of(i, k - lag, first)
                                elif not first:
                                    part_of(i - 1, k - lag + RG, False)
                    steps(0, True)
                    with eng.Fori(1, ROUNDS) as i:
                        steps(i, False)
                    for k in range(3):
                        for lag, part_of in parts:
                            if k < lag:
                                part_of(ROUNDS - 1, k - lag + RG, False)

                @block.tensor
                def _(pe):
                    pe.wait_ge(w1_in, 16 * 7)

                    def first_product(i, k, first):
                        if k % HALF == 0:
                            pe.wait_ge(ea_in[k // HALF], 16 * (i + 1))
                        if not (first and k < 2):
                            pe.wait_ge(r1, i * RG + k - 1)
                        pe.matmul(bank[k % 2][:, :], we1[:, :], ea[:, k // HALF, k % HALF * GE:(k % HALF + 1) * GE], start=True, stop=True).then_inc(h1, 1)

                    def second_product(i, k, first):
                        pe.wait_ge(r1, i * RG + k + 1)
                        if not (first and k < 2):
                            pe.wait_ge(efd, i * RG + k - 1)
                        pe.matmul(bank[2 + k % 2][:, :], we2[:, :], hidden[:, k % 2], start=True, stop=True).then_inc(h2, 1)

                    def third_product(i, k, first):
                        pe.wait_ge(efd, i * RG + k + 1)
                        if not (first and k < 2):
                            pe.wait_ge(radd, i * RG + k - 1)
                        for t in range(TG):
                            last = pe.matmul(bank[4 + k % 2][:, t * P:(t + 1) * P], ef[:, k % 2, t * P:(t + 1) * P], wn1b[:, :], start=True, stop=True)
                        last.then_inc(z1, 1)

                    def aggregate(i, k, first):
                        pe.wait_ge(r2, i * RG + k + 1)
                        pe.wait_ge(oh1, (i * RG + k + 1) * TG)
                        if not (first and k < 2):
                            pe.wait_ge(acc1, (i * RG + k - 1) * TG)
                        for t in range(TG):
                            last = pe.matmul(bank[6 + k % 2][:, t * P:(t + 1) * P], msg[:, k % 2, t, :], onehot[:, k % 2, t, :], start=True, stop=True)
                        last.then_inc(agg1, 1)
                    skewed(pe, ((0, first_product), (1, second_product), (2, third_product), (3, aggregate)))

                @block.scalar
                def _(act):
                    act.wait_ge(w1_in, 16 * 7)

                    def relu_hidden(i, k, first):
                        act.wait_ge(h1, i * RG + k + 1)
                        if not (first and k < 2):
                            act.wait_ge(h2, i * RG + k - 1)
                        act.activation(hidden[:, k % 2], bank[k % 2][:, :], ACT.Relu, bias=be1[:, 0:1]).then_inc(r1, 1)

                    def time_gate(i, k, first):
                        if k % HALF == 0:
                            act.wait_ge(ts_in[k // HALF], 16 * (i + 1))
                        if not (first and k < 2):
                            act.wait_ge(efd, i * RG + k - 1)
                        act.activation(gate[:, k % 2], ts[:, k // HALF, k % HALF * GE:(k % HALF + 1) * GE], ACT.Sigmoid,
                                       bias=bt[:, 0:1], scale=wt[:, 0:1]).then_inc(gt, 1)

                    def relu_message(i, k, first):
                        act.wait_ge(radd, i * RG + k + 1)
                        if not (first and k < 2):
                            act.wait_ge(agg1, i * RG + k - 1)
                        act.activation(msg[:, k % 2], pre[:, k % 2], ACT.Relu).then_inc(r2, 1)
                    skewed(act, ((0, relu_hidden), (0, time_gate), (2, relu_message)))

                @block.vector
                def _(dve):
                    regs = [dve.alloc_register(f"first1_{n}") for n in range(HALF * TG)]
                    dve.tensor_tensor(feat[:, :, :], count[:, :].unsqueeze(2).broadcast_to([P, NB, CH]),
                                      bn2_all[:, :].unsqueeze(1).broadcast_to([P, NB, CH]), ALU.mult).then_inc(base1, 1)
                    dve.wait_ge(base1, 1)
                    dve.tensor_tensor(x_rows[:, :, :], x_rows[:, :, :], feat[:, :, :], ALU.add).then_inc(base1, 1)
                    dve.wait_ge(base1, 2)
                    dve.wait_ge(w1_in, 16 * 7)

                    def masks(i, k, first):
                        if not (first and k < 2):
                            dve.wait_ge(agg1, i * RG + k - 1)
                        for t in range(TG):
                            dve.tensor_scalar(onehot[:, k % 2, t, :], iota_row[:, :], dst_rel[:, ds(i * RT + k * TG + t, 1)], None,
                                              ALU.is_equal).then_inc(oh1, 1)

                    def gated(i, k, first):
                        dve.wait_ge(h2, i * RG + k + 1)
                        dve.wait_ge(gt, i * RG + k + 1)
                        if not (first and k < 2):
                            dve.wait_ge(z1, i * RG + k - 1)
                        dve.scalar_tensor_tensor(ef[:, k % 2], bank[2 + k % 2][:, :], be2[:, 0:1], gate[:, k % 2], ALU.add, ALU.mult).then_inc(efd, 1)

                    def add_sender(i, k, first):
                        dve.wait_ge(z1, i * RG + k + 1)
                        dve.wait_ge(gathered[1][k], 16 * TG * (i + 1))
                        if not (first and k < 2):
                            dve.wait_ge(r2, i * RG + k - 1)
                        dve.tensor_tensor(pre[:, k % 2], bank[4 + k % 2][:, :].rearrange("p (t c) -> p t c", t=TG), rows[:, k], ALU.add).then_inc(radd, 1)

                    at = [None]

                    def add(i, k, first):
                        if k % HALF == 0:
                            at[0] = first_nodes(dve, regs, i, k // HALF)
                        dve.wait_ge(agg1, i * RG + k + 1)
                        for t in range(TG):
                            v = at[0][k % HALF * TG + t]
                            if not (first and k == 0 and t == 0):
                                dve.wait_ge(acc1, (i * RG + k) * TG + t)
                            dve.tensor_tensor(acc[:, ds(v, P)], acc[:, ds(v, P)], bank[6 + k % 2][:, t * P:(t + 1) * P], ALU.add).then_inc(acc1, 1)

                    def steps(i, first):
                        for k in range(RG):
                            for lag, part_of in ((2, masks), (1, gated), (2, add_sender), (3, add)):
                                if k >= lag:
                                    part_of(i, k - lag, first)
                                elif not first:
                                    part_of(i - 1, k - lag + RG, False)
                    steps(0, True)
                    with dve.Fori(1, ROUNDS) as i:
                        at[0] = [dve.snap(r, min_val=0, max_val=N) for r in regs]
                        steps(i, False)
                    at[0] = [dve.snap(r, min_val=0, max_val=N) for r in regs]
                    for k in range(3):
                        for lag, part_of in ((2, masks), (1, gated), (2, add_sender), (3, add)):
                            if k < lag:
                                part_of(ROUNDS - 1, k - lag + RG, False)
                    dve.wait_ge(acc1, TILES)

        f_done, o_done = sem("f_done"), sem("o_done")
        o_out = [sem(f"o_out{c}") for c in range(CHUNKS)]
        with nc.Block() as block:
            @block.tensor
            def _(pe):
                for c in range(CHUNKS):
                    if c >= 2:
                        pe.wait_ge(o_done, 2 * (c - 1))
                    for b in range(CB):
                        last = pe.matmul(bank[c % 2 * 2 + b // 4][:, b % 4 * P:(b % 4 + 1) * P],
                                         acc[:, (c * CB + b) * P:(c * CB + b + 1) * P], wn2[:, :], start=True, stop=True)
                        if b % 4 == 3 or b == CB - 1:
                            last.then_inc(f_done, 1)

            @block.vector
            def _(dve):
                for c in range(CHUNKS):
                    for j, (b0, m) in enumerate(((0, 4), (4, 3))):
                        dve.wait_ge(f_done, 2 * c + j + 1)
                        at = slice(c * CB + b0, c * CB + b0 + m)
                        dve.tensor_tensor(x_rows[:, at, :], bank[c % 2 * 2 + j][:, 0:m * P].rearrange("p (m c) -> p m c", m=m),
                                          x_rows[:, at, :], ALU.add).then_inc(o_done, 1)

            @block.sync
            def _(sp):
                for c in range(CHUNKS):
                    sp.wait_ge(o_done, 2 * (c + 1))
                    n0 = c * CB * P
                    full = min(CB, (N - n0) // P)
                    sp.dma_start(out[n0:n0 + full * P, :].rearrange("(b p) c -> p b c", p=P),
                                 x_rows[:, c * CB:c * CB + full, :]).then_inc(o_out[c], 16)
                    if full < CB:
                        rest = N - n0 - full * P
                        sp.dma_start(out[n0 + full * P:N, :], x_rows[0:rest, c * CB + full, :]).then_inc(o_out[c], 16)
                for c in range(CHUNKS):
                    sp.wait_ge(o_out[c], 32 if (c + 1) * CB * P > N else 16)


def kernel(**inputs):
    import numpy as np
    import concourse.bacc as bacc
    from concourse.bass_utils import run_bass_kernel_spmd

    def arr(name):
        return np.ascontiguousarray(np.asarray(inputs[name]))

    def padded(v, shape, fill=0):
        full = np.full(shape, fill, v.dtype)
        full[tuple(slice(0, s) for s in v.shape)] = v
        return full

    src = padded(arr("src"), (EPAD,))
    dst = padded(arr("dst"), (EPAD,), N)
    line = np.full((EPAD + 2,), -1, dst.dtype)
    line[1:EPAD + 1] = dst
    feed = {
        "x": padded(arr("x"), (NPAD, CH)),
        "src_lin": src.reshape(P, EPAD // P),
        "src_tile": np.ascontiguousarray(src.reshape(TILES, P).T),
        "dst_tile": np.ascontiguousarray(dst.reshape(TILES, P).T),
        "dst_first": np.ascontiguousarray(dst.reshape(TILES, P)[:, 0]).reshape(1, TILES),
        "dst_line": line,
        "ea_t": np.ascontiguousarray(padded(arr("edge_attr_64"), (EPAD, EC)).T),
        "ts": padded(arr("edge_weight"), (EPAD,)),
        "W": arr("L0_gnn_W"), "b_lin": arr("L0_gnn_b_lin"), "alpha": arr("L0_gnn_alpha"), "bias": arr("L0_gnn_bias"),
        "We1": arr("L1_gnn_We1"), "be1": arr("L1_gnn_be1"), "We2": arr("L1_gnn_We2"), "be2": arr("L1_gnn_be2"),
        "Wt": arr("L1_gnn_Wt"), "bt": arr("L1_gnn_bt"), "Wn1": arr("L1_gnn_Wn1"), "bn1": arr("L1_gnn_bn1"),
        "Wn2": arr("L1_gnn_Wn2"), "bn2": arr("L1_gnn_bn2"),
    }
    nc = bacc.Bacc("TRN2", target_bir_lowering=False, num_devices=1)
    arrays, aps = {}, {}
    for name, v in feed.items():
        arrays[f"in_{name}"] = v
        aps[name] = nc.dram_tensor(f"in_{name}", v.shape, mybir.dt.from_np(v.dtype), kind="ExternalInput").ap()
    fp32, bf16 = mybir.dt.float32, mybir.dt.bfloat16
    out = nc.dram_tensor("out_0", (N, CH), fp32, kind="ExternalOutput").ap()
    table1 = nc.dram_tensor("table1", (NPAD, CH), fp32, kind="Internal").ap()
    table2 = nc.dram_tensor("table2", (NPAD, CH), fp32, kind="Internal").ap()
    bound_dram = nc.dram_tensor("bound_dram", (len(SECTIONS), 2, SH), fp32, kind="Internal").ap()
    parts_dram = nc.dram_tensor("parts_dram", (2, EPAD), bf16, kind="Internal").ap()
    lin_dram = nc.dram_tensor("lin_dram", (SH, EPAD), fp32, kind="Internal").ap()
    w_dram = nc.dram_tensor("w_dram", (2 * SH, EPAD), fp32, kind="Internal").ap()
    gnn_layers(nc, aps, out, table1, table2, parts_dram, lin_dram, w_dram, bound_dram)
    return run_bass_kernel_spmd(nc, [arrays], core_ids=[0]).results[0]["out_0"]
```
